# Optimizing a Trainium2 kernel written in Bass

```python
import numpy as np
import jax
import jax.numpy as jnp

def _softmax(x, axis=-1):
    return jax.nn.softmax(x, axis=axis)

def _gelu(x):
    return jax.nn.gelu(x, approximate=True)

def _silu(x):
    return jax.nn.silu(x)

def _sigmoid(x):
    return jax.nn.sigmoid(x)

def _layernorm(x, axis=-1, eps=1e-05):
    m = jnp.mean(x, axis=axis, keepdims=True)
    v = jnp.var(x, axis=axis, keepdims=True)
    return (x - m) / jnp.sqrt(v + eps)

def _scatter_add(tgt, idx, src, axis=0):
    return tgt.at[idx].add(src)

def _segment_sum(src, seg, n):
    return jax.ops.segment_sum(src, seg, n)
kernel_name = 'mk_adaln_d1_jaxref_r4_68db62'

def setup_inputs(seed: int=0):
    np.random.seed(seed)
    _w = jnp.asarray

    def _L0_attn_setup():
        import jax, jax.numpy as jnp
        import numpy as np
        D_MODEL = 256
        N_HEADS = 16
        LATENT_HEADS = 8
        LATENT_DIM = 128
        N_LATENTS = 64
        WINDOW = 64
        HEAD_DIM = D_MODEL // N_HEADS
        LAT_HD = LATENT_DIM // LATENT_HEADS
        B, S = (2, 1024)

        def _pool_to_latents(x):
            Bx, Sx, C = x.shape
            chunk = max(1, Sx // N_LATENTS)
            return x.reshape(Bx, N_LATENTS, chunk, C).mean(axis=2)

        def _local_window_attn(Q, K, V):
            Bx, H, Sx, D = Q.shape
            W = WINDOW
            nb = Sx // W
            Qb = Q.reshape(Bx, H, nb, W, D)
            Kp = jnp.pad(K, ((0, 0), (0, 0), (W, 0), (0, 0))).reshape(Bx, H, nb + 1, W, D)
            Vp = jnp.pad(V, ((0, 0), (0, 0), (W, 0), (0, 0))).reshape(Bx, H, nb + 1, W, D)
            Kw = jnp.concatenate([Kp[:, :, :-1], Kp[:, :, 1:]], axis=3)
            Vw = jnp.concatenate([Vp[:, :, :-1], Vp[:, :, 1:]], axis=3)
            i = jnp.arange(W)[:, None]
            j = jnp.arange(2 * W)[None, :]
            base = (j > i) & (j <= i + W)
            blk0 = (jnp.arange(nb) > 0)[:, None, None] | (j >= W)[None, :, :]
            mask = base[None, :, :] & blk0
            sc = jnp.einsum('bhnid,bhnjd->bhnij', Qb, Kw) / np.sqrt(D).astype(np.float32)
            sc = jnp.where(mask[None, None], sc, -jnp.inf)
            p = jax.nn.softmax(sc, axis=-1)
            out = jnp.einsum('bhnij,bhnjd->bhnid', p, Vw)
            return out.reshape(Bx, H, Sx, D)
        key = jax.random.key(seed)
        ks = jax.random.split(key, 11)
        std = 0.02
        w = lambda k, shp: jax.random.normal(k, shp, jnp.float32) * std
        return {'x': jax.random.normal(ks[0], (B, S, D_MODEL), jnp.float32), 'wq': w(ks[1], (D_MODEL, D_MODEL)), 'wk': w(ks[2], (D_MODEL, D_MODEL)), 'wv': w(ks[3], (D_MODEL, D_MODEL)), 'wgq': w(ks[4], (D_MODEL, LATENT_DIM)), 'wgk': w(ks[5], (D_MODEL, LATENT_DIM)), 'wgv': w(ks[6], (D_MODEL, LATENT_DIM)), 'r_out_w': w(ks[7], (LATENT_DIM, D_MODEL)), 'gate_local_w': w(ks[8], (N_HEADS, HEAD_DIM)), 'gate_remote_w': w(ks[9], (N_HEADS, HEAD_DIM)), 'w_out': w(ks[10], (D_MODEL, D_MODEL))}
    _L0_attn_in = _L0_attn_setup()

    def _L0_ffn_setup():
        import jax, jax.numpy as jnp
        import numpy as np
        CAPACITY_FACTOR = 1.25
        key = jax.random.key(seed)
        k1, k2, k3, k4 = jax.random.split(key, 4)
        B, S, D, E, H = (2, 512, 256, 16, 1024)
        inputs = jax.random.normal(k1, (B, S, D), dtype=jnp.float32)
        gate_w = jax.random.normal(k2, (E, D), dtype=jnp.float32) / np.float32(np.sqrt(D))
        w1 = jax.random.normal(k3, (E, D, H), dtype=jnp.float32) / np.float32(np.sqrt(D))
        w2 = jax.random.normal(k4, (E, H, D), dtype=jnp.float32) / np.float32(np.sqrt(H))
        return {'inputs': inputs, 'gate_w': gate_w, 'w1': w1, 'w2': w2}
    _L0_ffn_in = _L0_ffn_setup()
    _L0_c = _w((lambda *s: np.random.randn(*s).astype(np.float32) * 0.05)(8, 256))
    _L0_wmod = _w((lambda *s: np.random.randn(*s).astype(np.float32) * 0.05)(256, 6 * 256) * 256 ** (-0.5))
    _d = {'L0_attn_x': _L0_attn_in['x'], 'L0_attn_wq': _L0_attn_in['wq'], 'L0_attn_wk': _L0_attn_in['wk'], 'L0_attn_wv': _L0_attn_in['wv'], 'L0_attn_wgq': _L0_attn_in['wgq'], 'L0_attn_wgk': _L0_attn_in['wgk'], 'L0_attn_wgv': _L0_attn_in['wgv'], 'L0_attn_r_out_w': _L0_attn_in['r_out_w'], 'L0_attn_gate_local_w': _L0_attn_in['gate_local_w'], 'L0_attn_gate_remote_w': _L0_attn_in['gate_remote_w'], 'L0_attn_w_out': _L0_attn_in['w_out'], 'L0_ffn_gate_w': _L0_ffn_in['gate_w'], 'L0_ffn_w1': _L0_ffn_in['w1'], 'L0_ffn_w2': _L0_ffn_in['w2'], 'L0_c': _L0_c, 'L0_wmod': _L0_wmod}
    _x0 = _d['L0_attn_x']
    _d['L0_attn_x'] = jax.random.normal(jax.random.fold_in(jax.random.key(seed), 1), (8, 512, 256), dtype=_x0.dtype)
    del _x0
    return _d

def reference(L0_attn_x, L0_attn_wq, L0_attn_wk, L0_attn_wv, L0_attn_wgq, L0_attn_wgk, L0_attn_wgv, L0_attn_r_out_w, L0_attn_gate_local_w, L0_attn_gate_remote_w, L0_attn_w_out, L0_ffn_gate_w, L0_ffn_w1, L0_ffn_w2, L0_c, L0_wmod):

    def _L0_attn_ref(x, wq, wk, wv, wgq, wgk, wgv, r_out_w, gate_local_w, gate_remote_w, w_out):
        import jax, jax.numpy as jnp
        import numpy as np
        D_MODEL = 256
        N_HEADS = 16
        LATENT_HEADS = 8
        LATENT_DIM = 128
        N_LATENTS = 64
        WINDOW = 64
        HEAD_DIM = D_MODEL // N_HEADS
        LAT_HD = LATENT_DIM // LATENT_HEADS
        B, S = (2, 1024)

        def _pool_to_latents(x):
            Bx, Sx, C = x.shape
            chunk = max(1, Sx // N_LATENTS)
            return x.reshape(Bx, N_LATENTS, chunk, C).mean(axis=2)

        def _local_window_attn(Q, K, V):
            Bx, H, Sx, D = Q.shape
            W = WINDOW
            nb = Sx // W
            Qb = Q.reshape(Bx, H, nb, W, D)
            Kp = jnp.pad(K, ((0, 0), (0, 0), (W, 0), (0, 0))).reshape(Bx, H, nb + 1, W, D)
            Vp = jnp.pad(V, ((0, 0), (0, 0), (W, 0), (0, 0))).reshape(Bx, H, nb + 1, W, D)
            Kw = jnp.concatenate([Kp[:, :, :-1], Kp[:, :, 1:]], axis=3)
            Vw = jnp.concatenate([Vp[:, :, :-1], Vp[:, :, 1:]], axis=3)
            i = jnp.arange(W)[:, None]
            j = jnp.arange(2 * W)[None, :]
            base = (j > i) & (j <= i + W)
            blk0 = (jnp.arange(nb) > 0)[:, None, None] | (j >= W)[None, :, :]
            mask = base[None, :, :] & blk0
            sc = jnp.einsum('bhnid,bhnjd->bhnij', Qb, Kw) / np.sqrt(D).astype(np.float32)
            sc = jnp.where(mask[None, None], sc, -jnp.inf)
            p = jax.nn.softmax(sc, axis=-1)
            out = jnp.einsum('bhnij,bhnjd->bhnid', p, Vw)
            return out.reshape(Bx, H, Sx, D)
        Bx, Sx, _ = x.shape
        chunk = max(1, Sx // N_LATENTS)
        Q = (x @ wq).reshape(Bx, Sx, N_HEADS, HEAD_DIM).transpose(0, 2, 1, 3)
        K = (x @ wk).reshape(Bx, Sx, N_HEADS, HEAD_DIM).transpose(0, 2, 1, 3)
        V = (x @ wv).reshape(Bx, Sx, N_HEADS, HEAD_DIM).transpose(0, 2, 1, 3)
        local = _local_window_attn(Q, K, V)
        GQ = (x @ wgq).reshape(Bx, Sx, LATENT_HEADS, LAT_HD).transpose(0, 2, 1, 3)
        GK = _pool_to_latents(x @ wgk).reshape(Bx, N_LATENTS, LATENT_HEADS, LAT_HD).transpose(0, 2, 1, 3)
        GV = _pool_to_latents(x @ wgv).reshape(Bx, N_LATENTS, LATENT_HEADS, LAT_HD).transpose(0, 2, 1, 3)
        lsc = jnp.einsum('bhsd,bhnd->bhsn', GQ, GK) / np.sqrt(LAT_HD).astype(np.float32)
        lmask = jnp.arange(N_LATENTS)[None, :] <= (jnp.arange(Sx) // chunk)[:, None]
        lsc = jnp.where(lmask[None, None], lsc, -jnp.inf)
        lp = jax.nn.softmax(lsc, axis=-1)
        rem = jnp.einsum('bhsn,bhnd->bhsd', lp, GV)
        rem = rem.transpose(0, 2, 1, 3).reshape(Bx, Sx, LATENT_DIM) @ r_out_w
        rem = rem.reshape(Bx, Sx, N_HEADS, HEAD_DIM).transpose(0, 2, 1, 3)
        gl = jax.nn.sigmoid(jnp.einsum('bhsd,hd->bhs', Q, gate_local_w))[..., None]
        gr = jax.nn.sigmoid(jnp.einsum('bhsd,hd->bhs', Q, gate_remote_w))[..., None]
        out = gl * local + gr * rem
        out = out.transpose(0, 2, 1, 3).reshape(Bx, Sx, D_MODEL)
        return out @ w_out

    def _L0_ffn_ref(inputs, gate_w, w1, w2):
        import jax, jax.numpy as jnp
        import numpy as np
        CAPACITY_FACTOR = 1.25
        orig_shape = inputs.shape
        D = orig_shape[-1]
        tokens = inputs.reshape(-1, D)
        T = tokens.shape[0]
        E = gate_w.shape[0]
        C = int(CAPACITY_FACTOR * T / E)
        logits = tokens @ gate_w.T
        probs = jax.nn.softmax(logits, axis=-1)
        expert_idx = jnp.argmax(probs, axis=-1)
        mask = jax.nn.one_hot(expert_idx, E, dtype=jnp.int32)
        locations = jnp.cumsum(mask, axis=0) - 1
        mask = mask * (locations < C)
        loc_oh = jax.nn.one_hot(locations, C, dtype=probs.dtype)
        sec_mask = mask[:, :, None].astype(probs.dtype) * loc_oh
        combine_weights = probs[:, :, None] * sec_mask
        dispatch = jnp.einsum('tec,td->ecd', sec_mask, tokens)
        h = jax.nn.relu(jnp.einsum('ecd,edh->ech', dispatch, w1))
        expert_out = jnp.einsum('ech,ehd->ecd', h, w2)
        ans = jnp.einsum('tec,ecd->td', combine_weights, expert_out)
        return ans.reshape(orig_shape)
    x = L0_attn_x
    mod = (_silu(L0_c) @ L0_wmod).reshape(L0_c.shape[0], 6, 1, -1)
    sa, ca, ga, sb, cb, gb = (mod[:, 0], mod[:, 1], mod[:, 2], mod[:, 3], mod[:, 4], mod[:, 5])
    ga = (2 * (ga >= 0) - 1) * jnp.maximum(jnp.abs(ga), 0.25)
    gb = (2 * (gb >= 0) - 1) * jnp.maximum(jnp.abs(gb), 0.25)
    h = _layernorm(x, axis=-1) * (1 + ca) + sa
    x = x + ga * _L0_attn_ref(h, L0_attn_wq, L0_attn_wk, L0_attn_wv, L0_attn_wgq, L0_attn_wgk, L0_attn_wgv, L0_attn_r_out_w, L0_attn_gate_local_w, L0_attn_gate_remote_w, L0_attn_w_out)
    h = _layernorm(x, axis=-1) * (1 + cb) + sb
    x = x + gb * _L0_ffn_ref(h, L0_ffn_gate_w, L0_ffn_w1, L0_ffn_w2)
    return x

_drawn_inputs = setup_inputs


def setup_inputs(seed=0):
    import zlib

    import numpy as np

    out = dict(_drawn_inputs(seed))
    spreads = {}
    factors = {'L0_attn_wq': 8.0,
     'L0_attn_wk': 8.0,
     'L0_attn_wv': 8.0,
     'L0_attn_wgq': 8.0,
     'L0_attn_wgk': 8.0,
     'L0_attn_wgv': 8.0,
     'L0_attn_r_out_w': 8.0,
     'L0_attn_gate_local_w': 8.0,
     'L0_attn_gate_remote_w': 8.0,
     'L0_attn_w_out': 8.0}
    for name, (base, spread) in spreads.items():
        noise = np.random.default_rng([zlib.crc32(name.encode()), seed]).standard_normal(out[name].shape)
        drawn = base * np.exp(spread * noise) if base else spread * noise
        out[name] = jnp.asarray(drawn.astype(out[name].dtype))
    for name, factor in factors.items():
        out[name] = (out[name] * factor).astype(out[name].dtype)
    return out
```

```python
from contextlib import ExitStack

import concourse.bass as bass
from concourse import mybir

ALU = mybir.AluOpType
ACT = mybir.ActivationFunctionType
F32 = mybir.dt.float32
F32R = mybir.dt.float32r
BF16 = mybir.dt.bfloat16
I32 = mybir.dt.int32
AX_X = mybir.AxisListType.X

P = 128
B, S, D = 8, 512, 256
KD = D // P
NT = S // P
H, HD = 16, 16
W = 64
NB = S // W
LH, LD, NL = 8, 128, 64
CH = S // NL
NP = LH // 2
E, HID = 16, 1024
T = B * S
CAP = int(1.25 * T / E)
SLOTS = E * CAP
MH = HID // P
ST = [(0, 128), (128, 128), (256, CAP - 256)]
EPS = 1e-5
BIG = -1.0e30
QPART = [0, 0, 0, 1, 1, 2]
KPART = [0, 1, 2, 0, 1, 0]
KS_ROWS = 16 * len(QPART)
VW = HD + 1
HH = H // 2
SB = 3

SLOT_JOBS = {
    0: [],
    1: ["D.OT0", "D.OT1"],
    2: ["A.T0", "A.T1"],
    3: ["A.Q0", "A.Q1"],
    4: ["A.K0", "A.K1", "D.WO0", "D.WO1"],
    5: ["A.GQ"],
    6: ["L.LT0", "A.V0"],
    7: ["A.V1", "A.V2", "A.V3"],
    8: ["A.GK", "A.GV", "C.R0"],
    9: ["C.R1", "D.H0", "D.H1"],
    10: ["L.LT1", "C.R2"],
    11: ["C.R3", "D.LG"],
    12: ["C.PR0", "C.PR1"],
    13: ["C.PR2", "D.LOC"],
    14: ["L.LT2", "C.PR3"],
    15: ["C.RP"],
    16: ["C.RO0", "C.RO1", "L.LT3"],
}
ALL_JOBS = [j for s in range(17) for j in SLOT_JOBS[s]]
PRO = [j for j in ALL_JOBS if j[0] == "A"]
FIRST = [j for j in ALL_JOBS if j[0] != "D"]
LAST = [j for j in ALL_JOBS if j[0] != "A"]
EPI = [j for j in ALL_JOBS if j[0] == "D"]
ORDER = {"pro": PRO, "first": FIRST, "mid": ALL_JOBS, "last": LAST, "epi": EPI}
BEFORE = {"pro": [], "first": PRO, "mid": ALL_JOBS, "last": ALL_JOBS, "epi": LAST}
START = {"pro": 0, "first": len(PRO), "mid": len(PRO) + len(FIRST)}
START["last"] = START["mid"] + (B - 2) * len(ALL_JOBS)
START["epi"] = START["last"] + len(LAST)


def batch_of(name, step):
    return {"A": step + 1, "C": step, "L": step, "D": step - 1}[name[0]]


class Job:

    def __init__(self, kind, step, name):
        at = ORDER[kind].index(name)
        turns = (step - 1) if kind == "mid" else 0
        self.bank = (START[kind] + at) % SB
        self.done = START[kind] + at + 1 + len(ALL_JOBS) * turns
        if at >= SB:
            prev = ORDER[kind][at - SB]
            self.before = (prev, batch_of(prev, step))
        elif BEFORE[kind]:
            prev = BEFORE[kind][at - SB]
            self.before = (prev, batch_of(prev, step - 1))
        else:
            self.before = None


class Signal:

    def __init__(self, sem, per, by=1):
        self.sem, self.per, self.by = sem, per, by

    def at(self, b, k):
        return b * (self.per * self.by) + k * self.by


def bc(ap, shape):
    return ap.to_broadcast(shape)


def adaln_moe_kernel(nc, x, wq, wk, wv, wgq, wgk, wgv, r_out, gl_w, gr_w, w_out, gate_w, w1, w2, c_in, wmod, out):
    top = ExitStack()
    sems = {}

    def sem(name):
        if name not in sems:
            sems[name] = top.enter_context(nc.semaphore(name))
        return sems[name]

    def alloc(ctx, name, shape, dt):
        return ctx.enter_context(nc.sbuf_tensor(name, shape, dt))

    with top:
        qk_d = nc.dram_tensor("qk_parts", [2, 2, 3, D, S], BF16).ap()
        mod_d = nc.dram_tensor("mod_rows", [B, 4, D], F32).ap()
        x1_d = nc.dram_tensor("x1_rows", [B, NT, P, D], F32).ap()
        xs_d = nc.dram_tensor("expert_in", [SLOTS, D], F32).ap()
        ys_d = nc.dram_tensor("expert_out", [SLOTS + 1, D], F32).ap()

        ident = alloc(top, "ident", [P, P], F32)
        blank_row = alloc(top, "blank_row", [1, 1], F32)
        slot_all = alloc(top, "slot_all", [P, B * NT], I32)
        prob_all = alloc(top, "prob_all", [P, B * NT], F32)
        ps = [top.enter_context(nc.psum_tensor(f"bank{i}", [P, 512], F32)) for i in range(8)]

        att = ExitStack()
        with att:
            def sb(name, shape, dt=F32):
                return alloc(att, name, shape, dt)

            ident_b = sb("ident_b", [P, P], BF16)
            mask_q = sb("mask_q", [P, NT, P], BF16)
            mask_k = sb("mask_k", [P, NB, W], BF16)
            mask_r = sb("mask_r", [P, NT, LH, NL], BF16)
            pick = sb("pick", [P, HH, P], BF16)
            tri = sb("tri", [P, P], BF16)
            ones_b = sb("ones_b", [P, P], BF16)
            head_rows = sb("head_rows", [P, LH])
            pair_rows = sb("pair_rows", [P, NP, 2, HD])
            iota_f = sb("iota_f", [P, E])
            wq_h, wq_l = sb("wq_h", [P, KD, D], F32R), sb("wq_l", [P, KD, D], F32R)
            wk_h, wk_l = sb("wk_h", [P, KD, D], F32R), sb("wk_l", [P, KD, D], F32R)
            wg_h, wg_l = sb("wg_h", [P, KD, LD], F32R), sb("wg_l", [P, KD, LD], F32R)
            VG = D + 2 * H
            wv_h, wv_l = sb("wv_h", [P, KD, VG], F32R), sb("wv_l", [P, KD, VG], F32R)
            wgk_s, wgv_s = sb("wgk_s", [P, KD, LD]), sb("wgv_s", [P, KD, LD])
            rout_s, wout_s = sb("rout_s", [P, D]), sb("wout_s", [P, KD, D])
            gate_t = sb("gate_t", [P, KD, E])
            mod_t = sb("mod_t", [P, B, 2, KD])

            setup = ExitStack()
            with setup:
                def st(name, shape, dt=F32):
                    return alloc(setup, name, shape, dt)

                wq_f, wk_f, wg_f = st("wq_f", [P, KD, D]), st("wk_f", [P, KD, D]), st("wg_f", [P, KD, LD])
                wv_f = st("wv_f", [P, KD, VG])
                gates_f = st("gates_f", [P, 2, D])
                gate_tmp = st("gate_tmp", [P, 2, KD, D])
                wmod_f = st("wmod_f", [P, KD, 6 * D])
                c_t, c_e = st("c_t", [P, KD, B]), st("c_e", [P, KD, B])
                mod_r = st("mod_r", [B, 6, D])
                mod_o = st("mod_o", [B, 4, D])
                mod_s = st("mod_s", [B, 2, D])
                zero = st("zero", [P, 2560])
                iota_i = st("iota_i", [P, E], I32)
                gate_r = st("gate_r", [E, D])
                w_in, c_inn, const_in = sem("weights_in"), sem("cond_in"), sem("setup_consts")
                with nc.Block() as block:
                    @block.sync
                    def _(sp):
                        with nc.allow_non_contiguous_dma("condition, transposed"):
                            for k in range(KD):
                                sp.dma_start(c_t[:, k, :], c_in.rearrange("b (k p) -> k p b", p=P)[k]).then_inc(c_inn, 16)
                        sp.dma_start(wmod_f[:, :, :], wmod.rearrange("(k p) n -> p k n", p=P)).then_inc(c_inn, 16)
                        for dst, src in ((wq_f, wq), (wk_f, wk), (wg_f, wgq), (wgk_s, wgk), (wgv_s, wgv), (wout_s, w_out)):
                            sp.dma_start(dst[:, :, :], src.rearrange("(k p) n -> p k n", p=P)).then_inc(w_in, 16)
                        sp.dma_start(wv_f[:, :, 0:D], wv.rearrange("(k p) n -> p k n", p=P)).then_inc(w_in, 16)
                        sp.dma_start(rout_s[:, :], r_out).then_inc(w_in, 16)
                        for i, g in enumerate((gl_w, gr_w)):
                            sp.dma_start(gates_f[:, i, :], g.rearrange("h d -> (h d)")[None, :].to_broadcast([P, D])).then_inc(w_in, 16)
                        sp.dma_start(gate_r[:, :], gate_w).then_inc(w_in, 16)
                        sp.wait_ge(sem("zero_set"), 1)
                        rows = SLOTS // P // 4
                        for i in range(4):
                            sp.dma_start(xs_d[i * rows * P:(i + 1) * rows * P, :].rearrange("(p r) d -> p (r d)", p=P),
                                         zero[:, 0:rows * D]).then_inc(sem("slots_zeroed"), 16)
                        sp.dma_start(ys_d[SLOTS:SLOTS + 1, :], zero[0:1, 0:D]).then_inc(sem("slots_zeroed"), 16)
                        sp.wait_ge(sem("mod_rows_ready"), 5)
                        sp.dma_start(mod_d, mod_o[:, :, :]).then_inc(sem("mod_stored"), 16)
                        sp.wait_ge(sem("mod_stored"), 16)
                        sp.wait_ge(sem("slots_zeroed"), 80)

                    @block.gpsimd
                    def _(pool):
                        blank = sem("blank")
                        nc.gpsimd.memset(zero[:, :], 0.0).then_inc(sem("zero_set"), 1)
                        for t_, v in ((ident, 0.0), (ident_b, 0.0), (mask_q, 0.0), (mask_k, 0.0), (mask_r, 0.0), (pick, 0.0),
                                      (tri, 1.0), (blank_row, 0.0), (ones_b, 1.0), (head_rows, 1.0), (pair_rows, 1.0)):
                            nc.gpsimd.memset(t_.ap(), v).then_inc(blank, 1)
                        pool.wait_ge(blank, 11)
                        n = [11]

                        def select(ap, cond, fill, base, pattern, mult):
                            nc.gpsimd.affine_select(out=ap, in_=ap, compare_op=cond, fill=fill, base=base,
                                                    pattern=pattern, channel_multiplier=mult).then_inc(blank, 1)
                            n[0] += 1
                            pool.wait_ge(blank, n[0])

                        select(ident[:, :], ALU.not_equal, 1.0, 0, [[-1, P]], 1)
                        select(ident_b[:, :], ALU.not_equal, 1.0, 0, [[-1, P]], 1)
                        for half in range(2):
                            m = mask_q[64 * half:64 * half + 64, :, :]
                            select(m, ALU.is_gt, BIG, 0, [[0, NT], [1, P]], -1)
                            select(m, ALU.is_ge, BIG, W, [[0, NT], [-1, P]], 1)
                        select(mask_q[0:64, 0, 0:W], ALU.is_gt, BIG, -1, [[0, W]], 0)
                        select(mask_k[:, :, :], ALU.is_gt, BIG, 0, [[0, NB], [-1, W]], 1)
                        select(mask_k[:, :, :], ALU.is_ge, BIG, W, [[0, NB], [1, W]], -1)
                        select(mask_k[0:64, 0, :], ALU.is_gt, BIG, -1, [[0, W]], 0)
                        select(mask_r[:, :, :, :], ALU.is_ge, BIG, 0, [[P, NT], [0, LH], [-CH, NL]], 1)
                        for j in range(3):
                            select(pick[:, :, :], ALU.not_equal, 1.0, -HH * j, [[-1, HH], [0, P]], 1)
                        select(tri[:, :], ALU.is_ge, 0.0, 0, [[1, P]], -1)
                        select(head_rows[:, :], ALU.is_ge, 0.0, 0, [[-HD, LH]], 1)
                        select(head_rows[:, :], ALU.is_ge, 0.0, HD - 1, [[HD, LH]], -1)
                        select(pair_rows[:, :, 0, :], ALU.is_ge, 0.0, NL - 1, [[0, NP], [0, HD]], -1)
                        select(pair_rows[:, :, 1, :], ALU.is_ge, 0.0, -NL, [[0, NP], [0, HD]], 1)
                        nc.gpsimd.iota(iota_i[:, :], pattern=[[1, E]], base=0, channel_multiplier=0).then_inc(const_in, 1)

                    @block.scalar
                    def _(act):
                        act.wait_ge(c_inn, 48)
                        nc.scalar.activation(c_e[:, :, :], c_t[:, :, :], ACT.Exp, scale=-1.0).then_inc(sem("cond_exp"), 1)

                    @block.tensor
                    def _(pe):
                        pe.wait_ge(sem("silu_ready"), 1)
                        for half in range(KD):
                            for kind in range(2):
                                o = (half * 2 + kind) * B
                                for k in range(KD):
                                    last = nc.tensor.matmul(
                                        ps[0][:, o:o + B], wmod_f[:, k, kind * D + half * P:kind * D + half * P + P],
                                        c_t[:, k, :], start=(k == 0), stop=(k == KD - 1))
                        last.then_inc(sem("mod_matmul"), 1)
                        for n in range(3):
                            for k in range(KD):
                                last = nc.tensor.matmul(ps[1 + n][0:B, :], c_t[:, k, :], wmod_f[:, k, n * 512:n * 512 + 512],
                                                        start=(k == 0), stop=(k == KD - 1))
                        last.then_inc(sem("mod_matmul"), 1)
                        pe.wait_ge(w_in, 16 * 11)
                        pe.wait_ge(sem("blank"), 12)
                        for k in range(KD):
                            last = nc.tensor.matmul(ps[4][:, k * E:(k + 1) * E], gate_r[:, k * P:(k + 1) * P],
                                                    ident[0:E, 0:E], start=True, stop=True, is_transpose=True)
                        last.then_inc(sem("mod_matmul"), 1)

                    @block.vector
                    def _(dve):
                        step = sem("setup_vector")
                        n = [0]

                        def then(ins):
                            ins.then_inc(step, 1)
                            n[0] += 1
                            dve.wait_ge(step, n[0])

                        dve.wait_ge(sem("cond_exp"), 1)
                        then(nc.vector.tensor_scalar(c_e[:, :, :], c_e[:, :, :], 1.0, None, ALU.add))
                        then(nc.vector.reciprocal(c_e[:, :, :], c_e[:, :, :]))
                        nc.vector.tensor_tensor(c_t[:, :, :], c_t[:, :, :], c_e[:, :, :], ALU.mult).then_inc(sem("silu_ready"), 1)
                        dve.wait_ge(w_in, 16 * 11)
                        for i in range(2):
                            for k in range(KD):
                                then(nc.vector.tensor_tensor(gate_tmp[:, i, k, :], wq_f[:, k, :], gates_f[:, i, :], ALU.mult))
                        for i in range(2):
                            then(nc.vector.tensor_reduce(wv_f[:, :, D + i * H:D + (i + 1) * H],
                                                         gate_tmp[:, i, :, :].rearrange("p k (h d) -> p k h d", d=HD), AX_X, ALU.add))
                        for f, hi, lo in ((wq_f, wq_h, wq_l), (wk_f, wk_h, wk_l), (wg_f, wg_h, wg_l), (wv_f, wv_h, wv_l)):
                            then(nc.vector.tensor_copy(hi[:, :, :], f[:, :, :]))
                            then(nc.vector.tensor_tensor(lo[:, :, :], f[:, :, :], hi[:, :, :].bitcast(F32), ALU.subtract))
                        dve.wait_ge(sem("mod_matmul"), 1)
                        nc.vector.tensor_copy(mod_t[:, :, 0, :], ps[0][:, 0:4 * B].rearrange("p (h k b) -> p k b h", k=2, b=B)[:, 0])
                        then(nc.vector.tensor_scalar(mod_t[:, :, 1, :], ps[0][:, 0:4 * B].rearrange("p (h k b) -> p k b h", k=2, b=B)[:, 1],
                                                     1.0, None, ALU.add))
                        dve.wait_ge(sem("mod_matmul"), 2)
                        for i in range(3):
                            then(nc.vector.tensor_copy(mod_r[:, 2 * i:2 * i + 2, :], ps[1 + i][0:B, :].rearrange("b (a d) -> b a d", a=2)))
                        rows = sem("mod_rows_ready")
                        for i, (src, dst) in enumerate(((2, 0), (5, 3))):
                            then(nc.vector.tensor_scalar(mod_s[:, i, :], mod_r[:, src, :], 0.0, 2.0, ALU.is_ge, ALU.mult))
                            then(nc.vector.tensor_scalar(mod_s[:, i, :], mod_s[:, i, :], 1.0, None, ALU.subtract))
                            then(nc.vector.tensor_tensor(mod_o[:, dst, :], mod_r[:, src, :], mod_s[:, i, :], ALU.mult))
                            then(nc.vector.tensor_scalar(mod_o[:, dst, :], mod_o[:, dst, :], 0.25, None, ALU.max))
                            nc.vector.tensor_tensor(mod_o[:, dst, :], mod_o[:, dst, :], mod_s[:, i, :], ALU.mult).then_inc(rows, 1)
                        nc.vector.tensor_scalar(mod_o[:, 1, :], mod_r[:, 4, :], 1.0, None, ALU.add).then_inc(rows, 1)
                        nc.vector.tensor_copy(mod_o[:, 2, :], mod_r[:, 3, :]).then_inc(rows, 1)
                        dve.wait_ge(const_in, 1)
                        nc.vector.tensor_copy(iota_f[:, :], iota_i[:, :]).then_inc(rows, 1)
                        dve.wait_ge(sem("mod_matmul"), 3)
                        then(nc.vector.tensor_copy(gate_t[:, :, :], ps[4][:, 0:KD * E].rearrange("p (k e) -> p k e", k=KD)))

            q_st = [sb(f"q_stack{i}", [KS_ROWS, H, S], BF16) for i in range(2)]
            k_st = [sb(f"k_stack{i}", [KS_ROWS, H, W + S], BF16) for i in range(2)]
            v_al = [sb(f"v_aligned{i}", [P, NT, H, VW]) for i in range(2)]
            v_sh = [sb(f"v_shifted{i}", [P, NT, H, VW]) for i in range(2)]
            xin = sb("xin", [P, NT, D])
            hT = sb("hT", [P, KD, S])
            hT_h, hT_l = sb("hT_h", [P, KD, S], F32R), sb("hT_l", [P, KD, S], F32R)
            hbar = sb("hbar", [P, KD, 2, NL])
            mod_b = sb("mod_b", [P, 2, KD])
            parts = [sb(f"parts{i}", [P, 3, S], BF16) for i in range(2)]
            rest = [sb(f"rest{i}", [P, S]) for i in range(2)]
            gates = [sb(f"gates{i}", [P, NT, 2 * H]) for i in range(2)]
            gq_t = [sb(f"gq_t{i}", [P, S]) for i in range(2)]
            gk_bd = [sb(f"gk_bd{i}", [P, LH, NL]) for i in range(2)]
            gv_bd = [sb(f"gv_bd{i}", [P, NP, 2, HD]) for i in range(2)]
            nmx = sb("nmx", [P, NT, H])
            nmx_r = sb("nmx_r", [P, NT, HH])
            mx_p = [sb(f"mx_parts{i}", [P, NT, P], BF16) for i in range(2)]
            mx_t = [sb(f"mx_t{i}", [P, S], BF16) for i in range(2)]
            NPT = 3
            p_t = [sb(f"p_t{i}", [P, S]) for i in range(NPT)]
            pv_s = sb("pv_s", [P, S])
            o = sb("o", [P, NT, D])
            fac = sb("fac", [P, 2, NT, 4])
            sr = sb("sr", [P, NT, LH, NL])
            rm = sr[:, 0:2, :, :].rearrange("p t h n -> p (t h n)").rearrange("p (t d) -> p t d", d=D)
            rstat = sb("rstat", [P, 3, NT, LH])
            pr_t = sb("pr_t", [P, NP, S])
            rem_t = sb("rem_t", [P, S])
            d_t = sb("d_t", [P, KD, S])
            x1 = sb("x1", [P, NT, D])
            h2 = sb("h2", [P, NT, D])
            mod_bc = sb("mod_bc", [P, 3, D])
            ln_raw = sb("ln_raw", [P, NT, 6])
            ln_mv = sb("ln_mv", [P, NT, 2])
            ln_ve = sb("ln_ve", [P, NT])
            ln_rs = sb("ln_rs", [P, NT])
            neg_half = sb("neg_half", [P, NT])
            turn = sb("turn", [1, 1])
            lg = sb("lg", [P, NT, E])
            lge = sb("lge", [P, NT, E])
            cand = sb("cand", [P, NT, E])
            loc_e = sb("loc_e", [P, NT, E])
            rt = sb("rt", [P, 8, NT])
            oh = sb("oh", [P, NT, E], BF16)
            seen = sb("seen", [P, NT + 1, E], BF16)
            slot_i = [sb(f"slot_i{i}", [P, NT], I32) for i in range(2)]

            S1 = [ps[0], ps[1]]
            S2 = [ps[2], ps[3]]
            PV = ps[4]
            RING = [ps[5], ps[6], ps[7]]

            def sig(name, per, by=1):
                return Signal(sem(name), per, by)

            x_in = sig("x_in", 1, 16)
            ln1_ready = sig("ln1_ready", NT)
            modb_ready = sig("modb_ready", 1)
            hT_ready = sig("hT_ready", KD)
            hTh_ready = sig("hTh_ready", KD)
            hTl_ready = sig("hTl_ready", KD)
            hbar_ready = sig("hbar_ready", KD)
            p1_ready, p2_ready, p3_ready = sig("part1_ready", 4), sig("part2_ready", 4), sig("part3_ready", 4)
            rest_ready = sig("rest_ready", 4)
            parts_stored = [sig(f"parts_stored{i}", 2, 16) for i in range(2)]
            stack_in = sig("stack_in", 12, 16)
            gq_ready, gk_ready = sig("gq_ready", 1), sig("gk_ready", 2)
            v_ready, v_shifted = sig("v_ready", NT), sig("v_shifted", 2, 16)
            gexp_ready = sig("gate_exp_ready", NT)
            gate_ready = sig("gate_ready", 1)
            s1_full, s1_free = sig("s1_full", 18), sig("s1_free", 18)
            mxp_ready = sig("max_parts_ready", 2)
            s2_full, exp_ready, pv_done = sig("s2_full", H), sig("exp_ready", H), sig("pv_done", H)
            pv_out = sig("pv_out", 4)
            lt_done = sig("local_done", 4)
            ring_full = sem("ring_full")
            rshift_ready, rexp_ready, rinv_ready = sig("r_shift_ready", NT), sig("r_exp_ready", NT), sig("r_inv_ready", NT)
            rprob_ready, prt_ready = sig("r_prob_ready", NT), sig("prt_ready", NT)
            remt_ready, rm_ready = sig("rem_t_ready", 1), sig("rm_ready", 2)
            o_ready, ot_ready = sig("o_ready", 2), sig("o_t_ready", 2)
            ao_ready, x1_ready, x1_stored = sig("attn_out_ready", 2), sig("x1_ready", 2), sig("x1_stored", 1, 16)
            xres_in, modbc_in = sig("x_again_in", 1, 16), sig("mod_bc_in", 1, 16)
            h2n_ready, h2_ready, h2t_ready = sig("h2_norm_ready", 2), sig("h2_ready", 2), sig("h2_t_ready", 2)
            lg_ready, lge_ready, oh_ready, slot_ready = sig("lg_ready", 1), sig("lg_exp_ready", 1), sig("onehot_ready", 1), sig("slot_ready", 1)
            scattered = sig("scattered", NT, 16)
            loc_ready = sig("loc_ready", 1)
            var1_ready, rstd1_ready = sig("var1_ready", 1), sig("rstd1_ready", 1)
            var2_ready, rstd2_ready = sig("var2_ready", 1), sig("rstd2_ready", 1)
            blanks, N_BLANKS = sem("buffers_blanked"), 11
            ln1_chain, hbar_chain = sig("ln1_chain", 2 * NT + 1), sig("hbar_chain", KD)
            gate_chain, mx_chain = sig("gate_chain", 1), sig("max_chain", 8)
            r_chain, lt_chain = sig("r_chain", 3 * NT), sig("lt_chain", 8)
            ln2_chain, route_chain = sig("ln2_chain", 2 * NT + 1), sig("route_chain", 13)
            add_chain = sig("modulate_chain", 2)
            read_by = {"A.GQ": (gq_ready, 1), "A.GK": (gk_ready, 1), "A.GV": (gk_ready, 2), "C.RP": (remt_ready, 1),
                       "D.LG": (lg_ready, 1), "D.LOC": (loc_ready, 1)}
            for i in range(2):
                read_by.update({f"A.T{i}": (hT_ready, i + 1), f"A.Q{i}": (rest_ready, i + 1), f"A.K{i}": (rest_ready, i + 3),
                                f"C.RO{i}": (rm_ready, i + 1), f"D.OT{i}": (ot_ready, i + 1), f"D.WO{i}": (ao_ready, i + 1),
                                f"D.H{i}": (h2t_ready, i + 1)})
            for i in range(4):
                read_by.update({f"A.V{i}": (gexp_ready, i + 1), f"C.R{i}": (rshift_ready, i + 1),
                                f"C.PR{i}": (prt_ready, i + 1), f"L.LT{i}": (lt_done, i + 1)})

            def steps(run):
                run("pro", -1, 1)
                run("first", 0, 0)
                run("mid", 1, 1)
                with run.engine.Fori(0, (B - 4) // 2) as i:
                    run("mid", i * 2 + 2, 0)
                    run("mid", i * 2 + 3, 1)
                run("mid", B - 2, 0)
                run("last", B - 1, 1)
                run("epi", B, 0)

            class Run:

                def __init__(self, engine, jobs, head=None):
                    self.engine, self.jobs, self.head = engine, jobs, head

                def __call__(self, kind, s, c):
                    for slot in range(17):
                        if self.head is not None:
                            self.head(kind, s, c, slot)
                        for name in SLOT_JOBS[slot]:
                            if name not in ORDER[kind]:
                                continue
                            stage, what = name.split(".")
                            b, p = batch_of(name, s), c if stage in "CL" else 1 - c
                            fn = self.jobs.get(what.rstrip("0123456789"))
                            if fn is not None:
                                fn(Job(kind, s, name), b, p, int(what[-1]) if what[-1].isdigit() else 0)

            def is0(b):
                return isinstance(b, int) and b == 0

            with nc.Block() as block:

                @block.tensor
                def _(pe):
                    mm = nc.tensor.matmul

                    def bank(job):
                        if job.before is not None:
                            name, b = job.before
                            last_read, k = read_by[name]
                            pe.wait_ge(last_read.sem, last_read.at(b, k))
                        return RING[job.bank]

                    def tr(dst, src, idn):
                        return mm(dst, src, idn, start=True, stop=True, is_transpose=True)

                    def mm3(dst, a, b_):
                        terms = [(a[i][k], b_[j][k]) for k in range(KD) for i, j in ((0, 0), (1, 0), (0, 1))]
                        for n, (l, r) in enumerate(terms):
                            last = mm(dst, l, r, start=(n == 0), stop=(n == len(terms) - 1))
                        return last

                    def job_T(job, b, p, k):
                        r = bank(job)
                        pe.wait_ge(ln1_ready.sem, ln1_ready.at(b, NT))
                        for t in range(NT):
                            last = tr(r[:, t * P:(t + 1) * P], xin[:, t, k * P:(k + 1) * P], ident[:, :])
                        last.then_inc(ring_full, 1)

                    def halves(hi, lo, c0, n):
                        return [[w[:, k, c0:c0 + n] for k in range(KD)] for w in (hi, lo)]

                    def proj(job, b, hi, lo, c0):
                        r = bank(job)
                        pe.wait_ge(hTl_ready.sem, hTl_ready.at(b, KD))
                        mm3(r[:, :], halves(hi, lo, c0, P), halves(hT_h, hT_l, 0, S)).then_inc(ring_full, 1)

                    def job_Q(job, b, p, m):
                        proj(job, b, wq_h, wq_l, m * P)

                    def job_K(job, b, p, m):
                        proj(job, b, wk_h, wk_l, m * P)

                    def job_GQ(job, b, p, m):
                        proj(job, b, wg_h, wg_l, 0)

                    def job_V(job, b, p, t):
                        r = bank(job)
                        mm3(r[:, 0:VG], halves(hT_h, hT_l, t * P, P), halves(wv_h, wv_l, 0, VG)).then_inc(ring_full, 1)

                    def job_GK(job, b, p, m):
                        r = bank(job)
                        pe.wait_ge(hbar_ready.sem, hbar_ready.at(b, KD))
                        for k in range(KD):
                            last = mm(r[:, 0:NL], wgk_s[:, k, :], hbar[:, k, 0, :], start=(k == 0), stop=(k == KD - 1))
                        last.then_inc(ring_full, 1)

                    def job_GV(job, b, p, m):
                        r = bank(job)
                        for k in range(KD):
                            last = mm(r[:, 0:LD], hbar[:, k, :, :], wgv_s[:, k, :], start=(k == 0), stop=(k == KD - 1))
                        last.then_inc(ring_full, 1)

                    def job_R(job, b, p, t):
                        r = bank(job)
                        pe.wait_ge(gq_ready.sem, gq_ready.at(b, 1))
                        pe.wait_ge(gk_ready.sem, gk_ready.at(b, 2))
                        mm(r[:, :], ident_b[:, :], mask_r[:, t, :, :], start=True, stop=False)
                        mm(r[:, :], gq_t[p][:, t * P:(t + 1) * P], gk_bd[p][:, :, :], start=False, stop=True).then_inc(ring_full, 1)

                    def job_PR(job, b, p, t):
                        r = bank(job)
                        pe.wait_ge(rprob_ready.sem, rprob_ready.at(b, t + 1))
                        for q in range(NP):
                            last = tr(r[:, q * P:(q + 1) * P], sr[:, t, 2 * q:2 * q + 2, :], ident[:, :])
                        last.then_inc(ring_full, 1)

                    def job_RP(job, b, p, m):
                        r = bank(job)
                        pe.wait_ge(prt_ready.sem, prt_ready.at(b, NT))
                        for q in range(NP):
                            last = mm(r[32 * q:32 * q + 32, :], gv_bd[p][:, q, :, :], pr_t[:, q, :], start=True, stop=True)
                        last.then_inc(ring_full, 1)

                    def job_RO(job, b, p, j):
                        r = bank(job)
                        pe.wait_ge(remt_ready.sem, remt_ready.at(b, 1))
                        for i in range(2):
                            t = 2 * j + i
                            last = mm(r[:, i * D:(i + 1) * D], rem_t[:, t * P:(t + 1) * P], rout_s[:, :], start=True, stop=True)
                        last.then_inc(ring_full, 1)

                    def job_LT(job, b, p, g):
                        r = bank(job)
                        pe.wait_ge(pv_out.sem, pv_out.at(b, g + 1))
                        for t in range(NT):
                            last = tr(r[:, t * P:(t + 1) * P], pv_s[:, t * P:(t + 1) * P], ident[:, :])
                        last.then_inc(ring_full, 1)

                    def pair_tr(job, src, j):
                        r = bank(job)
                        for i in range(2):
                            for k in range(KD):
                                at = (i * KD + k) * P
                                last = tr(r[:, at:at + P], src[:, 2 * j + i, k * P:(k + 1) * P], ident[:, :])
                        last.then_inc(ring_full, 1)

                    def job_OT(job, b, p, j):
                        pe.wait_ge(o_ready.sem, o_ready.at(b, j + 1))
                        pair_tr(job, o, j)

                    def job_WO(job, b, p, j):
                        r = bank(job)
                        pe.wait_ge(ot_ready.sem, ot_ready.at(b, j + 1))
                        for i in range(2):
                            t = 2 * j + i
                            for k in range(KD):
                                last = mm(r[:, i * D:(i + 1) * D], d_t[:, k, t * P:(t + 1) * P], wout_s[:, k, :],
                                          start=(k == 0), stop=(k == KD - 1))
                        last.then_inc(ring_full, 1)

                    def job_H(job, b, p, j):
                        pe.wait_ge(h2_ready.sem, h2_ready.at(b, j + 1))
                        pair_tr(job, h2, j)

                    def job_LG(job, b, p, j):
                        r = bank(job)
                        pe.wait_ge(h2t_ready.sem, h2t_ready.at(b, 2))
                        for t in range(NT):
                            for k in range(KD):
                                last = mm(r[:, t * E:(t + 1) * E], d_t[:, k, t * P:(t + 1) * P], gate_t[:, k, :],
                                          start=(k == 0), stop=(k == KD - 1))
                        last.then_inc(ring_full, 1)

                    def job_LOC(job, b, p, j):
                        r = bank(job)
                        pe.wait_ge(oh_ready.sem, oh_ready.at(b, 1))
                        mm(r[:, 0:NT * E], tri[:, :], oh[:, :, :], start=True, stop=False)
                        mm(r[:, 0:NT * E], ones_b[:, :], seen[:, 0:NT, :], start=False, stop=True).then_inc(ring_full, 1)

                    def s1_wait(b, half, n):
                        if not (is0(b) and half == 0 and n < 2):
                            pe.wait_ge(s1_free.sem, s1_free.at(b, 9 * half + n - 1))

                    def scores_q(b, p, h):
                        half, n = divmod(h, HH)
                        if n == 0 and half == 0:
                            pe.wait_ge(stack_in.sem, stack_in.at(b, 12))
                        s1_wait(b, half, n)
                        r = S1[(9 * half + n) % 2]
                        mm(r[:, :], ident_b[:, :], mask_q[:, :, :], start=True, stop=False, skip_group_check=True)
                        for w in range(NB):
                            t, a = divmod(w, 2)
                            last = mm(r[64 * a:64 * a + 64, t * P:(t + 1) * P], q_st[p][:, h, w * W:(w + 1) * W],
                                      k_st[p][:, h, w * W:w * W + 2 * W], start=False, stop=(w == NB - 1), skip_group_check=True)
                        last.then_inc(s1_full.sem, 1)

                    def max_rows(b, p, half):
                        pe.wait_ge(mxp_ready.sem, mxp_ready.at(b, half + 1))
                        s1_wait(b, half, HH)
                        r = S1[(9 * half + HH) % 2][:, 0:S // 2].bitcast(BF16)
                        for t in range(NT):
                            last = tr(r[:, t * P:(t + 1) * P], mx_p[half][:, t, :], ident_b[:, :])
                        last.then_inc(s1_full.sem, 1)

                    def scores_k(b, p, h):
                        half, n = divmod(h, HH)
                        if n == 0:
                            pe.wait_ge(s1_free.sem, s1_free.at(b, 9 * half + 9))
                        if not (is0(b) and h < 2):
                            pe.wait_ge(exp_ready.sem, exp_ready.at(b, h - 1))
                        r = S2[h % 2]
                        mm(r[:, :], ident_b[:, :], mask_k[:, :, :], start=True, stop=False, skip_group_check=True)
                        mm(r[:, :], pick[:, n, :], mx_t[half][:, :], start=False, stop=False, skip_group_check=True)
                        for w in range(NB):
                            last = mm(r[:, w * W:(w + 1) * W], k_st[p][:, h, w * W:w * W + 2 * W],
                                      q_st[p][:, h, w * W:(w + 1) * W], start=False, stop=(w == NB - 1), skip_group_check=True)
                        last.then_inc(s2_full.sem, 1)

                    def weigh_values(b, p, h):
                        if h == 0:
                            pe.wait_ge(v_shifted.sem, v_shifted.at(b, 2))
                        if h % 4 == 0 and not (is0(b) and h == 0):
                            pe.wait_ge(pv_out.sem, pv_out.at(b, h // 4))
                        pe.wait_ge(exp_ready.sem, exp_ready.at(b, h + 1))
                        g = h % 4
                        for w in range(NB):
                            v = v_al[p][:, w // 2, h, :] if w % 2 else v_sh[p][:, w // 2, h, :]
                            last = mm(PV[32 * g:32 * g + VW, w * W:(w + 1) * W], v, p_t[h % NPT][:, w * W:(w + 1) * W],
                                      start=True, stop=True, skip_group_check=True)
                        last.then_inc(pv_done.sem, 1)

                    def head(kind, s, c, slot):
                        if kind in ("first", "mid", "last"):
                            if slot < 4:
                                for h in (2 * slot, 2 * slot + 1):
                                    scores_q(s, c, HH + h)
                            if 10 <= slot < 14 and kind != "last":
                                for h in (2 * (slot - 10), 2 * (slot - 10) + 1):
                                    scores_q(s + 1, 1 - c, h)
                            if slot < H:
                                scores_k(s, c, slot)
                            if slot == 6:
                                max_rows(s, c, 1)
                            if slot == 15 and kind != "last":
                                max_rows(s + 1, 1 - c, 0)
                            if slot >= 1:
                                weigh_values(s, c, slot - 1)
                        elif kind == "pro" and slot == 16:
                            for h in range(HH):
                                scores_q(0, 0, h)
                            max_rows(0, 0, 0)

                    pe.wait_ge(blanks, N_BLANKS)
                    steps(Run(pe, {"T": job_T, "Q": job_Q, "K": job_K, "GQ": job_GQ, "V": job_V, "GK": job_GK, "GV": job_GV,
                                   "R": job_R, "PR": job_PR, "RP": job_RP, "RO": job_RO, "LT": job_LT, "OT": job_OT,
                                   "WO": job_WO, "H": job_H, "LG": job_LG, "LOC": job_LOC}, head))

                @block.scalar
                def _(act):
                    def full(job):
                        act.wait_ge(ring_full, job.done)
                        return RING[job.bank]

                    def job_T(job, b, p, k):
                        r = full(job)
                        act.wait_ge(modb_ready.sem, modb_ready.at(b, 1))
                        if not is0(b):
                            act.wait_ge(hbar_ready.sem, hbar_ready.at(b - 1, KD))
                            act.wait_ge(hTl_ready.sem, hTl_ready.at(b - 1, KD))
                        nc.scalar.activation(hT[:, k, :], r[:, :], ACT.Identity, bias=mod_b[:, 0, k:k + 1],
                                             scale=mod_b[:, 1, k:k + 1]).then_inc(hT_ready.sem, 1)

                    def first_part(job, b, m, scale):
                        r = full(job)
                        if not (is0(b) and m < 2):
                            act.wait_ge(parts_stored[m % 2].sem, parts_stored[m % 2].at(b, m // 2))
                        nc.scalar.activation(parts[m % 2][:, 0, :], r[:, :], ACT.Copy, scale=scale).then_inc(p1_ready.sem, 1)

                    def job_Q(job, b, p, m):
                        first_part(job, b, m, HD ** -0.5)

                    def job_K(job, b, p, m):
                        first_part(job, b, 2 + m, 1.0)

                    def job_GQ(job, b, p, m):
                        r = full(job)
                        nc.scalar.activation(gq_t[p][:, :], r[:, :], ACT.Copy, scale=HD ** -0.5).then_inc(gq_ready.sem, 1)

                    def job_V(job, b, p, t):
                        r = full(job)
                        nc.scalar.activation(v_al[p][:, t, :, 0:HD], r[:, 0:D].rearrange("p (h d) -> p h d", d=HD),
                                             ACT.Copy).then_inc(v_ready.sem, 1)
                        nc.scalar.activation(gates[p][:, t, :], r[:, D:VG], ACT.Exp, scale=-1.0).then_inc(gexp_ready.sem, 1)

                    def job_R(job, b, p, t):
                        act.wait_ge(rshift_ready.sem, rshift_ready.at(b, t + 1))
                        nc.scalar.activation(sr[:, t, :, :], sr[:, t, :, :], ACT.Exp).then_inc(rexp_ready.sem, 1)

                    def job_PR(job, b, p, t):
                        r = full(job)
                        nc.scalar.activation(pr_t[:, :, t * P:(t + 1) * P], r[:, :].rearrange("p (q n) -> p q n", q=NP),
                                             ACT.Copy).then_inc(prt_ready.sem, 1)

                    def job_RP(job, b, p, m):
                        r = full(job)
                        nc.scalar.activation(rem_t[:, :], r[:, :], ACT.Copy).then_inc(remt_ready.sem, 1)

                    def pair_out(job, j, ready):
                        r = full(job)
                        nc.scalar.activation(d_t[:, :, 2 * j * P:(2 * j + 2) * P].rearrange("p k (t n) -> p t k n", t=2),
                                             r[:, :].rearrange("p (t k n) -> p t k n", t=2, k=KD), ACT.Copy).then_inc(ready.sem, 1)

                    def job_OT(job, b, p, j):
                        pair_out(job, j, ot_ready)

                    def job_H(job, b, p, j):
                        pair_out(job, j, h2t_ready)

                    def job_LG(job, b, p, j):
                        act.wait_ge(lg_ready.sem, lg_ready.at(b, 1))
                        nc.scalar.activation(lge[:, :, :], lg[:, :, :], ACT.Exp).then_inc(lge_ready.sem, 1)

                    def head(kind, s, c, slot):
                        if kind not in ("first", "mid", "last"):
                            return
                        if slot in (5, 9, 13, 16):
                            g = {5: 0, 9: 1, 13: 2, 16: 3}[slot]
                            act.wait_ge(pv_done.sem, pv_done.at(s, 4 * g + 4))
                            nc.scalar.activation(pv_s[:, :], PV[:, :], ACT.Copy).then_inc(pv_out.sem, 1)
                        if slot < H:
                            act.wait_ge(s2_full.sem, s2_full.at(s, slot + 1))
                            if not (is0(s) and slot < NPT):
                                act.wait_ge(pv_done.sem, pv_done.at(s, slot - NPT + 1))
                            nc.scalar.activation(p_t[slot % NPT][:, :], S2[slot % 2][:, :], ACT.Exp).then_inc(exp_ready.sem, 1)

                    steps(Run(act, {"T": job_T, "Q": job_Q, "K": job_K, "GQ": job_GQ, "V": job_V, "R": job_R, "PR": job_PR,
                                    "RP": job_RP, "OT": job_OT, "H": job_H, "LG": job_LG}, head))

                @block.vector
                def _(dve):
                    v = nc.vector

                    def chained(ins, chain, b, k):
                        ins.then_inc(chain.sem, 1)
                        dve.wait_ge(chain.sem, chain.at(b, k))

                    def full(job):
                        dve.wait_ge(ring_full, job.done)
                        return RING[job.bank]

                    def norm(x_, y_, b, chain, var, rstd, ready, per_pair):
                        for t in range(NT):
                            v.bn_stats(ln_raw[:, t, :], x_[:, t, :]).then_inc(chain.sem, 1)
                        dve.wait_ge(chain.sem, chain.at(b, NT))
                        v.memset(ln_ve[:, :], EPS).then_inc(chain.sem, 1)
                        for t in range(NT):
                            v.bn_aggr(ln_mv[:, t, :], ln_raw[:, t, :]).then_inc(chain.sem, 1)
                        dve.wait_ge(chain.sem, chain.at(b, 2 * NT + 1))
                        v.tensor_tensor(ln_ve[:, :], ln_ve[:, :], ln_mv[:, :, 1], ALU.add).then_inc(var.sem, 1)
                        dve.wait_ge(rstd.sem, rstd.at(b, 1))
                        for t in range(NT):
                            last = v.tensor_scalar(y_[:, t, :], x_[:, t, :], ln_mv[:, t, 0:1], ln_rs[:, t:t + 1], ALU.subtract, ALU.mult)
                            if (t + 1) % per_pair == 0:
                                last.then_inc(ready.sem, 1)

                    def first_norm(b):
                        dve.wait_ge(x_in.sem, x_in.at(b, 1))
                        norm(xin, xin, b, ln1_chain, var1_ready, rstd1_ready, ln1_ready, 1)
                        if not is0(b):
                            dve.wait_ge(hT_ready.sem, hT_ready.at(b - 1, KD))
                        v.tensor_copy(mod_b[:, :, :], mod_t[:, b, :, :]).then_inc(modb_ready.sem, 1)

                    def job_T(job, b, p, k):
                        dve.wait_ge(hT_ready.sem, hT_ready.at(b, k + 1))
                        v.tensor_copy(hT_h[:, k, :], hT[:, k, :]).then_inc(hTh_ready.sem, 1)
                        chained(v.tensor_reduce(hbar[:, k, 0, :], hT[:, k, :].rearrange("p (n c) -> p n c", c=CH), AX_X, ALU.add),
                                hbar_chain, b, k + 1)
                        v.tensor_copy(hbar[:, k, 1, :], hbar[:, k, 0, :]).then_inc(hbar_ready.sem, 1)

                    def part_rest(job, b, m, scale):
                        r = RING[job.bank]
                        dve.wait_ge(p1_ready.sem, p1_ready.at(b, m + 1))
                        if not (is0(b) and m < 2):
                            dve.wait_ge(p3_ready.sem, p3_ready.at(b, m - 1))
                        v.scalar_tensor_tensor(rest[m % 2][:, :], r[:, :], scale, parts[m % 2][:, 0, :], ALU.mult,
                                               ALU.subtract).then_inc(rest_ready.sem, 1)
                        dve.wait_ge(rest_ready.sem, rest_ready.at(b, m + 1))
                        v.tensor_copy(parts[m % 2][:, 1, :], rest[m % 2][:, :]).then_inc(p2_ready.sem, 1)

                    def job_Q(job, b, p, m):
                        part_rest(job, b, m, HD ** -0.5)

                    def job_K(job, b, p, m):
                        part_rest(job, b, 2 + m, 1.0)

                    def job_V(job, b, p, t):
                        if t == NT - 1:
                            dve.wait_ge(gexp_ready.sem, gexp_ready.at(b, NT))
                            chained(v.tensor_scalar(gates[p][:, :, :], gates[p][:, :, :], 1.0, None, ALU.add), gate_chain, b, 1)
                            v.reciprocal(gates[p][:, :, :], gates[p][:, :, :]).then_inc(gate_ready.sem, 1)

                    def job_GK(job, b, p, m):
                        r = full(job)
                        v.scalar_tensor_tensor(gk_bd[p][:, :, :], bc(r[:, 0:NL].unsqueeze(1), [P, LH, NL]), 1.0 / CH,
                                               bc(head_rows[:, :].unsqueeze(2), [P, LH, NL]), ALU.mult, ALU.mult).then_inc(gk_ready.sem, 1)

                    def job_GV(job, b, p, m):
                        r = full(job)
                        v.scalar_tensor_tensor(gv_bd[p][:, :, :, :], r[:, 0:LD].rearrange("p (q e d) -> p q e d", q=NP, e=2), 1.0 / CH,
                                               pair_rows[:, :, :, :], ALU.mult, ALU.mult).then_inc(gk_ready.sem, 1)

                    def job_R(job, b, p, t):
                        r = full(job)
                        r3 = r[:, :].rearrange("p (h n) -> p h n", h=LH)
                        chained(v.tensor_reduce(rstat[:, 0, t, :], r3, AX_X, ALU.max, negate=True), r_chain, b, 3 * t + 1)
                        v.tensor_tensor(sr[:, t, :, :], r3, bc(rstat[:, 0, t, :].unsqueeze(2), [P, LH, NL]),
                                        ALU.add).then_inc(rshift_ready.sem, 1)
                        dve.wait_ge(rexp_ready.sem, rexp_ready.at(b, t + 1))
                        chained(v.tensor_reduce(rstat[:, 1, t, :], sr[:, t, :, :], AX_X, ALU.add), r_chain, b, 3 * t + 2)
                        chained(v.reciprocal(rstat[:, 2, t, :], rstat[:, 1, t, :]), r_chain, b, 3 * t + 3)
                        v.tensor_copy(rstat[:, 1, t, :], rstat[:, 2, t, :]).then_inc(rinv_ready.sem, 1)

                    def job_RO(job, b, p, j):
                        r = full(job)
                        dve.wait_ge(gate_ready.sem, gate_ready.at(b, 1))
                        if not is0(b):
                            dve.wait_ge(o_ready.sem, o_ready.at(b - 1, 2))
                        v.tensor_tensor(rm[:, 2 * j:2 * j + 2, :].rearrange("p t (h d) -> p t h d", d=HD),
                                        r[:, :].rearrange("p (t h d) -> p t h d", t=2, d=HD),
                                        bc(gates[p][:, 2 * j:2 * j + 2, H:2 * H].unsqueeze(3), [P, 2, H, HD]),
                                        ALU.mult).then_inc(rm_ready.sem, 1)

                    def job_LT(job, b, p, g):
                        r = full(job)
                        r4 = r[:, :].rearrange("p (t h d) -> p t h d", t=NT, d=32)
                        dve.wait_ge(gate_ready.sem, gate_ready.at(b, 1))
                        chained(v.reciprocal(fac[:, 0, :, :], r4[:, :, :, HD]), lt_chain, b, 2 * g + 1)
                        chained(v.tensor_tensor(fac[:, 1, :, :], fac[:, 0, :, :], gates[p][:, :, 4 * g:4 * g + 4], ALU.mult),
                                lt_chain, b, 2 * g + 2)
                        v.tensor_tensor(o[:, :, g * 64:g * 64 + 64].rearrange("p t (h d) -> p t h d", d=HD), r4[:, :, :, 0:HD],
                                        bc(fac[:, 1, :, :].unsqueeze(3), [P, NT, 4, HD]), ALU.mult).then_inc(lt_done.sem, 1)

                    def job_WO(job, b, p, j):
                        r = full(job)
                        dve.wait_ge(modbc_in.sem, modbc_in.at(b, 1))
                        if not is0(b):
                            dve.wait_ge(scattered.sem, scattered.at(b - 1, NT))
                        v.tensor_tensor(h2[:, 2 * j:2 * j + 2, :], r[:, :].rearrange("p (t d) -> p t d", t=2),
                                        bc(mod_bc[:, 0:1, :], [P, 2, D]), ALU.mult).then_inc(ao_ready.sem, 1)

                    def second_norm(b):
                        dve.wait_ge(x1_ready.sem, x1_ready.at(b, 2))
                        norm(x1, h2, b, ln2_chain, var2_ready, rstd2_ready, h2n_ready, 2)

                    def job_LG(job, b, p, j):
                        r = full(job)
                        r3 = r[:, 0:NT * E].rearrange("p (t e) -> p t e", e=E)
                        chained(v.tensor_reduce(rt[:, 0, :], r3, AX_X, ALU.max), route_chain, b, 1)
                        v.tensor_tensor(lg[:, :, :], r3, bc(rt[:, 0, :].unsqueeze(2), [P, NT, E]), ALU.subtract).then_inc(lg_ready.sem, 1)
                        dve.wait_ge(lg_ready.sem, lg_ready.at(b, 1))
                        chained(v.tensor_scalar(cand[:, :, :], lg[:, :, :], 0.0, -float(E), ALU.is_ge, ALU.mult), route_chain, b, 2)
                        chained(v.tensor_tensor(cand[:, :, :], cand[:, :, :], bc(iota_f[:, :].unsqueeze(1), [P, NT, E]), ALU.add),
                                route_chain, b, 3)
                        chained(v.tensor_reduce(rt[:, 1, :], cand[:, :, :], AX_X, ALU.min), route_chain, b, 4)
                        chained(v.tensor_tensor(oh[:, :, :], cand[:, :, :], bc(rt[:, 1, :].unsqueeze(2), [P, NT, E]), ALU.is_equal),
                                route_chain, b, 5)
                        if not is0(b):
                            chained(v.tensor_copy(seen[:, 0, :], seen[:, NT, :]), route_chain, b, 6)
                        else:
                            chained(v.memset(seen[:, 0, :], 0.0), route_chain, b, 6)
                        for t in range(NT):
                            last = v.tensor_tensor(seen[:, t + 1, :], seen[:, t, :], oh[:, t, :], ALU.add)
                            if t < NT - 1:
                                chained(last, route_chain, b, 7 + t)
                            else:
                                last.then_inc(oh_ready.sem, 1)
                        dve.wait_ge(lge_ready.sem, lge_ready.at(b, 1))
                        chained(v.tensor_reduce(rt[:, 2, :], lge[:, :, :], AX_X, ALU.add), route_chain, b, 10)
                        v.reciprocal(prob_all[:, bass.ds(b * NT, NT)], rt[:, 2, :])

                    def job_LOC(job, b, p, j):
                        r = full(job)
                        v.tensor_tensor(loc_e[:, :, :], r[:, 0:NT * E].rearrange("p (t e) -> p t e", e=E), oh[:, :, :],
                                        ALU.mult).then_inc(loc_ready.sem, 1)
                        dve.wait_ge(loc_ready.sem, loc_ready.at(b, 1))
                        chained(v.tensor_reduce(rt[:, 3, :], loc_e[:, :, :], AX_X, ALU.add), route_chain, b, 11)
                        v.tensor_scalar(rt[:, 4, :], rt[:, 3, :], float(CAP), None, ALU.is_le)
                        chained(v.scalar_tensor_tensor(rt[:, 5, :], rt[:, 1, :], float(CAP), rt[:, 3, :], ALU.mult, ALU.add),
                                route_chain, b, 12)
                        chained(v.scalar_tensor_tensor(rt[:, 6, :], rt[:, 5, :], -1.0, rt[:, 4, :], ALU.add, ALU.mult), route_chain, b, 13)
                        v.tensor_scalar(slot_all[:, bass.ds(b * NT, NT)], rt[:, 6, :], float(SLOTS), None, ALU.add)
                        v.tensor_scalar(slot_i[p][:, :], rt[:, 6, :], float(SLOTS), None, ALU.add).then_inc(slot_ready.sem, 1)

                    def take_max(b, h, n):
                        dve.wait_ge(s1_full.sem, s1_full.at(b, 9 * (h // HH) + n + 1))
                        v.tensor_reduce(nmx[:, :, h], S1[(9 * (h // HH) + n) % 2][:, :].rearrange("p (t j) -> p t j", t=NT),
                                        AX_X, ALU.max, negate=True).then_inc(s1_free.sem, 1)

                    def max_parts(b, half):
                        dve.wait_ge(s1_free.sem, s1_free.at(b, 9 * half + HH))
                        m = nmx[:, :, half * HH:(half + 1) * HH]
                        pt = [mx_p[half][:, :, j * HH:(j + 1) * HH] for j in range(3)]
                        k = 4 * half
                        chained(v.tensor_copy(pt[0], m), mx_chain, b, k + 1)
                        chained(v.tensor_tensor(nmx_r[:, :, :], m, pt[0], ALU.subtract), mx_chain, b, k + 2)
                        chained(v.tensor_copy(pt[1], nmx_r[:, :, :]), mx_chain, b, k + 3)
                        chained(v.tensor_tensor(nmx_r[:, :, :], nmx_r[:, :, :], pt[1], ALU.subtract), mx_chain, b, k + 4)
                        v.tensor_copy(pt[2], nmx_r[:, :, :]).then_inc(mxp_ready.sem, 1)

                    def max_rows_out(b, half):
                        dve.wait_ge(s1_full.sem, s1_full.at(b, 9 * half + 9))
                        v.tensor_copy(mx_t[half][:, :], S1[(9 * half + HH) % 2][:, 0:S // 2].bitcast(BF16)).then_inc(s1_free.sem, 1)

                    def head(kind, s, c, slot):
                        if kind in ("mid", "last", "epi") and slot == 7:
                            second_norm(s - 1)
                        if kind in ("first", "mid", "last"):
                            if slot == 0 and kind != "last":
                                first_norm(s + 1)
                            if slot < 4:
                                for n in (2 * slot, 2 * slot + 1):
                                    take_max(s, HH + n, n)
                            if slot == 4:
                                max_parts(s, 1)
                            if slot == 7:
                                max_rows_out(s, 1)
                            if kind != "last":
                                if 10 <= slot < 14:
                                    for n in (2 * (slot - 10), 2 * (slot - 10) + 1):
                                        take_max(s + 1, n, n)
                                if slot == 14:
                                    max_parts(s + 1, 0)
                                if slot == 16:
                                    max_rows_out(s + 1, 0)
                        elif kind == "pro":
                            if slot == 0:
                                first_norm(0)
                            if slot == 16:
                                for n in range(HH):
                                    take_max(0, n, n)
                                max_parts(0, 0)
                                max_rows_out(0, 0)

                    for i in range(2):
                        v.memset(k_st[i][:, :, 0:W], 0.0).then_inc(blanks, 1)
                        v.memset(v_al[i][:, :, :, HD:VW], 1.0).then_inc(blanks, 1)
                        v.memset(v_sh[i][0:64, 0, :, :], 0.0).then_inc(blanks, 1)
                        v.memset(mx_p[i][:, :, :], 0.0).then_inc(blanks, 1)
                    v.memset(PV[:, :], 0.0).then_inc(blanks, 3)
                    steps(Run(dve, {"T": job_T, "Q": job_Q, "K": job_K, "V": job_V, "GK": job_GK, "GV": job_GV, "R": job_R,
                                    "RO": job_RO, "LT": job_LT, "WO": job_WO, "LG": job_LG, "LOC": job_LOC}, head))

                @block.gpsimd
                def _(pool):
                    g = nc.gpsimd

                    def job_T(job, b, p, k):
                        pool.wait_ge(hTh_ready.sem, hTh_ready.at(b, k + 1))
                        g.tensor_tensor(hT_l[:, k, :], hT[:, k, :], hT_h[:, k, :].bitcast(F32), ALU.subtract).then_inc(hTl_ready.sem, 1)

                    def third_part(b, m):
                        pool.wait_ge(p2_ready.sem, p2_ready.at(b, m + 1))
                        g.tensor_tensor(parts[m % 2][:, 2, :], rest[m % 2][:, :], parts[m % 2][:, 1, :],
                                        ALU.subtract).then_inc(p3_ready.sem, 1)

                    def job_Q(job, b, p, m):
                        third_part(b, m)

                    def job_K(job, b, p, m):
                        third_part(b, 2 + m)

                    def job_R(job, b, p, t):
                        pool.wait_ge(rinv_ready.sem, rinv_ready.at(b, t + 1))
                        g.tensor_tensor(sr[:, t, :, :], sr[:, t, :, :], bc(rstat[:, 1, t, :].unsqueeze(2), [P, LH, NL]),
                                        ALU.mult).then_inc(rprob_ready.sem, 1)

                    def add_latent(b):
                        pool.wait_ge(lt_done.sem, lt_done.at(b, 4))
                        pool.wait_ge(rm_ready.sem, rm_ready.at(b, 2))
                        for j in range(2):
                            g.tensor_tensor(o[:, 2 * j:2 * j + 2, :], o[:, 2 * j:2 * j + 2, :], rm[:, 2 * j:2 * j + 2, :],
                                            ALU.add).then_inc(o_ready.sem, 1)

                    def job_WO(job, b, p, j):
                        pool.wait_ge(ao_ready.sem, ao_ready.at(b, j + 1))
                        pool.wait_ge(xres_in.sem, xres_in.at(b, 1))
                        g.tensor_tensor(x1[:, 2 * j:2 * j + 2, :], x1[:, 2 * j:2 * j + 2, :], h2[:, 2 * j:2 * j + 2, :],
                                        ALU.add).then_inc(x1_ready.sem, 1)

                    def modulate(b, p):
                        for j in range(2):
                            pool.wait_ge(h2n_ready.sem, h2n_ready.at(b, j + 1))
                            h = h2[:, 2 * j:2 * j + 2, :]
                            g.tensor_tensor(h, h, bc(mod_bc[:, 1:2, :], [P, 2, D]), ALU.mult).then_inc(add_chain.sem, 1)
                            pool.wait_ge(add_chain.sem, add_chain.at(b, j + 1))
                            g.tensor_tensor(h, h, bc(mod_bc[:, 2:3, :], [P, 2, D]), ALU.add).then_inc(h2_ready.sem, 1)

                    def job_LOC(job, b, p, j):
                        pool.wait_ge(slot_ready.sem, slot_ready.at(b, 1))
                        pool.wait_ge(h2_ready.sem, h2_ready.at(b, 2))
                        g.tensor_tensor(turn[:, :], blank_row[:, :], blank_row[:, :], ALU.add)
                        for t in range(NT):
                            g.indirect_dma_start(xs_d, bass.IndirectOffsetOnAxis(slot_i[p][:, t:t + 1], 0), h2[:, t, :], None,
                                                 bounds_check=SLOTS - 1, oob_is_err=False).then_inc(scattered.sem, 16)

                    def inverse_deviation(b, var, rstd):
                        pool.wait_ge(var.sem, var.at(b, 1))
                        g.tensor_tensor(ln_rs[:, :], ln_ve[:, :], neg_half[:, :], ALU.pow).then_inc(rstd.sem, 1)

                    def head(kind, s, c, slot):
                        if slot == 0:
                            if kind in ("mid", "last", "epi"):
                                add_latent(s - 1)
                            if kind in ("pro", "first", "mid"):
                                inverse_deviation(s + 1, var1_ready, rstd1_ready)
                        if slot == 7 and kind in ("mid", "last", "epi"):
                            inverse_deviation(s - 1, var2_ready, rstd2_ready)
                            modulate(s - 1, 1 - c)

                    g.memset(neg_half[:, :], -0.5).then_inc(sem("exponent_set"), 1)
                    pool.wait_ge(sem("exponent_set"), 1)

                    steps(Run(pool, {"T": job_T, "Q": job_Q, "K": job_K, "R": job_R, "WO": job_WO, "LOC": job_LOC}, head))
                    pool.wait_ge(scattered.sem, scattered.at(B - 1, NT))

                @block.sync
                def _(sp):
                    xv = x.rearrange("b (t p) d -> b p t d", p=P)

                    def head(kind, s, c, slot):
                        if kind in ("pro", "first", "mid"):
                            b, p = s + 1, 1 - c
                            if slot == 0:
                                if not is0(b):
                                    sp.wait_ge(hT_ready.sem, hT_ready.at(b - 1, KD))
                                sp.dma_start(xin[:, :, :], xv[b]).then_inc(x_in.sem, 16)
                            if slot == 4:
                                for m in range(4):
                                    sp.wait_ge(p3_ready.sem, p3_ready.at(b, m + 1))
                                    sp.dma_start(qk_d[p, m // 2, :, (m % 2) * P:(m % 2 + 1) * P, :].rearrange("j r n -> r j n"),
                                                 parts[m % 2][:, :, :]).then_inc(parts_stored[m % 2].sem, 16)
                                for kq, (dst, off, slots) in enumerate(((q_st[p], 0, QPART), (k_st[p], W, KPART))):
                                    for i in range(2):
                                        sp.wait_ge(parts_stored[i].sem, parts_stored[i].at(b, kq + 1))
                                    for n, part in enumerate(slots):
                                        sp.dma_start(dst[16 * n:16 * n + 16, :, off:off + S],
                                                     qk_d[p, kq, part, :, :].rearrange("(h r) n -> r h n", r=HD)).then_inc(stack_in.sem, 16)
                            if slot == 8:
                                sp.wait_ge(blanks, N_BLANKS)
                                sp.wait_ge(v_ready.sem, v_ready.at(b, NT))
                                sp.dma_start(v_sh[p][64:128, :, :, :], v_al[p][0:64, :, :, :]).then_inc(v_shifted.sem, 16)
                                sp.dma_start(v_sh[p][0:64, 1:NT, :, :], v_al[p][64:128, 0:NT - 1, :, :]).then_inc(v_shifted.sem, 16)
                        if kind in ("mid", "last", "epi"):
                            b, p = s - 1, 1 - c
                            if slot == 0:
                                if not is0(b):
                                    sp.wait_ge(x1_stored.sem, x1_stored.at(b - 1, 1))
                                    sp.wait_ge(h2_ready.sem, h2_ready.at(b - 1, 2))
                                sp.dma_start(x1[:, :, :], xv[b]).then_inc(xres_in.sem, 16)
                                sp.dma_start(mod_bc[:, :, :], mod_d[b, 0:3, :].unsqueeze(0).to_broadcast([P, 3, D])).then_inc(modbc_in.sem, 16)
                            if slot == 6:
                                sp.wait_ge(x1_ready.sem, x1_ready.at(b, 2))
                                sp.dma_start(x1_d[b].rearrange("t p d -> p t d"), x1[:, :, :]).then_inc(x1_stored.sem, 16)

                    steps(Run(sp, {}, head))
                    sp.wait_ge(x1_stored.sem, x1_stored.at(B - 1, 1))

        ffn = ExitStack()
        with ffn:
            def fb(name, shape, dt=F32):
                return alloc(ffn, name, shape, dt)

            w1_f = [fb(f"w1_f{i}", [P, KD, HID]) for i in range(2)]
            w2_f = [fb(f"w2_f{i}", [P, MH, D]) for i in range(2)]
            w1_h, w1_l = fb("w1_h", [P, KD, HID], F32R), fb("w1_l", [P, KD, HID], F32R)
            w2_h, w2_l = fb("w2_h", [P, MH, D], F32R), fb("w2_l", [P, MH, D], F32R)
            xg = [fb(f"xg{i}", [P, 3, D]) for i in range(2)]
            xt_h, xt_l = fb("xt_h", [P, KD, CAP], F32R), fb("xt_l", [P, KD, CAP], F32R)
            h_h, h_l = fb("h_h", [P, MH, CAP], F32R), fb("h_l", [P, MH, CAP], F32R)
            y_t = fb("y_t", [P, KD, CAP])
            y_s = fb("y_s", [P, 3, D])
            yg = [fb(f"yg{i}", [P, NT, D]) for i in range(2)]
            x1b = [fb(f"x1b{i}", [P, NT, D]) for i in range(2)]
            gb = [fb(f"gb{i}", [P, 1, D]) for i in range(2)]
            XT = [ps[0], ps[1]]
            YA = [ps[2], ps[3]]
            YT = ps[4]
            UP = [ps[5], ps[6], ps[7]]
            NU = len(UP)
            LASTROWS = UP[5 % NU]

            def esig(name, per, by=1):
                return Signal(sem(name), per, by)

            w1_in, w2_in, xg_in = ([esig(f"{name}{i}", per, 16) for i in range(2)] for name, per in (("w1_in", 1), ("w2_in", 1), ("xg_in", 3)))
            w1h_ready, w1_split = esig("w1_hi", KD), esig("w1_split", KD)
            w2h_ready, w2_split = esig("w2_hi", 4), esig("w2_split", 4)
            xt_full, xth_ready, xt_split = esig("xt_full", 1), esig("xt_hi", KD), esig("xt_split", KD)
            up_full, hh_ready, h_split = esig("up_full", MH), esig("h_hi", MH), esig("h_split", MH)
            down_full, yt_ready = esig("down_full", KD), esig("y_t_ready", KD)
            ytr_full, ys_ready, ys_stored = esig("y_rows_full", 1), esig("y_rows_ready", 2), esig("y_rows_stored", 3, 16)
            gathered, x1_back, gb_in, out_stored = ([esig(f"{name}{i}", per, 16) for i in range(2)] for name, per in
                                                    (("gathered", NT), ("x1_back", 1), ("gb_in", 1), ("out_stored", 1)))
            comb, out_ready = esig("combine_chain", 2 * NT), esig("out_ready", 1)

            def expert_steps(eng, run):
                run("first", 0, 0, 0)
                run("mid", 0, 1, 1)
                with eng.Fori(0, (E - 4) // 2) as i:
                    run("mid", i + 1, 0, i * 2 + 2)
                    run("mid", i + 1, 1, i * 2 + 3)
                run("noload", E // 2 - 1, 0, E - 2)
                run("last", E // 2 - 1, 1, E - 1)

            def pairs(eng, run):
                run(0, 0, 0)
                run(0, 1, 1)
                with eng.Fori(0, (B - 2) // 2) as i:
                    run(i + 1, 0, i * 2 + 2)
                    run(i + 1, 1, i * 2 + 3)

            with nc.Block() as block:
                @block.sync
                def _(sp):
                    def load(e, p):
                        sp.dma_start(w1_f[p][:, :, :], w1[e].rearrange("(k p) n -> p k n", p=P)).then_inc(w1_in[p].sem, 16)
                        sp.dma_start(xg[p][:, 0:2, :], xs_d.rearrange("(e s) d -> e s d", e=E)[e, 0:2 * P].rearrange("(s p) d -> p s d", p=P)
                                     ).then_inc(xg_in[p].sem, 16)
                        sp.dma_start(xg[p][0:64, 2, :], xs_d.rearrange("(e s) d -> e s d", e=E)[e, 2 * P:CAP]).then_inc(xg_in[p].sem, 32)

                    def load2(e, p):
                        sp.dma_start(w2_f[p][:, :, :], w2[e].rearrange("(m p) n -> p m n", p=P)).then_inc(w2_in[p].sem, 16)

                    for e in range(2):
                        load(e, e)
                        load2(e, e)

                    def run(kind, j, p, e):
                        if kind in ("first", "mid"):
                            sp.wait_ge(xt_split.sem, xt_split.at(e, KD))
                            load(e + 2, p)
                            sp.wait_ge(w2_split.sem, w2_split.at(e, 4))
                            load2(e + 2, p)

                    expert_steps(sp, run)

                    def back(j, p, b):
                        if not (isinstance(b, int) and b < 2):
                            sp.wait_ge(out_ready.sem, out_ready.at(b - 2, 1))
                        sp.dma_start(x1b[p][:, :, :], x1_d[b].rearrange("t p d -> p t d")).then_inc(x1_back[p].sem, 16)
                        sp.dma_start(gb[p][:, :, :], mod_d[b, 3:4, :].unsqueeze(0).to_broadcast([P, 1, D])).then_inc(gb_in[p].sem, 16)

                    pairs(sp, back)

                @block.tensor
                def _(pe):
                    mm = nc.tensor.matmul

                    def transpose_rows(j, p, e):
                        pe.wait_ge(xg_in[p].sem, xg_in[p].at(j, 3))
                        if not (isinstance(e, int) and e == 0):
                            pe.wait_ge(xt_split.sem, xt_split.at(e - 1, KD))
                        for k in range(KD):
                            for i, (s0, n) in enumerate(ST):
                                last = mm(XT[k][:, s0:s0 + n], xg[p][0:n, i, k * P:(k + 1) * P], ident[0:n, 0:n],
                                          start=True, stop=True, is_transpose=True)
                        last.then_inc(xt_full.sem, 1)

                    def mm3(dst, terms):
                        for n, (l, r) in enumerate(terms):
                            last = mm(dst, l, r, start=(n == 0), stop=(n == len(terms) - 1))
                        return last

                    def rows_out(e, free_from, up_jobs):
                        pe.wait_ge(h_split.sem, h_split.at(free_from, up_jobs))
                        pe.wait_ge(yt_ready.sem, yt_ready.at(e, KD))
                        if not (isinstance(e, int) and e == 0):
                            pe.wait_ge(ys_ready.sem, ys_ready.at(e - 1, 2))
                        for k in range(KD):
                            for i in range(2):
                                mm(YT[:, i * D + k * P:i * D + (k + 1) * P], y_t[:, k, i * P:(i + 1) * P], ident[:, :],
                                   start=True, stop=True, is_transpose=True)
                            last = mm(LASTROWS[0:64, k * P:(k + 1) * P], y_t[:, k, 2 * P:CAP], ident[:, :], start=True, stop=True, is_transpose=True)
                        last.then_inc(ytr_full.sem, 1)

                    def run(kind, j, p, e):
                        pe.wait_ge(xt_split.sem, xt_split.at(e, KD))
                        for m in range(MH):
                            if m == 0:
                                pe.wait_ge(w1_split.sem, w1_split.at(e, KD))
                            if not (kind == "first" and m < NU):
                                pe.wait_ge(h_split.sem, h_split.at(e, m - NU + 1 if m >= NU else min(m - 1, 0)))
                            if m == 5 % NU and kind != "first" and not (isinstance(e, int) and e < 2):
                                pe.wait_ge(ys_ready.sem, ys_ready.at(e - 2, 2))
                            c = slice(m * P, (m + 1) * P)
                            terms = [(w[:, k, c], x_[:, k, :]) for k in range(KD) for w, x_ in ((w1_h, xt_h), (w1_l, xt_h), (w1_h, xt_l))]
                            mm3(UP[m % NU][:, 0:CAP], terms).then_inc(up_full.sem, 1)
                        if kind != "first":
                            rows_out(e - 1, e, 6)
                        if kind != "last":
                            transpose_rows(j + p, 1 - p, e + 1)
                        for k in range(KD):
                            if k == 0:
                                pe.wait_ge(w2_split.sem, w2_split.at(e, 4))
                                pe.wait_ge(h_split.sem, h_split.at(e, MH))
                            if kind != "first":
                                pe.wait_ge(yt_ready.sem, yt_ready.at(e - 1, k + 1))
                            c = slice(k * P, (k + 1) * P)
                            terms = [(w[:, m, c], h_[:, m, :]) for m in range(MH) for w, h_ in ((w2_h, h_h), (w2_l, h_h), (w2_h, h_l))]
                            mm3(YA[k][:, 0:CAP], terms).then_inc(down_full.sem, 1)

                    transpose_rows(0, 0, 0)
                    expert_steps(pe, run)
                    rows_out(E - 1, E - 1, MH)

                @block.scalar
                def _(act):
                    def split_rows(e):
                        act.wait_ge(xt_full.sem, xt_full.at(e, 1))
                        if not (isinstance(e, int) and e == 0):
                            act.wait_ge(up_full.sem, up_full.at(e - 1, MH))
                        for k in range(KD):
                            nc.scalar.activation(xt_h[:, k, :], XT[k][:, 0:CAP], ACT.Copy).then_inc(xth_ready.sem, 1)

                    def split_w1(j, p, e):
                        act.wait_ge(w1_in[p].sem, w1_in[p].at(j, 1))
                        if not (isinstance(e, int) and e == 0):
                            act.wait_ge(up_full.sem, up_full.at(e - 1, MH))
                        for k in range(KD):
                            nc.scalar.activation(w1_h[:, k, :], w1_f[p][:, k, :], ACT.Copy).then_inc(w1h_ready.sem, 1)

                    def rows_out(e):
                        act.wait_ge(ytr_full.sem, ytr_full.at(e, 1))
                        if not (isinstance(e, int) and e == 0):
                            act.wait_ge(ys_stored.sem, ys_stored.at(e - 1, 3))
                        nc.scalar.activation(y_s[:, 0:2, :], YT[:, :].rearrange("p (s d) -> p s d", s=2), ACT.Copy).then_inc(ys_ready.sem, 1)
                        nc.scalar.activation(y_s[0:64, 2, :], LASTROWS[0:64, 0:D], ACT.Copy).then_inc(ys_ready.sem, 1)
                        act.wait_ge(ys_ready.sem, ys_ready.at(e, 2))
                        ys = ys_d[0:SLOTS, :].rearrange("(e s) d -> e s d", e=E)
                        act.dma_start(ys[e, 0:2 * P].rearrange("(s p) d -> p s d", p=P), y_s[:, 0:2, :]).then_inc(ys_stored.sem, 16)
                        act.dma_start(ys[e, 2 * P:CAP], y_s[0:64, 2, :]).then_inc(ys_stored.sem, 32)

                    def run(kind, j, p, e):
                        act.wait_ge(w2_in[p].sem, w2_in[p].at(j, 1))
                        if kind != "first":
                            act.wait_ge(down_full.sem, down_full.at(e - 1, KD))
                        for m in range(MH):
                            act.wait_ge(up_full.sem, up_full.at(e, m + 1))
                            nc.scalar.activation(h_h[:, m, :], UP[m % NU][:, 0:CAP], ACT.Relu).then_inc(hh_ready.sem, 1)
                            if m % 2 == 1:
                                c = slice(m - 1, m + 1)
                                nc.scalar.activation(w2_h[:, c, :], w2_f[p][:, c, :], ACT.Copy).then_inc(w2h_ready.sem, 1)
                        if kind != "last":
                            split_w1(j + p, 1 - p, e + 1)
                        if kind != "first":
                            rows_out(e - 1)
                        if kind != "last":
                            split_rows(e + 1)
                        for k in range(KD):
                            act.wait_ge(down_full.sem, down_full.at(e, k + 1))
                            nc.scalar.activation(y_t[:, k, :], YA[k][:, 0:CAP], ACT.Copy).then_inc(yt_ready.sem, 1)

                    split_w1(0, 0, 0)
                    split_rows(0)
                    expert_steps(act, run)
                    rows_out(E - 1)

                    def store(j, p, b):
                        act.wait_ge(out_ready.sem, out_ready.at(b, 1))
                        act.dma_start(out.rearrange("b (t p) d -> b p t d", p=P)[b], yg[p][:, :, :]).then_inc(out_stored[p].sem, 16)

                    pairs(act, store)
                    for i in range(2):
                        act.wait_ge(out_stored[i].sem, out_stored[i].at(B // 2 - 1, 1))

                @block.vector
                def _(dve):
                    v = nc.vector

                    def split_w1(j, p, e):
                        for k in range(KD):
                            dve.wait_ge(w1h_ready.sem, w1h_ready.at(e, k + 1))
                            v.tensor_tensor(w1_l[:, k, :], w1_f[p][:, k, :], w1_h[:, k, :].bitcast(F32), ALU.subtract).then_inc(w1_split.sem, 1)

                    def split_rows(e):
                        for k in range(KD):
                            dve.wait_ge(xth_ready.sem, xth_ready.at(e, k + 1))
                            v.tensor_tensor(xt_l[:, k, :], XT[k][:, 0:CAP], xt_h[:, k, :].bitcast(F32), ALU.subtract).then_inc(xt_split.sem, 1)

                    def run(kind, j, p, e):
                        for m in range(MH):
                            dve.wait_ge(hh_ready.sem, hh_ready.at(e, m + 1))
                            v.scalar_tensor_tensor(h_l[:, m, :], UP[m % NU][:, 0:CAP], 0.0, h_h[:, m, :].bitcast(F32), ALU.max,
                                                   ALU.subtract).then_inc(h_split.sem, 1)
                            if m % 2 == 1:
                                c = slice(m - 1, m + 1)
                                dve.wait_ge(w2h_ready.sem, w2h_ready.at(e, m // 2 + 1))
                                v.tensor_tensor(w2_l[:, c, :], w2_f[p][:, c, :], w2_h[:, c, :].bitcast(F32), ALU.subtract).then_inc(w2_split.sem, 1)
                        if kind != "last":
                            split_w1(j + p, 1 - p, e + 1)
                            split_rows(e + 1)

                    split_w1(0, 0, 0)
                    split_rows(0)
                    expert_steps(dve, run)

                    prob_b = [fb(f"prob_b{i}", [P, NT]) for i in range(2)]

                    def combine(j, p, b):
                        v.tensor_copy(prob_b[p][:, :], prob_all[:, bass.ds(b * NT, NT)]).then_inc(comb.sem, NT)
                        dve.wait_ge(comb.sem, comb.at(b, NT))
                        dve.wait_ge(x1_back[p].sem, x1_back[p].at(j, 1))
                        dve.wait_ge(gb_in[p].sem, gb_in[p].at(j, 1))
                        dve.wait_ge(gathered[p].sem, gathered[p].at(j, NT))
                        for t in range(NT):
                            v.scalar_tensor_tensor(yg[p][:, t, :], yg[p][:, t, :], prob_b[p][:, t:t + 1], gb[p][:, 0, :], ALU.mult,
                                                   ALU.mult).then_inc(comb.sem, 1)
                        dve.wait_ge(comb.sem, comb.at(b, 2 * NT))
                        v.tensor_tensor(yg[p][:, :, :], yg[p][:, :, :], x1b[p][:, :, :], ALU.add).then_inc(out_ready.sem, 1)

                    pairs(dve, combine)

                @block.gpsimd
                def _(pool):
                    slot_b = [fb(f"slot_b{i}", [P, NT], I32) for i in range(2)]
                    pool.wait_ge(ys_stored.sem, ys_stored.at(E - 1, 3))
                    turn2 = fb("turn2", [1, 1])

                    def gather(j, p, b):
                        if not (isinstance(b, int) and b < 2):
                            pool.wait_ge(out_stored[p].sem, out_stored[p].at(j - 1, 1))
                        nc.gpsimd.tensor_copy(slot_b[p][:, :], slot_all[:, bass.ds(b * NT, NT)]).then_inc(sem("slot_copied"), 1)
                        pool.wait_ge(sem("slot_copied"), b + 1)
                        nc.gpsimd.tensor_tensor(turn2[:, :], blank_row[:, :], blank_row[:, :], ALU.add)
                        for t in range(NT):
                            nc.gpsimd.indirect_dma_start(yg[p][:, t, :], None, ys_d, bass.IndirectOffsetOnAxis(slot_b[p][:, t:t + 1], 0),
                                                         bounds_check=SLOTS, oob_is_err=False).then_inc(gathered[p].sem, 16)

                    pairs(pool, gather)


_INS = ["L0_attn_x", "L0_attn_wq", "L0_attn_wk", "L0_attn_wv", "L0_attn_wgq", "L0_attn_wgk", "L0_attn_wgv", "L0_attn_r_out_w",
        "L0_attn_gate_local_w", "L0_attn_gate_remote_w", "L0_attn_w_out", "L0_ffn_gate_w", "L0_ffn_w1", "L0_ffn_w2", "L0_c", "L0_wmod"]


def kernel(**inputs):
    import numpy as np
    import concourse.bacc as bacc
    from concourse.bass_utils import run_bass_kernel_spmd

    nc = bacc.Bacc("TRN2", target_bir_lowering=False, num_devices=1)
    arrays, args = {}, []
    for name in _INS:
        a = np.ascontiguousarray(inputs[name])
        arrays[f"in_{name}"] = a
        args.append(nc.dram_tensor(f"in_{name}", a.shape, mybir.dt.from_np(a.dtype), kind="ExternalInput").ap())
    args.append(nc.dram_tensor("out_rows", (B, S, D), F32, kind="ExternalOutput").ap())
    adaln_moe_kernel(nc, *args)
    r = run_bass_kernel_spmd(nc, [arrays], core_ids=[0])
    return r.results[0]["out_rows"]
```

```python
from contextlib import ExitStack

import concourse.bass as bass
from concourse import mybir

ALU = mybir.AluOpType
ACT = mybir.ActivationFunctionType
F32 = mybir.dt.float32
F32R = mybir.dt.float32r
BF16 = mybir.dt.bfloat16
I32 = mybir.dt.int32
AX_X = mybir.AxisListType.X

P = 128
B, S, D = 8, 512, 256
KD = D // P
NT = S // P
H, HD = 16, 16
W = 64
NB = S // W
LH, LD, NL = 8, 128, 64
CH = S // NL
NP = LH // 2
E, HID = 16, 1024
T = B * S
CAP = int(1.25 * T / E)
SLOTS = E * CAP
ROW_X, ROW_P, ROW_T, ROW_G, ROW = D, 2 * D, 2 * D + 1, 2 * D + 2, 2 * D + 3
MH = HID // P
ST = [(0, 128), (128, 128), (256, CAP - 256)]
EPS = 1e-5
BIG = -1.0e30
QPART = [0, 0, 0, 1, 1, 2]
KPART = [0, 1, 2, 0, 1, 0]
KS_ROWS = 16 * len(QPART)
VW = HD + 1
HH = H // 2
SB = 3

SLOT_JOBS = {
    0: ["A.T0", "A.T1"],
    1: ["D.OT0", "D.OT1"],
    2: ["A.Q0", "A.Q1"],
    3: ["A.K0", "A.K1"],
    4: ["D.WO0", "D.WO1", "A.GQ"],
    5: ["A.V0"],
    6: ["L.LT0", "A.V1"],
    7: ["A.V2", "A.V3"],
    8: ["A.GK", "A.GV", "C.R0"],
    9: ["C.R1", "D.H0", "D.H1"],
    10: ["L.LT1", "C.R2"],
    11: ["C.R3", "D.LG"],
    12: ["C.PR0", "C.PR1"],
    13: ["C.PR2", "D.LOC"],
    14: ["L.LT2", "C.PR3"],
    15: ["C.RP"],
    16: ["C.RO0", "C.RO1", "L.LT3"],
}
S1_NEXT = {9: [0], 10: [1], 11: [2], 12: [3], 13: [4, 5], 14: [6, 7], 15: [8], 16: ["M0", 9]}
S1_NOW = {0: [10], 1: [11], 2: [12], 3: [13], 4: [14], 5: [15], 7: ["M1"]}
S1_ORDER = [j for s in range(17) for j in S1_NEXT.get(s, [])] + [j for s in range(17) for j in S1_NOW.get(s, [])]
S1_PARTS = {15: 0, 6: 1}
R_SUMS = {9: [0], 10: [1], 11: [2], 12: [3]}
ALL_JOBS = [j for s in range(17) for j in SLOT_JOBS[s]]
PRO = [j for j in ALL_JOBS if j[0] == "A"]
FIRST = [j for j in ALL_JOBS if j[0] != "D"]
LAST = [j for j in ALL_JOBS if j[0] != "A"]
EPI = [j for j in ALL_JOBS if j[0] == "D"]
ORDER = {"pro": PRO, "first": FIRST, "mid": ALL_JOBS, "last": LAST, "epi": EPI}
BEFORE = {"pro": [], "first": PRO, "mid": ALL_JOBS, "last": ALL_JOBS, "epi": LAST}
START = {"pro": 0, "first": len(PRO), "mid": len(PRO) + len(FIRST)}
START["last"] = START["mid"] + (B - 2) * len(ALL_JOBS)
START["epi"] = START["last"] + len(LAST)


def batch_of(name, step):
    return {"A": step + 1, "C": step, "L": step, "D": step - 1}[name[0]]


class Job:

    def __init__(self, kind, step, name):
        at = ORDER[kind].index(name)
        turns = (step - 1) if kind == "mid" else 0
        self.bank = (START[kind] + at) % SB
        self.done = START[kind] + at + 1 + len(ALL_JOBS) * turns
        if at >= SB:
            prev = ORDER[kind][at - SB]
            self.before = (prev, batch_of(prev, step))
        elif BEFORE[kind]:
            prev = BEFORE[kind][at - SB]
            self.before = (prev, batch_of(prev, step - 1))
        else:
            self.before = None


class Signal:

    def __init__(self, sem, per, by=1):
        self.sem, self.per, self.by = sem, per, by

    def at(self, b, k):
        return b * (self.per * self.by) + k * self.by


def bc(ap, shape):
    return ap.to_broadcast(shape)


def adaln_moe_kernel(nc, x, wq, wk, wv, wgq, wgk, wgv, r_out, gl_w, gr_w, w_out, gate_w, w1, w2, c_in, wmod, out):
    top = ExitStack()
    sems = {}

    def sem(name):
        if name not in sems:
            sems[name] = top.enter_context(nc.semaphore(name))
        return sems[name]

    def alloc(ctx, name, shape, dt):
        return ctx.enter_context(nc.sbuf_tensor(name, shape, dt))

    with top:
        qk_d = nc.dram_tensor("qk_parts", [2, 2, 3, D, S], BF16).ap()
        mod_d = nc.dram_tensor("mod_rows", [B, 4, D], F32).ap()
        xs_d = nc.dram_tensor("expert_in", [SLOTS, ROW], F32).ap()

        ident = alloc(top, "ident", [P, P], F32)
        blank_row = alloc(top, "blank_row", [1, 1], F32)
        ps = [top.enter_context(nc.psum_tensor(f"bank{i}", [P, 512], F32)) for i in range(8)]

        att = ExitStack()
        with att:
            def sb(name, shape, dt=F32):
                return alloc(att, name, shape, dt)

            ident_b = sb("ident_b", [P, P], BF16)
            mask_q = sb("mask_q", [P, NT, P], BF16)
            mask_k = sb("mask_k", [P, NB, W], BF16)
            mask_r = sb("mask_r", [P, NT, LH, NL], BF16)
            pick = sb("pick", [P, HH, P], BF16)
            tri = sb("tri", [P, P], BF16)
            ones_b = sb("ones_b", [P, P], BF16)
            head_rows = sb("head_rows", [P, LH])
            pair_rows = sb("pair_rows", [P, NP, 2, HD])
            iota_f = sb("iota_f", [P, E])
            token_i = sb("token_i", [P, NT], I32)
            zero = sb("zero", [P, ROW])
            slots_zeroed = sem("slots_zeroed")
            N_ZERO, ZERO_ROWS = 10, SLOTS // P // 10
            wq_h, wq_l = sb("wq_h", [P, KD, D], F32R), sb("wq_l", [P, KD, D], F32R)
            wk_h, wk_l = sb("wk_h", [P, KD, D], F32R), sb("wk_l", [P, KD, D], F32R)
            wg_h, wg_l = sb("wg_h", [P, KD, LD], F32R), sb("wg_l", [P, KD, LD], F32R)
            VG = D + 2 * H
            wv_h, wv_l = sb("wv_h", [P, KD, VG], F32R), sb("wv_l", [P, KD, VG], F32R)
            wgk_s, wgv_s = sb("wgk_s", [P, KD, LD]), sb("wgv_s", [P, KD, LD])
            rout_s, wout_s = sb("rout_s", [P, D]), sb("wout_s", [P, KD, D])
            gate_t = sb("gate_t", [P, KD, E])
            mod_t = sb("mod_t", [P, B, 2, KD])

            setup = ExitStack()
            with setup:
                def st(name, shape, dt=F32):
                    return alloc(setup, name, shape, dt)

                wq_f, wk_f, wg_f = st("wq_f", [P, KD, D]), st("wk_f", [P, KD, D]), st("wg_f", [P, KD, LD])
                wv_f = st("wv_f", [P, KD, VG])
                gates_f = st("gates_f", [P, 2, D])
                gate_tmp = st("gate_tmp", [P, 2, KD, D])
                wmod_f = st("wmod_f", [P, KD, 6 * D])
                c_t, c_e = st("c_t", [P, KD, B]), st("c_e", [P, KD, B])
                mod_r = st("mod_r", [B, 6, D])
                mod_o = st("mod_o", [B, 4, D])
                mod_s = st("mod_s", [B, 2, D])
                iota_i = st("iota_i", [P, E], I32)
                gate_r = st("gate_r", [E, D])
                w_in, c_inn, const_in = sem("weights_in"), sem("cond_in"), sem("setup_consts")
                with nc.Block() as block:
                    @block.sync
                    def _(sp):
                        with nc.allow_non_contiguous_dma("condition, transposed"):
                            for k in range(KD):
                                sp.dma_start(c_t[:, k, :], c_in.rearrange("b (k p) -> k p b", p=P)[k]).then_inc(c_inn, 16)
                        sp.dma_start(wmod_f[:, :, :], wmod.rearrange("(k p) n -> p k n", p=P)).then_inc(c_inn, 16)
                        for dst, src in ((wq_f, wq), (wk_f, wk), (wg_f, wgq), (wgk_s, wgk), (wgv_s, wgv), (wout_s, w_out)):
                            sp.dma_start(dst[:, :, :], src.rearrange("(k p) n -> p k n", p=P)).then_inc(w_in, 16)
                        sp.dma_start(wv_f[:, :, 0:D], wv.rearrange("(k p) n -> p k n", p=P)).then_inc(w_in, 16)
                        sp.dma_start(rout_s[:, :], r_out).then_inc(w_in, 16)
                        for i, g in enumerate((gl_w, gr_w)):
                            sp.dma_start(gates_f[:, i, :], g.rearrange("h d -> (h d)")[None, :].to_broadcast([P, D])).then_inc(w_in, 16)
                        sp.dma_start(gate_r[:, :], gate_w).then_inc(w_in, 16)
                        sp.wait_ge(sem("mod_rows_ready"), 5)
                        sp.dma_start(mod_d, mod_o[:, :, :]).then_inc(sem("mod_stored"), 16)
                        sp.wait_ge(sem("mod_stored"), 16)

                        sp.wait_ge(sem("zero_set"), 1)
                        for i in range(N_ZERO):
                            sp.dma_start(xs_d[i * ZERO_ROWS * P:(i + 1) * ZERO_ROWS * P, :].rearrange("(p r) d -> p r d", p=P),
                                         zero[:, :].unsqueeze(1).to_broadcast([P, ZERO_ROWS, ROW])).then_inc(slots_zeroed, 16)

                    @block.gpsimd
                    def _(pool):
                        blank = sem("blank")
                        nc.gpsimd.memset(zero[:, :], 0.0).then_inc(sem("zero_set"), 1)
                        for t_, v in ((ident, 0.0), (ident_b, 0.0), (mask_q, 0.0), (mask_k, 0.0), (mask_r, 0.0), (pick, 0.0),
                                      (tri, 1.0), (blank_row, 0.0), (ones_b, 1.0), (head_rows, 1.0), (pair_rows, 1.0)):
                            nc.gpsimd.memset(t_.ap(), v).then_inc(blank, 1)
                        pool.wait_ge(blank, 11)
                        n = [11]

                        def select(ap, cond, fill, base, pattern, mult):
                            nc.gpsimd.affine_select(out=ap, in_=ap, compare_op=cond, fill=fill, base=base,
                                                    pattern=pattern, channel_multiplier=mult).then_inc(blank, 1)
                            n[0] += 1
                            pool.wait_ge(blank, n[0])

                        select(ident[:, :], ALU.not_equal, 1.0, 0, [[-1, P]], 1)
                        select(ident_b[:, :], ALU.not_equal, 1.0, 0, [[-1, P]], 1)
                        for half in range(2):
                            m = mask_q[64 * half:64 * half + 64, :, :]
                            select(m, ALU.is_gt, BIG, 0, [[0, NT], [1, P]], -1)
                            select(m, ALU.is_ge, BIG, W, [[0, NT], [-1, P]], 1)
                        select(mask_q[0:64, 0, 0:W], ALU.is_gt, BIG, -1, [[0, W]], 0)
                        select(mask_k[:, :, :], ALU.is_gt, BIG, 0, [[0, NB], [-1, W]], 1)
                        select(mask_k[:, :, :], ALU.is_ge, BIG, W, [[0, NB], [1, W]], -1)
                        select(mask_k[0:64, 0, :], ALU.is_gt, BIG, -1, [[0, W]], 0)
                        select(mask_r[:, :, :, :], ALU.is_ge, BIG, 0, [[P, NT], [0, LH], [-CH, NL]], 1)
                        for j in range(3):
                            select(pick[:, :, :], ALU.not_equal, 1.0, -HH * j, [[-1, HH], [0, P]], 1)
                        select(tri[:, :], ALU.is_ge, 0.0, 0, [[1, P]], -1)
                        select(head_rows[:, :], ALU.is_ge, 0.0, 0, [[-HD, LH]], 1)
                        select(head_rows[:, :], ALU.is_ge, 0.0, HD - 1, [[HD, LH]], -1)
                        select(pair_rows[:, :, 0, :], ALU.is_ge, 0.0, NL - 1, [[0, NP], [0, HD]], -1)
                        select(pair_rows[:, :, 1, :], ALU.is_ge, 0.0, -NL, [[0, NP], [0, HD]], 1)
                        nc.gpsimd.iota(iota_i[:, :], pattern=[[1, E]], base=0, channel_multiplier=0).then_inc(const_in, 1)
                        nc.gpsimd.iota(token_i[:, :], pattern=[[P, NT]], base=-T - S, channel_multiplier=1).then_inc(const_in, 1)

                    @block.scalar
                    def _(act):
                        act.wait_ge(c_inn, 48)
                        nc.scalar.activation(c_e[:, :, :], c_t[:, :, :], ACT.Exp, scale=-1.0).then_inc(sem("cond_exp"), 1)

                    @block.tensor
                    def _(pe):
                        pe.wait_ge(sem("silu_ready"), 1)
                        for half in range(KD):
                            for kind in range(2):
                                o = (half * 2 + kind) * B
                                for k in range(KD):
                                    last = nc.tensor.matmul(
                                        ps[0][:, o:o + B], wmod_f[:, k, kind * D + half * P:kind * D + half * P + P],
                                        c_t[:, k, :], start=(k == 0), stop=(k == KD - 1))
                        last.then_inc(sem("mod_matmul"), 1)
                        for n in range(3):
                            for k in range(KD):
                                last = nc.tensor.matmul(ps[1 + n][0:B, :], c_t[:, k, :], wmod_f[:, k, n * 512:n * 512 + 512],
                                                        start=(k == 0), stop=(k == KD - 1))
                        last.then_inc(sem("mod_matmul"), 1)
                        pe.wait_ge(w_in, 16 * 11)
                        pe.wait_ge(sem("blank"), 12)
                        for k in range(KD):
                            last = nc.tensor.matmul(ps[4][:, k * E:(k + 1) * E], gate_r[:, k * P:(k + 1) * P],
                                                    ident[0:E, 0:E], start=True, stop=True, is_transpose=True)
                        last.then_inc(sem("mod_matmul"), 1)

                    @block.vector
                    def _(dve):
                        step = sem("setup_vector")
                        n = [0]

                        def then(ins):
                            ins.then_inc(step, 1)
                            n[0] += 1
                            dve.wait_ge(step, n[0])

                        dve.wait_ge(sem("cond_exp"), 1)
                        then(nc.vector.tensor_scalar(c_e[:, :, :], c_e[:, :, :], 1.0, None, ALU.add))
                        then(nc.vector.reciprocal(c_e[:, :, :], c_e[:, :, :]))
                        nc.vector.tensor_tensor(c_t[:, :, :], c_t[:, :, :], c_e[:, :, :], ALU.mult).then_inc(sem("silu_ready"), 1)
                        dve.wait_ge(w_in, 16 * 11)
                        for i in range(2):
                            for k in range(KD):
                                then(nc.vector.tensor_tensor(gate_tmp[:, i, k, :], wq_f[:, k, :], gates_f[:, i, :], ALU.mult))
                        for i in range(2):
                            then(nc.vector.tensor_reduce(wv_f[:, :, D + i * H:D + (i + 1) * H],
                                                         gate_tmp[:, i, :, :].rearrange("p k (h d) -> p k h d", d=HD), AX_X, ALU.add))
                        for f, hi, lo in ((wq_f, wq_h, wq_l), (wk_f, wk_h, wk_l), (wg_f, wg_h, wg_l), (wv_f, wv_h, wv_l)):
                            then(nc.vector.tensor_copy(hi[:, :, :], f[:, :, :]))
                            then(nc.vector.tensor_tensor(lo[:, :, :], f[:, :, :], hi[:, :, :].bitcast(F32), ALU.subtract))
                        dve.wait_ge(sem("mod_matmul"), 1)
                        nc.vector.tensor_copy(mod_t[:, :, 0, :], ps[0][:, 0:4 * B].rearrange("p (h k b) -> p k b h", k=2, b=B)[:, 0])
                        then(nc.vector.tensor_scalar(mod_t[:, :, 1, :], ps[0][:, 0:4 * B].rearrange("p (h k b) -> p k b h", k=2, b=B)[:, 1],
                                                     1.0, None, ALU.add))
                        dve.wait_ge(sem("mod_matmul"), 2)
                        for i in range(3):
                            then(nc.vector.tensor_copy(mod_r[:, 2 * i:2 * i + 2, :], ps[1 + i][0:B, :].rearrange("b (a d) -> b a d", a=2)))
                        rows = sem("mod_rows_ready")
                        for i, (src, dst) in enumerate(((2, 0), (5, 3))):
                            then(nc.vector.tensor_scalar(mod_s[:, i, :], mod_r[:, src, :], 0.0, 2.0, ALU.is_ge, ALU.mult))
                            then(nc.vector.tensor_scalar(mod_s[:, i, :], mod_s[:, i, :], 1.0, None, ALU.subtract))
                            then(nc.vector.tensor_tensor(mod_o[:, dst, :], mod_r[:, src, :], mod_s[:, i, :], ALU.mult))
                            then(nc.vector.tensor_scalar(mod_o[:, dst, :], mod_o[:, dst, :], 0.25, None, ALU.max))
                            nc.vector.tensor_tensor(mod_o[:, dst, :], mod_o[:, dst, :], mod_s[:, i, :], ALU.mult).then_inc(rows, 1)
                        nc.vector.tensor_scalar(mod_o[:, 1, :], mod_r[:, 4, :], 1.0, None, ALU.add).then_inc(rows, 1)
                        nc.vector.tensor_copy(mod_o[:, 2, :], mod_r[:, 3, :]).then_inc(rows, 1)
                        dve.wait_ge(const_in, 2)
                        nc.vector.tensor_copy(iota_f[:, :], iota_i[:, :]).then_inc(rows, 1)
                        dve.wait_ge(sem("mod_matmul"), 3)
                        then(nc.vector.tensor_copy(gate_t[:, :, :], ps[4][:, 0:KD * E].rearrange("p (k e) -> p k e", k=KD)))

            q_st = [sb(f"q_stack{i}", [KS_ROWS, H, S], BF16) for i in range(2)]
            k_st = [sb(f"k_stack{i}", [KS_ROWS, H, W + S], BF16) for i in range(2)]
            v_al = [sb(f"v_aligned{i}", [P, NT, H, VW]) for i in range(2)]
            v_sh = [sb(f"v_shifted{i}", [P, NT, H, VW]) for i in range(2)]
            xin = sb("xin", [P, NT, D])
            hT = sb("hT", [P, KD, S])
            hT_h, hT_l = sb("hT_h", [P, KD, S], F32R), sb("hT_l", [P, KD, S], F32R)
            hbar = sb("hbar", [P, KD, 2, NL])
            mod_b = sb("mod_b", [P, 2, KD])
            parts = [sb(f"parts{i}", [P, 3, S], BF16) for i in range(2)]
            rest = [sb(f"rest{i}", [P, S]) for i in range(2)]
            gates = [sb(f"gates{i}", [P, NT, 2 * H]) for i in range(2)]
            gq_t = [sb(f"gq_t{i}", [P, S]) for i in range(2)]
            gk_bd = [sb(f"gk_bd{i}", [P, LH, NL]) for i in range(2)]
            gv_bd = [sb(f"gv_bd{i}", [P, NP, 2, HD]) for i in range(2)]
            nmx = sb("nmx", [P, NT, H])
            nmx_r = sb("nmx_r", [P, NT, HH])
            mx_p = [sb(f"mx_parts{i}", [P, NT, P], BF16) for i in range(2)]
            mx_t = [sb(f"mx_t{i}", [P, S], BF16) for i in range(2)]
            NPT = 3
            p_t = [sb(f"p_t{i}", [P, S]) for i in range(NPT)]
            pv_s = sb("pv_s", [P, S])
            o = sb("o", [P, NT, D])
            fac = sb("fac", [P, 2, NT, 4])
            sr = sb("sr", [P, NT, LH, NL])
            rm = sr[:, 0:2, :, :].rearrange("p t h n -> p (t h n)").rearrange("p (t d) -> p t d", d=D)
            rstat = sb("rstat", [P, 3, NT, LH])
            pr_t = sb("pr_t", [P, NP, S])
            rem_t = sb("rem_t", [P, S])
            d_t = sb("d_t", [P, KD, S])
            rows = sb("rows", [P, NT, ROW])
            h2, x1 = rows[:, :, 0:D], rows[:, :, ROW_X:ROW_X + D]
            mod_bc = sb("mod_bc", [P, 3, D])
            ln_raw = sb("ln_raw", [P, NT, 6])
            ln_mv = sb("ln_mv", [P, NT, 2])
            ln_ve = sb("ln_ve", [P, NT])
            ln_rs = sb("ln_rs", [P, NT])
            neg_half = sb("neg_half", [P, NT])
            turn = sb("turn", [1, 1])
            lg = sb("lg", [P, NT, E])
            lge = sb("lge", [P, NT, E])
            cand = sb("cand", [P, NT, E])
            loc_e = sb("loc_e", [P, NT, E])
            rt = sb("rt", [P, 8, NT])
            oh = sb("oh", [P, NT, E], BF16)
            seen = sb("seen", [P, NT + 1, E], BF16)
            slot_i = [sb(f"slot_i{i}", [P, NT], I32) for i in range(2)]

            S1 = [ps[0], ps[1]]
            S2 = [ps[2], ps[3]]
            PV = ps[4]
            RING = [ps[5], ps[6], ps[7]]

            def sig(name, per, by=1):
                return Signal(sem(name), per, by)

            x_in = sig("x_in", 1, 16)
            ln1_ready = sig("ln1_ready", NT)
            modb_ready = sig("modb_ready", 1)
            hT_ready = sig("hT_ready", KD)
            hTh_ready = sig("hTh_ready", KD)
            hTl_ready = sig("hTl_ready", KD)
            hbar_ready = sig("hbar_ready", KD)
            p1_ready, p2_ready, p3_ready = sig("part1_ready", 4), sig("part2_ready", 4), sig("part3_ready", 4)
            rest_ready = sig("rest_ready", 4)
            parts_stored = [sig(f"parts_stored{i}", 2, 16) for i in range(2)]
            stack_in = sig("stack_in", 12, 16)
            gq_ready, gk_ready = sig("gq_ready", 1), sig("gk_ready", 2)
            v_ready, v_shifted = sig("v_ready", NT), sig("v_shifted", 2, 16)
            gexp_ready = sig("gate_exp_ready", NT)
            gate_ready = sig("gate_ready", 1)
            s1_full, s1_free = sig("s1_full", 18), sig("s1_free", 18)
            mxp_ready = sig("max_parts_ready", 2)
            s2_full, exp_ready, pv_done = sig("s2_full", H), sig("exp_ready", H), sig("pv_done", H)
            pv_out = sig("pv_out", 4)
            lt_done = sig("local_done", 4)
            ring_full = sem("ring_full")
            rshift_ready, rexp_ready, rinv_ready = sig("r_shift_ready", NT), sig("r_exp_ready", NT), sig("r_inv_ready", NT)
            rprob_ready, prt_ready = sig("r_prob_ready", NT), sig("prt_ready", NT)
            remt_ready, rm_ready = sig("rem_t_ready", 1), sig("rm_ready", 2)
            o_ready, ot_ready = sig("o_ready", 2), sig("o_t_ready", 2)
            ao_ready, x1_ready, x1_stored = sig("attn_out_ready", 2), sig("x1_ready", 2), sig("x1_stored", 1, 16)
            xres_in, modbc_in = sig("x_again_in", 1, 16), sig("mod_bc_in", 1, 16)
            h2n_ready, h2_ready, h2t_ready = sig("h2_norm_ready", 2), sig("h2_ready", 2), sig("h2_t_ready", 2)
            lg_ready, lge_ready, oh_ready, slot_ready = sig("lg_ready", 1), sig("lg_exp_ready", 1), sig("onehot_ready", 1), sig("slot_ready", 1)
            scattered = sig("scattered", NT, 16)
            loc_ready = sig("loc_ready", 1)
            var1_ready, rstd1_ready = sig("var1_ready", 1), sig("rstd1_ready", 1)
            var2_ready, rstd2_ready = sig("var2_ready", 1), sig("rstd2_ready", 1)
            blanks, N_BLANKS = sem("buffers_blanked"), 11
            ln1_chain, hbar_chain = sig("ln1_chain", 2 * NT + 1), sig("hbar_chain", KD)
            gate_chain, mx_chain = sig("gate_chain", 1), sig("max_chain", 8)
            r_chain, lt_chain = sig("r_chain", 2 * NT), sig("lt_chain", 8)
            rmax_chain = sig("r_max_chain", NT)
            ln2_chain, route_chain = sig("ln2_chain", 2 * NT + 1), sig("route_chain", 13)
            add_chain = sig("modulate_chain", 2)
            read_by = {"A.GQ": (gq_ready, 1), "A.GK": (gk_ready, 1), "A.GV": (gk_ready, 2), "C.RP": (remt_ready, 1),
                       "D.LG": (lg_ready, 1), "D.LOC": (loc_ready, 1)}
            for i in range(2):
                read_by.update({f"A.T{i}": (hT_ready, i + 1), f"A.Q{i}": (rest_ready, i + 1), f"A.K{i}": (rest_ready, i + 3),
                                f"C.RO{i}": (rm_ready, i + 1), f"D.OT{i}": (ot_ready, i + 1), f"D.WO{i}": (ao_ready, i + 1),
                                f"D.H{i}": (h2t_ready, i + 1)})
            for i in range(4):
                read_by.update({f"A.V{i}": (gexp_ready, i + 1), f"C.R{i}": (rshift_ready, i + 1),
                                f"C.PR{i}": (prt_ready, i + 1), f"L.LT{i}": (lt_done, i + 1)})

            def steps(run):
                run("pro", -1, 1)
                run("first", 0, 0)
                run("mid", 1, 1)
                with run.engine.Fori(0, (B - 4) // 2) as i:
                    run("mid", i * 2 + 2, 0)
                    run("mid", i * 2 + 3, 1)
                run("mid", B - 2, 0)
                run("last", B - 1, 1)
                run("epi", B, 0)

            class Run:

                def __init__(self, engine, jobs, head=None):
                    self.engine, self.jobs, self.head = engine, jobs, head

                def __call__(self, kind, s, c):
                    for slot in range(17):
                        if self.head is not None:
                            self.head(kind, s, c, slot)
                        for name in SLOT_JOBS[slot]:
                            if name not in ORDER[kind]:
                                continue
                            stage, what = name.split(".")
                            b, p = batch_of(name, s), c if stage in "CL" else 1 - c
                            fn = self.jobs.get(what.rstrip("0123456789"))
                            if fn is not None:
                                fn(Job(kind, s, name), b, p, int(what[-1]) if what[-1].isdigit() else 0)

            def is0(b):
                return isinstance(b, int) and b == 0

            def norm_batch(kind, s, slot, at):
                if kind == "pro" and slot == 0:
                    return 0
                if slot == at and kind in ("pro", "first", "mid") and not (isinstance(s, int) and s + 2 >= B):
                    return s + 2
                return None

            with nc.Block() as block:

                @block.tensor
                def _(pe):
                    mm = nc.tensor.matmul

                    def bank(job):
                        if job.before is not None:
                            name, b = job.before
                            last_read, k = read_by[name]
                            pe.wait_ge(last_read.sem, last_read.at(b, k))
                        return RING[job.bank]

                    def tr(dst, src, idn):
                        return mm(dst, src, idn, start=True, stop=True, is_transpose=True)

                    def mm3(dst, a, b_):
                        terms = [(a[i][k], b_[j][k]) for k in range(KD) for i, j in ((0, 0), (1, 0), (0, 1))]
                        for n, (l, r) in enumerate(terms):
                            last = mm(dst, l, r, start=(n == 0), stop=(n == len(terms) - 1))
                        return last

                    def job_T(job, b, p, k):
                        r = bank(job)
                        pe.wait_ge(ln1_ready.sem, ln1_ready.at(b, NT))
                        for t in range(NT):
                            last = tr(r[:, t * P:(t + 1) * P], xin[:, t, k * P:(k + 1) * P], ident[:, :])
                        last.then_inc(ring_full, 1)

                    def halves(hi, lo, c0, n):
                        return [[w[:, k, c0:c0 + n] for k in range(KD)] for w in (hi, lo)]

                    def proj(job, b, hi, lo, c0):
                        r = bank(job)
                        pe.wait_ge(hTl_ready.sem, hTl_ready.at(b, KD))
                        mm3(r[:, :], halves(hi, lo, c0, P), halves(hT_h, hT_l, 0, S)).then_inc(ring_full, 1)

                    def job_Q(job, b, p, m):
                        proj(job, b, wq_h, wq_l, m * P)

                    def job_K(job, b, p, m):
                        proj(job, b, wk_h, wk_l, m * P)

                    def job_GQ(job, b, p, m):
                        proj(job, b, wg_h, wg_l, 0)

                    def job_V(job, b, p, t):
                        r = bank(job)
                        mm3(r[:, 0:VG], halves(hT_h, hT_l, t * P, P), halves(wv_h, wv_l, 0, VG)).then_inc(ring_full, 1)

                    def job_GK(job, b, p, m):
                        r = bank(job)
                        pe.wait_ge(hbar_ready.sem, hbar_ready.at(b, KD))
                        for k in range(KD):
                            last = mm(r[:, 0:NL], wgk_s[:, k, :], hbar[:, k, 0, :], start=(k == 0), stop=(k == KD - 1))
                        last.then_inc(ring_full, 1)

                    def job_GV(job, b, p, m):
                        r = bank(job)
                        for k in range(KD):
                            last = mm(r[:, 0:LD], hbar[:, k, :, :], wgv_s[:, k, :], start=(k == 0), stop=(k == KD - 1))
                        last.then_inc(ring_full, 1)

                    def job_R(job, b, p, t):
                        r = bank(job)
                        pe.wait_ge(gq_ready.sem, gq_ready.at(b, 1))
                        pe.wait_ge(gk_ready.sem, gk_ready.at(b, 2))
                        mm(r[:, :], ident_b[:, :], mask_r[:, t, :, :], start=True, stop=False)
                        mm(r[:, :], gq_t[p][:, t * P:(t + 1) * P], gk_bd[p][:, :, :], start=False, stop=True).then_inc(ring_full, 1)

                    def job_PR(job, b, p, t):
                        r = bank(job)
                        pe.wait_ge(rprob_ready.sem, rprob_ready.at(b, t + 1))
                        for q in range(NP):
                            last = tr(r[:, q * P:(q + 1) * P], sr[:, t, 2 * q:2 * q + 2, :], ident[:, :])
                        last.then_inc(ring_full, 1)

                    def job_RP(job, b, p, m):
                        r = bank(job)
                        pe.wait_ge(prt_ready.sem, prt_ready.at(b, NT))
                        for q in range(NP):
                            last = mm(r[32 * q:32 * q + 32, :], gv_bd[p][:, q, :, :], pr_t[:, q, :], start=True, stop=True)
                        last.then_inc(ring_full, 1)

                    def job_RO(job, b, p, j):
                        r = bank(job)
                        pe.wait_ge(remt_ready.sem, remt_ready.at(b, 1))
                        for i in range(2):
                            t = 2 * j + i
                            last = mm(r[:, i * D:(i + 1) * D], rem_t[:, t * P:(t + 1) * P], rout_s[:, :], start=True, stop=True)
                        last.then_inc(ring_full, 1)

                    def job_LT(job, b, p, g):
                        r = bank(job)
                        pe.wait_ge(pv_out.sem, pv_out.at(b, g + 1))
                        for t in range(NT):
                            last = tr(r[:, t * P:(t + 1) * P], pv_s[:, t * P:(t + 1) * P], ident[:, :])
                        last.then_inc(ring_full, 1)

                    def pair_tr(job, src, j):
                        r = bank(job)
                        for i in range(2):
                            for k in range(KD):
                                at = (i * KD + k) * P
                                last = tr(r[:, at:at + P], src[:, 2 * j + i, k * P:(k + 1) * P], ident[:, :])
                        last.then_inc(ring_full, 1)

                    def job_OT(job, b, p, j):
                        pe.wait_ge(o_ready.sem, o_ready.at(b, j + 1))
                        pair_tr(job, o, j)

                    def job_WO(job, b, p, j):
                        r = bank(job)
                        pe.wait_ge(ot_ready.sem, ot_ready.at(b, j + 1))
                        for i in range(2):
                            t = 2 * j + i
                            for k in range(KD):
                                last = mm(r[:, i * D:(i + 1) * D], d_t[:, k, t * P:(t + 1) * P], wout_s[:, k, :],
                                          start=(k == 0), stop=(k == KD - 1))
                        last.then_inc(ring_full, 1)

                    def job_H(job, b, p, j):
                        pe.wait_ge(h2_ready.sem, h2_ready.at(b, j + 1))
                        pair_tr(job, h2, j)

                    def job_LG(job, b, p, j):
                        r = bank(job)
                        pe.wait_ge(h2t_ready.sem, h2t_ready.at(b, 2))
                        for t in range(NT):
                            for k in range(KD):
                                last = mm(r[:, t * E:(t + 1) * E], d_t[:, k, t * P:(t + 1) * P], gate_t[:, k, :],
                                          start=(k == 0), stop=(k == KD - 1))
                        last.then_inc(ring_full, 1)

                    def job_LOC(job, b, p, j):
                        r = bank(job)
                        pe.wait_ge(oh_ready.sem, oh_ready.at(b, 1))
                        mm(r[:, 0:NT * E], tri[:, :], oh[:, :, :], start=True, stop=False)
                        mm(r[:, 0:NT * E], ones_b[:, :], seen[:, 0:NT, :], start=False, stop=True).then_inc(ring_full, 1)

                    def s1_bank(b, job):
                        n = S1_ORDER.index(job)
                        if not (is0(b) and n < 2):
                            pe.wait_ge(s1_free.sem, s1_free.at(b, n - 1))
                        return S1[n % 2]

                    def scores_q(b, p, h):
                        if h == 0:
                            pe.wait_ge(stack_in.sem, stack_in.at(b, 12))
                        r = s1_bank(b, h)
                        mm(r[:, :], ident_b[:, :], mask_q[:, :, :], start=True, stop=False, skip_group_check=True)
                        for w in range(NB):
                            t, a = divmod(w, 2)
                            last = mm(r[64 * a:64 * a + 64, t * P:(t + 1) * P], q_st[p][:, h, w * W:(w + 1) * W],
                                      k_st[p][:, h, w * W:w * W + 2 * W], start=False, stop=(w == NB - 1), skip_group_check=True)
                        last.then_inc(s1_full.sem, 1)

                    def max_rows(b, p, half):
                        pe.wait_ge(mxp_ready.sem, mxp_ready.at(b, half + 1))
                        r = s1_bank(b, f"M{half}")[:, 0:S // 2].bitcast(BF16)
                        for t in range(NT):
                            last = tr(r[:, t * P:(t + 1) * P], mx_p[half][:, t, :], ident_b[:, :])
                        last.then_inc(s1_full.sem, 1)

                    def s1_jobs(b, p, jobs):
                        for job in jobs:
                            if isinstance(job, int):
                                scores_q(b, p, job)
                            else:
                                max_rows(b, p, int(job[1]))

                    def scores_k(b, p, h):
                        half, n = divmod(h, HH)
                        if n == 0:
                            pe.wait_ge(s1_free.sem, s1_free.at(b, S1_ORDER.index(f"M{half}") + 1))
                        if not (is0(b) and h < 2):
                            pe.wait_ge(exp_ready.sem, exp_ready.at(b, h - 1))
                        r = S2[h % 2]
                        mm(r[:, :], ident_b[:, :], mask_k[:, :, :], start=True, stop=False, skip_group_check=True)
                        mm(r[:, :], pick[:, n, :], mx_t[half][:, :], start=False, stop=False, skip_group_check=True)
                        for w in range(NB):
                            last = mm(r[:, w * W:(w + 1) * W], k_st[p][:, h, w * W:w * W + 2 * W],
                                      q_st[p][:, h, w * W:(w + 1) * W], start=False, stop=(w == NB - 1), skip_group_check=True)
                        last.then_inc(s2_full.sem, 1)

                    def weigh_values(b, p, h):
                        if h == 0:
                            pe.wait_ge(v_shifted.sem, v_shifted.at(b, 2))
                        if h % 4 == 0 and not (is0(b) and h == 0):
                            pe.wait_ge(pv_out.sem, pv_out.at(b, h // 4))
                        pe.wait_ge(exp_ready.sem, exp_ready.at(b, h + 1))
                        g = h % 4
                        for w in range(NB):
                            v = v_al[p][:, w // 2, h, :] if w % 2 else v_sh[p][:, w // 2, h, :]
                            last = mm(PV[32 * g:32 * g + VW, w * W:(w + 1) * W], v, p_t[h % NPT][:, w * W:(w + 1) * W],
                                      start=True, stop=True, skip_group_check=True)
                        last.then_inc(pv_done.sem, 1)

                    def head(kind, s, c, slot):
                        if kind in ("first", "mid", "last"):
                            s1_jobs(s, c, S1_NOW.get(slot, []))
                            if kind != "last":
                                s1_jobs(s + 1, 1 - c, S1_NEXT.get(slot, []))
                            if slot < H:
                                scores_k(s, c, slot)
                            if slot >= 1:
                                weigh_values(s, c, slot - 1)
                        elif kind == "pro" and slot == 16:
                            for at in range(17):
                                s1_jobs(0, 0, S1_NEXT.get(at, []))

                    pe.wait_ge(blanks, N_BLANKS)
                    steps(Run(pe, {"T": job_T, "Q": job_Q, "K": job_K, "GQ": job_GQ, "V": job_V, "GK": job_GK, "GV": job_GV,
                                   "R": job_R, "PR": job_PR, "RP": job_RP, "RO": job_RO, "LT": job_LT, "OT": job_OT,
                                   "WO": job_WO, "H": job_H, "LG": job_LG, "LOC": job_LOC}, head))

                @block.scalar
                def _(act):
                    def full(job):
                        act.wait_ge(ring_full, job.done)
                        return RING[job.bank]

                    def job_T(job, b, p, k):
                        r = full(job)
                        act.wait_ge(modb_ready.sem, modb_ready.at(b, 1))
                        if not is0(b):
                            act.wait_ge(hbar_ready.sem, hbar_ready.at(b - 1, KD))
                            act.wait_ge(hTl_ready.sem, hTl_ready.at(b - 1, KD))
                        nc.scalar.activation(hT[:, k, :], r[:, :], ACT.Identity, bias=mod_b[:, 0, k:k + 1],
                                             scale=mod_b[:, 1, k:k + 1]).then_inc(hT_ready.sem, 1)

                    def first_part(job, b, m, scale):
                        r = full(job)
                        if not (is0(b) and m < 2):
                            act.wait_ge(parts_stored[m % 2].sem, parts_stored[m % 2].at(b, m // 2))
                        nc.scalar.activation(parts[m % 2][:, 0, :], r[:, :], ACT.Copy, scale=scale).then_inc(p1_ready.sem, 1)

                    def job_Q(job, b, p, m):
                        first_part(job, b, m, HD ** -0.5)

                    def job_K(job, b, p, m):
                        first_part(job, b, 2 + m, 1.0)

                    def job_GQ(job, b, p, m):
                        r = full(job)
                        nc.scalar.activation(gq_t[p][:, :], r[:, :], ACT.Copy, scale=HD ** -0.5).then_inc(gq_ready.sem, 1)

                    def job_V(job, b, p, t):
                        r = full(job)
                        nc.scalar.activation(v_al[p][:, t, :, 0:HD], r[:, 0:D].rearrange("p (h d) -> p h d", d=HD),
                                             ACT.Copy).then_inc(v_ready.sem, 1)
                        nc.scalar.activation(gates[p][:, t, :], r[:, D:VG], ACT.Exp, scale=-1.0).then_inc(gexp_ready.sem, 1)

                    def job_R(job, b, p, t):
                        act.wait_ge(rshift_ready.sem, rshift_ready.at(b, t + 1))
                        nc.scalar.activation(sr[:, t, :, :], sr[:, t, :, :], ACT.Exp).then_inc(rexp_ready.sem, 1)

                    def job_PR(job, b, p, t):
                        r = full(job)
                        nc.scalar.activation(pr_t[:, :, t * P:(t + 1) * P], r[:, :].rearrange("p (q n) -> p q n", q=NP),
                                             ACT.Copy).then_inc(prt_ready.sem, 1)

                    def job_RP(job, b, p, m):
                        r = full(job)
                        nc.scalar.activation(rem_t[:, :], r[:, :], ACT.Copy).then_inc(remt_ready.sem, 1)

                    def pair_out(job, j, ready):
                        r = full(job)
                        nc.scalar.activation(d_t[:, :, 2 * j * P:(2 * j + 2) * P].rearrange("p k (t n) -> p t k n", t=2),
                                             r[:, :].rearrange("p (t k n) -> p t k n", t=2, k=KD), ACT.Copy).then_inc(ready.sem, 1)

                    def job_OT(job, b, p, j):
                        pair_out(job, j, ot_ready)

                    def job_H(job, b, p, j):
                        pair_out(job, j, h2t_ready)

                    def job_LG(job, b, p, j):
                        act.wait_ge(lg_ready.sem, lg_ready.at(b, 1))
                        nc.scalar.activation(lge[:, :, :], lg[:, :, :], ACT.Exp).then_inc(lge_ready.sem, 1)

                    def head(kind, s, c, slot):
                        if kind not in ("first", "mid", "last"):
                            return
                        if slot in (5, 9, 13, 16):
                            g = {5: 0, 9: 1, 13: 2, 16: 3}[slot]
                            act.wait_ge(pv_done.sem, pv_done.at(s, 4 * g + 4))
                            nc.scalar.activation(pv_s[:, :], PV[:, :], ACT.Copy).then_inc(pv_out.sem, 1)
                        if slot < H:
                            act.wait_ge(s2_full.sem, s2_full.at(s, slot + 1))
                            if not (is0(s) and slot < NPT):
                                act.wait_ge(pv_done.sem, pv_done.at(s, slot - NPT + 1))
                            nc.scalar.activation(p_t[slot % NPT][:, :], S2[slot % 2][:, :], ACT.Exp).then_inc(exp_ready.sem, 1)

                    steps(Run(act, {"T": job_T, "Q": job_Q, "K": job_K, "GQ": job_GQ, "V": job_V, "R": job_R, "PR": job_PR,
                                    "RP": job_RP, "OT": job_OT, "H": job_H, "LG": job_LG}, head))

                @block.vector
                def _(dve):
                    v = nc.vector

                    def chained(ins, chain, b, k):
                        ins.then_inc(chain.sem, 1)
                        dve.wait_ge(chain.sem, chain.at(b, k))

                    def full(job):
                        dve.wait_ge(ring_full, job.done)
                        return RING[job.bank]

                    def norm_stats(x_, b, chain, var):
                        for t in range(NT):
                            v.bn_stats(ln_raw[:, t, :], x_[:, t, :]).then_inc(chain.sem, 1)
                        dve.wait_ge(chain.sem, chain.at(b, NT))
                        v.memset(ln_ve[:, :], EPS).then_inc(chain.sem, 1)
                        for t in range(NT):
                            v.bn_aggr(ln_mv[:, t, :], ln_raw[:, t, :]).then_inc(chain.sem, 1)
                        dve.wait_ge(chain.sem, chain.at(b, 2 * NT + 1))
                        v.tensor_tensor(ln_ve[:, :], ln_ve[:, :], ln_mv[:, :, 1], ALU.add).then_inc(var.sem, 1)

                    def norm_apply(x_, y_, b, rstd, ready, per_pair):
                        dve.wait_ge(rstd.sem, rstd.at(b, 1))
                        for t in range(NT):
                            last = v.tensor_scalar(y_[:, t, :], x_[:, t, :], ln_mv[:, t, 0:1], ln_rs[:, t:t + 1], ALU.subtract, ALU.mult)
                            if (t + 1) % per_pair == 0:
                                last.then_inc(ready.sem, 1)

                    def first_stats(b):
                        dve.wait_ge(x_in.sem, x_in.at(b, 1))
                        norm_stats(xin, b, ln1_chain, var1_ready)

                    def first_norm(b):
                        norm_apply(xin, xin, b, rstd1_ready, ln1_ready, 1)
                        if not is0(b):
                            dve.wait_ge(hT_ready.sem, hT_ready.at(b - 1, KD))
                        v.tensor_copy(mod_b[:, :, :], mod_t[:, b, :, :]).then_inc(modb_ready.sem, 1)

                    def job_T(job, b, p, k):
                        dve.wait_ge(hT_ready.sem, hT_ready.at(b, k + 1))
                        v.tensor_copy(hT_h[:, k, :], hT[:, k, :]).then_inc(hTh_ready.sem, 1)
                        chained(v.tensor_reduce(hbar[:, k, 0, :], hT[:, k, :].rearrange("p (n c) -> p n c", c=CH), AX_X, ALU.add),
                                hbar_chain, b, k + 1)
                        v.tensor_copy(hbar[:, k, 1, :], hbar[:, k, 0, :]).then_inc(hbar_ready.sem, 1)

                    def part_rest(job, b, m, scale):
                        r = RING[job.bank]
                        dve.wait_ge(p1_ready.sem, p1_ready.at(b, m + 1))
                        if not (is0(b) and m < 2):
                            dve.wait_ge(p3_ready.sem, p3_ready.at(b, m - 1))
                        v.scalar_tensor_tensor(rest[m % 2][:, :], r[:, :], scale, parts[m % 2][:, 0, :], ALU.mult,
                                               ALU.subtract).then_inc(rest_ready.sem, 1)
                        dve.wait_ge(rest_ready.sem, rest_ready.at(b, m + 1))
                        v.tensor_copy(parts[m % 2][:, 1, :], rest[m % 2][:, :]).then_inc(p2_ready.sem, 1)

                    def job_Q(job, b, p, m):
                        part_rest(job, b, m, HD ** -0.5)

                    def job_K(job, b, p, m):
                        part_rest(job, b, 2 + m, 1.0)

                    def job_V(job, b, p, t):
                        if t == NT - 1:
                            dve.wait_ge(gexp_ready.sem, gexp_ready.at(b, NT))
                            chained(v.tensor_scalar(gates[p][:, :, :], gates[p][:, :, :], 1.0, None, ALU.add), gate_chain, b, 1)
                            v.reciprocal(gates[p][:, :, :], gates[p][:, :, :]).then_inc(gate_ready.sem, 1)

                    def job_GK(job, b, p, m):
                        r = full(job)
                        v.scalar_tensor_tensor(gk_bd[p][:, :, :], bc(r[:, 0:NL].unsqueeze(1), [P, LH, NL]), 1.0 / CH,
                                               bc(head_rows[:, :].unsqueeze(2), [P, LH, NL]), ALU.mult, ALU.mult).then_inc(gk_ready.sem, 1)

                    def job_GV(job, b, p, m):
                        r = full(job)
                        v.scalar_tensor_tensor(gv_bd[p][:, :, :, :], r[:, 0:LD].rearrange("p (q e d) -> p q e d", q=NP, e=2), 1.0 / CH,
                                               pair_rows[:, :, :, :], ALU.mult, ALU.mult).then_inc(gk_ready.sem, 1)

                    def job_R(job, b, p, t):
                        r = full(job)
                        r3 = r[:, :].rearrange("p (h n) -> p h n", h=LH)
                        chained(v.tensor_reduce(rstat[:, 0, t, :], r3, AX_X, ALU.max, negate=True), rmax_chain, b, t + 1)
                        v.tensor_tensor(sr[:, t, :, :], r3, bc(rstat[:, 0, t, :].unsqueeze(2), [P, LH, NL]),
                                        ALU.add).then_inc(rshift_ready.sem, 1)

                    def latent_sum(b, t):
                        dve.wait_ge(rexp_ready.sem, rexp_ready.at(b, t + 1))
                        chained(v.tensor_reduce(rstat[:, 1, t, :], sr[:, t, :, :], AX_X, ALU.add), r_chain, b, 2 * t + 1)
                        chained(v.reciprocal(rstat[:, 2, t, :], rstat[:, 1, t, :]), r_chain, b, 2 * t + 2)
                        v.tensor_copy(rstat[:, 1, t, :], rstat[:, 2, t, :]).then_inc(rinv_ready.sem, 1)

                    def job_RO(job, b, p, j):
                        r = full(job)
                        dve.wait_ge(gate_ready.sem, gate_ready.at(b, 1))
                        if not is0(b):
                            dve.wait_ge(o_ready.sem, o_ready.at(b - 1, 2))
                        v.tensor_tensor(rm[:, 2 * j:2 * j + 2, :].rearrange("p t (h d) -> p t h d", d=HD),
                                        r[:, :].rearrange("p (t h d) -> p t h d", t=2, d=HD),
                                        bc(gates[p][:, 2 * j:2 * j + 2, H:2 * H].unsqueeze(3), [P, 2, H, HD]),
                                        ALU.mult).then_inc(rm_ready.sem, 1)

                    def job_LT(job, b, p, g):
                        r = full(job)
                        r4 = r[:, :].rearrange("p (t h d) -> p t h d", t=NT, d=32)
                        dve.wait_ge(gate_ready.sem, gate_ready.at(b, 1))
                        chained(v.reciprocal(fac[:, 0, :, :], r4[:, :, :, HD]), lt_chain, b, 2 * g + 1)
                        chained(v.tensor_tensor(fac[:, 1, :, :], fac[:, 0, :, :], gates[p][:, :, 4 * g:4 * g + 4], ALU.mult),
                                lt_chain, b, 2 * g + 2)
                        v.tensor_tensor(o[:, :, g * 64:g * 64 + 64].rearrange("p t (h d) -> p t h d", d=HD), r4[:, :, :, 0:HD],
                                        bc(fac[:, 1, :, :].unsqueeze(3), [P, NT, 4, HD]), ALU.mult).then_inc(lt_done.sem, 1)

                    def job_WO(job, b, p, j):
                        r = full(job)
                        dve.wait_ge(modbc_in.sem, modbc_in.at(b, 1))
                        if not is0(b):
                            dve.wait_ge(scattered.sem, scattered.at(b - 1, NT))
                        v.tensor_tensor(h2[:, 2 * j:2 * j + 2, :], r[:, :].rearrange("p (t d) -> p t d", t=2),
                                        bc(mod_bc[:, 0:1, :], [P, 2, D]), ALU.mult).then_inc(ao_ready.sem, 1)

                    def second_stats(b):
                        dve.wait_ge(x1_ready.sem, x1_ready.at(b, 2))
                        norm_stats(x1, b, ln2_chain, var2_ready)

                    def second_norm(b):
                        norm_apply(x1, h2, b, rstd2_ready, h2n_ready, 2)

                    def job_LG(job, b, p, j):
                        r = full(job)
                        r3 = r[:, 0:NT * E].rearrange("p (t e) -> p t e", e=E)
                        chained(v.tensor_reduce(rt[:, 0, :], r3, AX_X, ALU.max), route_chain, b, 1)
                        v.tensor_tensor(lg[:, :, :], r3, bc(rt[:, 0, :].unsqueeze(2), [P, NT, E]), ALU.subtract).then_inc(lg_ready.sem, 1)
                        dve.wait_ge(lg_ready.sem, lg_ready.at(b, 1))
                        chained(v.tensor_scalar(cand[:, :, :], lg[:, :, :], 0.0, -float(E), ALU.is_ge, ALU.mult), route_chain, b, 2)
                        chained(v.tensor_tensor(cand[:, :, :], cand[:, :, :], bc(iota_f[:, :].unsqueeze(1), [P, NT, E]), ALU.add),
                                route_chain, b, 3)
                        chained(v.tensor_reduce(rt[:, 1, :], cand[:, :, :], AX_X, ALU.min), route_chain, b, 4)
                        chained(v.tensor_tensor(oh[:, :, :], cand[:, :, :], bc(rt[:, 1, :].unsqueeze(2), [P, NT, E]), ALU.is_equal),
                                route_chain, b, 5)
                        if not is0(b):
                            chained(v.tensor_copy(seen[:, 0, :], seen[:, NT, :]), route_chain, b, 6)
                        else:
                            chained(v.memset(seen[:, 0, :], 0.0), route_chain, b, 6)
                        for t in range(NT):
                            last = v.tensor_tensor(seen[:, t + 1, :], seen[:, t, :], oh[:, t, :], ALU.add)
                            if t < NT - 1:
                                chained(last, route_chain, b, 7 + t)
                            else:
                                last.then_inc(oh_ready.sem, 1)
                        dve.wait_ge(lge_ready.sem, lge_ready.at(b, 1))
                        chained(v.tensor_reduce(rt[:, 2, :], lge[:, :, :], AX_X, ALU.add), route_chain, b, 10)
                        v.reciprocal(rows[:, :, ROW_P], rt[:, 2, :])
                        v.tensor_scalar(rows[:, :, ROW_T], rows[:, :, ROW_T], float(S), None, ALU.add)
                        v.tensor_scalar(rows[:, :, ROW_G], rows[:, :, ROW_G], 4.0, None, ALU.add)

                    def job_LOC(job, b, p, j):
                        r = full(job)
                        v.tensor_tensor(loc_e[:, :, :], r[:, 0:NT * E].rearrange("p (t e) -> p t e", e=E), oh[:, :, :],
                                        ALU.mult).then_inc(loc_ready.sem, 1)
                        dve.wait_ge(loc_ready.sem, loc_ready.at(b, 1))
                        chained(v.tensor_reduce(rt[:, 3, :], loc_e[:, :, :], AX_X, ALU.add), route_chain, b, 11)
                        v.tensor_scalar(rt[:, 4, :], rt[:, 3, :], float(CAP), None, ALU.is_le)
                        chained(v.scalar_tensor_tensor(rt[:, 5, :], rt[:, 1, :], float(CAP), rt[:, 3, :], ALU.mult, ALU.add),
                                route_chain, b, 12)
                        chained(v.scalar_tensor_tensor(rt[:, 6, :], rt[:, 5, :], -1.0, rt[:, 4, :], ALU.add, ALU.mult), route_chain, b, 13)
                        v.tensor_scalar(slot_i[p][:, :], rt[:, 6, :], float(SLOTS), None, ALU.add).then_inc(slot_ready.sem, 1)

                    def take_max(b, h):
                        n = S1_ORDER.index(h)
                        dve.wait_ge(s1_full.sem, s1_full.at(b, n + 1))
                        v.tensor_reduce(nmx[:, :, h], S1[n % 2][:, :].rearrange("p (t j) -> p t j", t=NT),
                                        AX_X, ALU.max, negate=True).then_inc(s1_free.sem, 1)

                    def max_parts(b, half):
                        dve.wait_ge(s1_free.sem, s1_free.at(b, S1_ORDER.index(half * HH + HH - 1) + 1))
                        m = nmx[:, :, half * HH:(half + 1) * HH]
                        pt = [mx_p[half][:, :, j * HH:(j + 1) * HH] for j in range(3)]
                        k = 4 * half
                        chained(v.tensor_copy(pt[0], m), mx_chain, b, k + 1)
                        chained(v.tensor_tensor(nmx_r[:, :, :], m, pt[0], ALU.subtract), mx_chain, b, k + 2)
                        chained(v.tensor_copy(pt[1], nmx_r[:, :, :]), mx_chain, b, k + 3)
                        chained(v.tensor_tensor(nmx_r[:, :, :], nmx_r[:, :, :], pt[1], ALU.subtract), mx_chain, b, k + 4)
                        v.tensor_copy(pt[2], nmx_r[:, :, :]).then_inc(mxp_ready.sem, 1)

                    def max_rows_out(b, half):
                        n = S1_ORDER.index(f"M{half}")
                        dve.wait_ge(s1_full.sem, s1_full.at(b, n + 1))
                        v.tensor_copy(mx_t[half][:, :], S1[n % 2][:, 0:S // 2].bitcast(BF16)).then_inc(s1_free.sem, 1)

                    def s1_jobs(b, jobs):
                        for job in jobs:
                            if isinstance(job, int):
                                take_max(b, job)
                            else:
                                max_rows_out(b, int(job[1]))

                    def head(kind, s, c, slot):
                        if kind in ("first", "mid", "last"):
                            s1_jobs(s, S1_NOW.get(slot, []))
                            if S1_PARTS.get(slot) == 1:
                                max_parts(s, 1)
                            if kind != "last":
                                s1_jobs(s + 1, S1_NEXT.get(slot, []))
                                if S1_PARTS.get(slot) == 0:
                                    max_parts(s + 1, 0)
                            for t in R_SUMS.get(slot, []):
                                latent_sum(s, t)
                        elif kind == "pro" and slot == 16:
                            for at in range(17):
                                s1_jobs(0, S1_NEXT.get(at, []))
                                if S1_PARTS.get(at) == 0:
                                    max_parts(0, 0)
                        b = norm_batch(kind, s, slot, 14)
                        if b is not None:
                            first_stats(b)
                        b = norm_batch(kind, s, slot, 15)
                        if b is not None:
                            first_norm(b)
                        if kind in ("mid", "last", "epi"):
                            if slot == 7:
                                second_stats(s - 1)
                            if slot == 8:
                                second_norm(s - 1)

                    for i in range(2):
                        v.memset(k_st[i][:, :, 0:W], 0.0).then_inc(blanks, 1)
                        v.memset(v_al[i][:, :, :, HD:VW], 1.0).then_inc(blanks, 1)
                        v.memset(v_sh[i][0:64, 0, :, :], 0.0).then_inc(blanks, 1)
                        v.memset(mx_p[i][:, :, :], 0.0).then_inc(blanks, 1)
                    v.memset(PV[:, :], 0.0).then_inc(blanks, 3)
                    v.tensor_copy(rows[:, :, ROW_T], token_i[:, :])
                    v.memset(rows[:, :, ROW_G], -1.0)
                    steps(Run(dve, {"T": job_T, "Q": job_Q, "K": job_K, "V": job_V, "GK": job_GK, "GV": job_GV, "R": job_R,
                                    "RO": job_RO, "LT": job_LT, "WO": job_WO, "LG": job_LG, "LOC": job_LOC}, head))

                @block.gpsimd
                def _(pool):
                    g = nc.gpsimd

                    def job_T(job, b, p, k):
                        pool.wait_ge(hTh_ready.sem, hTh_ready.at(b, k + 1))
                        g.tensor_tensor(hT_l[:, k, :], hT[:, k, :], hT_h[:, k, :].bitcast(F32), ALU.subtract).then_inc(hTl_ready.sem, 1)

                    def third_part(b, m):
                        pool.wait_ge(p2_ready.sem, p2_ready.at(b, m + 1))
                        g.tensor_tensor(parts[m % 2][:, 2, :], rest[m % 2][:, :], parts[m % 2][:, 1, :],
                                        ALU.subtract).then_inc(p3_ready.sem, 1)

                    def job_Q(job, b, p, m):
                        third_part(b, m)

                    def job_K(job, b, p, m):
                        third_part(b, 2 + m)

                    def job_R(job, b, p, t):
                        pool.wait_ge(rinv_ready.sem, rinv_ready.at(b, t + 1))
                        g.tensor_tensor(sr[:, t, :, :], sr[:, t, :, :], bc(rstat[:, 1, t, :].unsqueeze(2), [P, LH, NL]),
                                        ALU.mult).then_inc(rprob_ready.sem, 1)

                    def add_latent(b):
                        pool.wait_ge(lt_done.sem, lt_done.at(b, 4))
                        pool.wait_ge(rm_ready.sem, rm_ready.at(b, 2))
                        for j in range(2):
                            g.tensor_tensor(o[:, 2 * j:2 * j + 2, :], o[:, 2 * j:2 * j + 2, :], rm[:, 2 * j:2 * j + 2, :],
                                            ALU.add).then_inc(o_ready.sem, 1)

                    def job_WO(job, b, p, j):
                        pool.wait_ge(ao_ready.sem, ao_ready.at(b, j + 1))
                        pool.wait_ge(xres_in.sem, xres_in.at(b, 1))
                        g.tensor_tensor(x1[:, 2 * j:2 * j + 2, :], x1[:, 2 * j:2 * j + 2, :], h2[:, 2 * j:2 * j + 2, :],
                                        ALU.add).then_inc(x1_ready.sem, 1)

                    def modulate(b, p):
                        for j in range(2):
                            pool.wait_ge(h2n_ready.sem, h2n_ready.at(b, j + 1))
                            h = h2[:, 2 * j:2 * j + 2, :]
                            g.tensor_tensor(h, h, bc(mod_bc[:, 1:2, :], [P, 2, D]), ALU.mult).then_inc(add_chain.sem, 1)
                            pool.wait_ge(add_chain.sem, add_chain.at(b, j + 1))
                            g.tensor_tensor(h, h, bc(mod_bc[:, 2:3, :], [P, 2, D]), ALU.add).then_inc(h2_ready.sem, 1)

                    def job_LOC(job, b, p, j):
                        pool.wait_ge(slot_ready.sem, slot_ready.at(b, 1))
                        pool.wait_ge(h2_ready.sem, h2_ready.at(b, 2))
                        pool.wait_ge(slots_zeroed, 16 * N_ZERO)
                        g.tensor_tensor(turn[:, :], blank_row[:, :], blank_row[:, :], ALU.add)
                        for t in range(NT):
                            g.indirect_dma_start(xs_d, bass.IndirectOffsetOnAxis(slot_i[p][:, t:t + 1], 0), rows[:, t, :], None,
                                                 bounds_check=SLOTS - 1, oob_is_err=False).then_inc(scattered.sem, 16)

                    def inverse_deviation(b, var, rstd):
                        pool.wait_ge(var.sem, var.at(b, 1))
                        g.tensor_tensor(ln_rs[:, :], ln_ve[:, :], neg_half[:, :], ALU.pow).then_inc(rstd.sem, 1)

                    def head(kind, s, c, slot):
                        if slot == 0:
                            if kind in ("mid", "last", "epi"):
                                add_latent(s - 1)
                        b = norm_batch(kind, s, slot, 14)
                        if b is not None:
                            inverse_deviation(b, var1_ready, rstd1_ready)
                        if slot == 7 and kind in ("mid", "last", "epi"):
                            inverse_deviation(s - 1, var2_ready, rstd2_ready)
                            modulate(s - 1, 1 - c)

                    g.memset(neg_half[:, :], -0.5).then_inc(sem("exponent_set"), 1)
                    pool.wait_ge(sem("exponent_set"), 1)

                    steps(Run(pool, {"T": job_T, "Q": job_Q, "K": job_K, "R": job_R, "WO": job_WO, "LOC": job_LOC}, head))
                    pool.wait_ge(scattered.sem, scattered.at(B - 1, NT))

                @block.sync
                def _(sp):
                    xv = x.rearrange("b (t p) d -> b p t d", p=P)

                    def head(kind, s, c, slot):
                        b = norm_batch(kind, s, slot, 1)
                        if b is not None:
                            if not is0(b):
                                sp.wait_ge(hT_ready.sem, hT_ready.at(b - 1, KD))
                            sp.dma_start(xin[:, :, :], xv[b]).then_inc(x_in.sem, 16)
                        if kind in ("pro", "first", "mid"):
                            b, p = s + 1, 1 - c
                            if slot == 4:
                                for m in range(4):
                                    sp.wait_ge(p3_ready.sem, p3_ready.at(b, m + 1))
                                    sp.dma_start(qk_d[p, m // 2, :, (m % 2) * P:(m % 2 + 1) * P, :].rearrange("j r n -> r j n"),
                                                 parts[m % 2][:, :, :]).then_inc(parts_stored[m % 2].sem, 16)
                                for kq, (dst, off, slots) in enumerate(((q_st[p], 0, QPART), (k_st[p], W, KPART))):
                                    for i in range(2):
                                        sp.wait_ge(parts_stored[i].sem, parts_stored[i].at(b, kq + 1))
                                    for n, part in enumerate(slots):
                                        sp.dma_start(dst[16 * n:16 * n + 16, :, off:off + S],
                                                     qk_d[p, kq, part, :, :].rearrange("(h r) n -> r h n", r=HD)).then_inc(stack_in.sem, 16)
                            if slot == 8:
                                sp.wait_ge(blanks, N_BLANKS)
                                sp.wait_ge(v_ready.sem, v_ready.at(b, NT))
                                sp.dma_start(v_sh[p][64:128, :, :, :], v_al[p][0:64, :, :, :]).then_inc(v_shifted.sem, 16)
                                sp.dma_start(v_sh[p][0:64, 1:NT, :, :], v_al[p][64:128, 0:NT - 1, :, :]).then_inc(v_shifted.sem, 16)
                        if kind in ("mid", "last", "epi"):
                            b, p = s - 1, 1 - c
                            if slot == 0:
                                if not is0(b):
                                    sp.wait_ge(x1_stored.sem, x1_stored.at(b - 1, 1))
                                    sp.wait_ge(scattered.sem, scattered.at(b - 1, NT))
                                sp.dma_start(x1[:, :, :], xv[b]).then_inc(xres_in.sem, 16)
                                sp.dma_start(mod_bc[:, :, :], mod_d[b, 0:3, :].unsqueeze(0).to_broadcast([P, 3, D])).then_inc(modbc_in.sem, 16)
                            if slot == 6:
                                sp.wait_ge(x1_ready.sem, x1_ready.at(b, 2))
                                sp.dma_start(out.rearrange("b (t p) d -> b p t d", p=P)[b], x1[:, :, :]).then_inc(x1_stored.sem, 16)

                    steps(Run(sp, {}, head))
                    sp.wait_ge(x1_stored.sem, x1_stored.at(B - 1, 1))

        ffn = ExitStack()
        with ffn:
            def fb(name, shape, dt=F32):
                return alloc(ffn, name, shape, dt)

            w1_f = [fb(f"w1_f{i}", [P, KD, HID]) for i in range(2)]
            w2_f = [fb(f"w2_f{i}", [P, MH, D]) for i in range(2)]
            w1_h, w1_l = fb("w1_h", [P, KD, HID], F32R), fb("w1_l", [P, KD, HID], F32R)
            w2_h, w2_l = fb("w2_h", [P, MH, D], F32R), fb("w2_l", [P, MH, D], F32R)
            xg = [fb(f"xg{i}", [P, 3, D]) for i in range(2)]
            xt_h, xt_l = fb("xt_h", [P, KD, CAP], F32R), fb("xt_l", [P, KD, CAP], F32R)
            h_h, h_l = fb("h_h", [P, MH, CAP], F32R), fb("h_l", [P, MH, CAP], F32R)
            y_t = fb("y_t", [P, KD, CAP])
            res = [fb(f"residual{i}", [P, 3, ROW - D]) for i in range(2)]
            token = [fb(f"token{i}", [P, 3], I32) for i in range(2)]
            gate_row = [fb(f"gate_row{i}", [P, 3], I32) for i in range(2)]
            gb = [fb(f"gb{i}", [P, 3, D]) for i in range(2)]
            y_s = fb("y_s", [P, 3, D])
            turn2 = fb("turn2", [1, 3])
            SR = [P, P, CAP - 2 * P]
            XT = [ps[0], ps[1]]
            YA = [ps[2], ps[3]]
            YT = ps[4]
            UP = [ps[5], ps[6], ps[7]]
            NU = len(UP)
            LASTROWS = UP[5 % NU]

            def esig(name, per, by=1):
                return Signal(sem(name), per, by)

            w1_in, w2_in, xg_in = ([esig(f"{name}{i}", per, 16) for i in range(2)] for name, per in (("w1_in", 1), ("w2_in", 1), ("xg_in", 3)))
            w1h_ready, w1_split = esig("w1_hi", KD), esig("w1_split", KD)
            w2h_ready, w2_split = esig("w2_hi", 4), esig("w2_split", 4)
            xt_full, xth_ready, xt_split = esig("xt_full", 1), esig("xt_hi", KD), esig("xt_split", KD)
            up_full, hh_ready, h_split = esig("up_full", MH), esig("h_hi", MH), esig("h_split", MH)
            down_full, yt_ready = esig("down_full", KD), esig("y_t_ready", KD)
            ytr_full, y_weighed, y_added = esig("y_rows_full", 1), esig("y_weighed", 3), esig("y_added", 2)
            res_in, gb_in = ([esig(f"{name}{i}", per, 16) for i in range(2)] for name, per in (("residual_in", 3), ("gb_in", 3)))
            index_ready, y_out = esig("index_ready", 2), esig("y_out", 3, 16)
            xs_e = xs_d.rearrange("(e s) d -> e s d", e=E)

            def expert_steps(eng, run):
                run("first", 0, 0, 0)
                run("mid", 0, 1, 1)
                with eng.Fori(0, (E - 4) // 2) as i:
                    run("mid", i + 1, 0, i * 2 + 2)
                    run("mid", i + 1, 1, i * 2 + 3)
                run("noload", E // 2 - 1, 0, E - 2)
                run("last", E // 2 - 1, 1, E - 1)

            with nc.Block() as block:
                @block.sync
                def _(sp):
                    def rows_in(e, dst, cols, sig_):
                        sp.dma_start(dst[:, 0:2, :], xs_e[e, 0:2 * P, cols].rearrange("(s p) d -> p s d", p=P)).then_inc(sig_.sem, 16)
                        sp.dma_start(dst[0:SR[2], 2, :], xs_e[e, 2 * P:CAP, cols]).then_inc(sig_.sem, 32)

                    def load_res(e, p):
                        rows_in(e, res[p], slice(D, ROW), res_in[p])

                    def load(e, p):
                        sp.dma_start(w1_f[p][:, :, :], w1[e].rearrange("(k p) n -> p k n", p=P)).then_inc(w1_in[p].sem, 16)
                        rows_in(e, xg[p], slice(0, D), xg_in[p])

                    def load2(e, p):
                        sp.dma_start(w2_f[p][:, :, :], w2[e].rearrange("(m p) n -> p m n", p=P)).then_inc(w2_in[p].sem, 16)

                    for e in range(2):
                        load(e, e)
                        load2(e, e)
                    for e in range(2):
                        load_res(e, e)

                    def run(kind, j, p, e):
                        if kind in ("first", "mid"):
                            sp.wait_ge(xt_split.sem, xt_split.at(e, KD))
                            load(e + 2, p)
                            sp.wait_ge(w2_split.sem, w2_split.at(e, 4))
                            load2(e + 2, p)

                        if kind in ("mid", "noload"):
                            sp.wait_ge(y_out.sem, y_out.at(e - 1, 3))
                            load_res(e + 1, 1 - p)

                    expert_steps(sp, run)

                @block.tensor
                def _(pe):
                    mm = nc.tensor.matmul

                    def transpose_rows(j, p, e):
                        pe.wait_ge(xg_in[p].sem, xg_in[p].at(j, 3))
                        if not (isinstance(e, int) and e == 0):
                            pe.wait_ge(xt_split.sem, xt_split.at(e - 1, KD))
                        for k in range(KD):
                            for i, (s0, n) in enumerate(ST):
                                last = mm(XT[k][:, s0:s0 + n], xg[p][0:n, i, k * P:(k + 1) * P], ident[0:n, 0:n],
                                          start=True, stop=True, is_transpose=True)
                        last.then_inc(xt_full.sem, 1)

                    def mm3(dst, terms):
                        for n, (l, r) in enumerate(terms):
                            last = mm(dst, l, r, start=(n == 0), stop=(n == len(terms) - 1))
                        return last

                    def rows_out(e, free_from, up_jobs):
                        pe.wait_ge(h_split.sem, h_split.at(free_from, up_jobs))
                        pe.wait_ge(yt_ready.sem, yt_ready.at(e, KD))
                        if not (isinstance(e, int) and e == 0):
                            pe.wait_ge(y_weighed.sem, y_weighed.at(e - 1, 3))
                        for k in range(KD):
                            for i in range(2):
                                mm(YT[:, i * D + k * P:i * D + (k + 1) * P], y_t[:, k, i * P:(i + 1) * P], ident[:, :],
                                   start=True, stop=True, is_transpose=True)
                            last = mm(LASTROWS[0:64, k * P:(k + 1) * P], y_t[:, k, 2 * P:CAP], ident[:, :], start=True, stop=True, is_transpose=True)
                        last.then_inc(ytr_full.sem, 1)

                    def run(kind, j, p, e):
                        pe.wait_ge(xt_split.sem, xt_split.at(e, KD))
                        for m in range(MH):
                            if m == 0:
                                pe.wait_ge(w1_split.sem, w1_split.at(e, KD))
                            if not (kind == "first" and m < NU):
                                pe.wait_ge(h_split.sem, h_split.at(e, m - NU + 1 if m >= NU else min(m - 1, 0)))
                            if m == 5 % NU and kind != "first" and not (isinstance(e, int) and e < 2):
                                pe.wait_ge(y_weighed.sem, y_weighed.at(e - 2, 3))
                            c = slice(m * P, (m + 1) * P)
                            terms = [(w[:, k, c], x_[:, k, :]) for k in range(KD) for w, x_ in ((w1_h, xt_h), (w1_l, xt_h), (w1_h, xt_l))]
                            mm3(UP[m % NU][:, 0:CAP], terms).then_inc(up_full.sem, 1)
                        if kind != "first":
                            rows_out(e - 1, e, 6)
                        if kind != "last":
                            transpose_rows(j + p, 1 - p, e + 1)
                        for k in range(KD):
                            if k == 0:
                                pe.wait_ge(w2_split.sem, w2_split.at(e, 4))
                                pe.wait_ge(h_split.sem, h_split.at(e, MH))
                            if kind != "first":
                                pe.wait_ge(yt_ready.sem, yt_ready.at(e - 1, k + 1))
                            c = slice(k * P, (k + 1) * P)
                            terms = [(w[:, m, c], h_[:, m, :]) for m in range(MH) for w, h_ in ((w2_h, h_h), (w2_l, h_h), (w2_h, h_l))]
                            mm3(YA[k][:, 0:CAP], terms).then_inc(down_full.sem, 1)

                    transpose_rows(0, 0, 0)
                    expert_steps(pe, run)
                    rows_out(E - 1, E - 1, MH)

                @block.scalar
                def _(act):
                    def split_rows(e):
                        act.wait_ge(xt_full.sem, xt_full.at(e, 1))
                        if not (isinstance(e, int) and e == 0):
                            act.wait_ge(up_full.sem, up_full.at(e - 1, MH))
                        for k in range(KD):
                            nc.scalar.activation(xt_h[:, k, :], XT[k][:, 0:CAP], ACT.Copy).then_inc(xth_ready.sem, 1)

                    def split_w1(j, p, e):
                        act.wait_ge(w1_in[p].sem, w1_in[p].at(j, 1))
                        if not (isinstance(e, int) and e == 0):
                            act.wait_ge(up_full.sem, up_full.at(e - 1, MH))
                        for k in range(KD):
                            nc.scalar.activation(w1_h[:, k, :], w1_f[p][:, k, :], ACT.Copy).then_inc(w1h_ready.sem, 1)

                    def run(kind, j, p, e):
                        act.wait_ge(w2_in[p].sem, w2_in[p].at(j, 1))
                        if kind != "first":
                            act.wait_ge(down_full.sem, down_full.at(e - 1, KD))
                        for m in range(MH):
                            act.wait_ge(up_full.sem, up_full.at(e, m + 1))
                            nc.scalar.activation(h_h[:, m, :], UP[m % NU][:, 0:CAP], ACT.Relu).then_inc(hh_ready.sem, 1)
                            if m % 2 == 1:
                                c = slice(m - 1, m + 1)
                                nc.scalar.activation(w2_h[:, c, :], w2_f[p][:, c, :], ACT.Copy).then_inc(w2h_ready.sem, 1)
                        if kind != "last":
                            split_w1(j + p, 1 - p, e + 1)
                        if kind != "last":
                            split_rows(e + 1)
                        for k in range(KD):
                            act.wait_ge(down_full.sem, down_full.at(e, k + 1))
                            nc.scalar.activation(y_t[:, k, :], YA[k][:, 0:CAP], ACT.Copy).then_inc(yt_ready.sem, 1)

                    split_w1(0, 0, 0)
                    split_rows(0)
                    expert_steps(act, run)

                @block.vector
                def _(dve):
                    v = nc.vector

                    def split_w1(j, p, e):
                        for k in range(KD):
                            dve.wait_ge(w1h_ready.sem, w1h_ready.at(e, k + 1))
                            v.tensor_tensor(w1_l[:, k, :], w1_f[p][:, k, :], w1_h[:, k, :].bitcast(F32), ALU.subtract).then_inc(w1_split.sem, 1)

                    def split_rows(e):
                        for k in range(KD):
                            dve.wait_ge(xth_ready.sem, xth_ready.at(e, k + 1))
                            v.tensor_tensor(xt_l[:, k, :], XT[k][:, 0:CAP], xt_h[:, k, :].bitcast(F32), ALU.subtract).then_inc(xt_split.sem, 1)

                    def run(kind, j, p, e):
                        for m in range(MH):
                            dve.wait_ge(hh_ready.sem, hh_ready.at(e, m + 1))
                            v.scalar_tensor_tensor(h_l[:, m, :], UP[m % NU][:, 0:CAP], 0.0, h_h[:, m, :].bitcast(F32), ALU.max,
                                                   ALU.subtract).then_inc(h_split.sem, 1)
                            if m % 2 == 1:
                                c = slice(m - 1, m + 1)
                                dve.wait_ge(w2h_ready.sem, w2h_ready.at(e, m // 2 + 1))
                                v.tensor_tensor(w2_l[:, c, :], w2_f[p][:, c, :], w2_h[:, c, :].bitcast(F32), ALU.subtract).then_inc(w2_split.sem, 1)
                        indices(j, p, e)
                        if kind != "last":
                            split_w1(j + p, 1 - p, e + 1)
                        if kind != "first":
                            weigh(j - 1 + p, 1 - p, e - 1)
                        if kind != "last":
                            split_rows(e + 1)

                    def indices(j, p, e):
                        dve.wait_ge(res_in[p].sem, res_in[p].at(j, 3))
                        v.tensor_scalar(token[p][:, 0:2], res[p][:, 0:2, ROW_T - D], float(T), None, ALU.add)
                        v.tensor_scalar(token[p][0:SR[2], 2:3], res[p][0:SR[2], 2:3, ROW_T - D], float(T), None, ALU.add
                                        ).then_inc(index_ready.sem, 1)
                        v.tensor_scalar(gate_row[p][:, 0:2], res[p][:, 0:2, ROW_G - D], 0.0, None, ALU.add)
                        v.tensor_scalar(gate_row[p][0:SR[2], 2:3], res[p][0:SR[2], 2:3, ROW_G - D], 0.0, None, ALU.add
                                        ).then_inc(index_ready.sem, 1)

                    def weigh(j, p, e):
                        dve.wait_ge(ytr_full.sem, ytr_full.at(e, 1))
                        dve.wait_ge(gb_in[p].sem, gb_in[p].at(j, 3))
                        if not (isinstance(e, int) and e == 0):
                            dve.wait_ge(y_out.sem, y_out.at(e - 1, 3))
                        for i, n in enumerate(SR):
                            y = YT[:, i * D:(i + 1) * D] if i < 2 else LASTROWS[0:n, 0:D]
                            v.scalar_tensor_tensor(y_s[0:n, i, :], y, res[p][0:n, i, ROW_P - D:ROW_P - D + 1], gb[p][0:n, i, :],
                                                   ALU.mult, ALU.mult).then_inc(y_weighed.sem, 1)

                    split_w1(0, 0, 0)
                    split_rows(0)
                    expert_steps(dve, run)
                    weigh(E // 2 - 1, 1, E - 1)

                @block.gpsimd
                def _(pool):
                    g = nc.gpsimd

                    def gather_gates(e, p):
                        pool.wait_ge(index_ready.sem, index_ready.at(e, 2))
                        g.tensor_tensor(turn2[:, p:p + 1], blank_row[:, :], blank_row[:, :], ALU.add)
                        for i, n in enumerate(SR):
                            g.indirect_dma_start(gb[p][0:n, i, :], None, mod_d.rearrange("b r d -> (b r) d"),
                                                 bass.IndirectOffsetOnAxis(gate_row[p][0:n, i:i + 1], 0),
                                                 bounds_check=4 * B - 1, oob_is_err=False).then_inc(gb_in[p].sem, 16)

                    def rows_out(e, p):
                        pool.wait_ge(y_weighed.sem, y_weighed.at(e, 3))
                        g.tensor_tensor(y_s[:, 0:2, :], y_s[:, 0:2, :], res[p][:, 0:2, 0:D], ALU.add).then_inc(y_added.sem, 1)
                        g.tensor_tensor(y_s[0:SR[2], 2, :], y_s[0:SR[2], 2, :], res[p][0:SR[2], 2, 0:D], ALU.add).then_inc(y_added.sem, 1)
                        pool.wait_ge(y_added.sem, y_added.at(e, 2))
                        g.tensor_tensor(turn2[:, 2:3], blank_row[:, :], blank_row[:, :], ALU.add)
                        for i, n in enumerate(SR):
                            g.indirect_dma_start(out.rearrange("b s d -> (b s) d"), bass.IndirectOffsetOnAxis(token[p][0:n, i:i + 1], 0),
                                                 y_s[0:n, i, :], None, bounds_check=T - 1, oob_is_err=False).then_inc(y_out.sem, 16)

                    def run(kind, j, p, e):
                        gather_gates(e, p)
                        if kind != "first":
                            rows_out(e - 1, 1 - p)

                    expert_steps(pool, run)
                    rows_out(E - 1, 1)
                    pool.wait_ge(y_out.sem, y_out.at(E - 1, 3))


_INS = ["L0_attn_x", "L0_attn_wq", "L0_attn_wk", "L0_attn_wv", "L0_attn_wgq", "L0_attn_wgk", "L0_attn_wgv", "L0_attn_r_out_w",
        "L0_attn_gate_local_w", "L0_attn_gate_remote_w", "L0_attn_w_out", "L0_ffn_gate_w", "L0_ffn_w1", "L0_ffn_w2", "L0_c", "L0_wmod"]


def kernel(**inputs):
    import numpy as np
    import concourse.bacc as bacc
    from concourse.bass_utils import run_bass_kernel_spmd

    nc = bacc.Bacc("TRN2", target_bir_lowering=False, num_devices=1)
    arrays, args = {}, []
    for name in _INS:
        a = np.ascontiguousarray(inputs[name])
        arrays[f"in_{name}"] = a
        args.append(nc.dram_tensor(f"in_{name}", a.shape, mybir.dt.from_np(a.dtype), kind="ExternalInput").ap())
    args.append(nc.dram_tensor("out_rows", (B, S, D), F32, kind="ExternalOutput").ap())
    adaln_moe_kernel(nc, *args)
    r = run_bass_kernel_spmd(nc, [arrays], core_ids=[0])
    return r.results[0]["out_rows"]
```

```python
from contextlib import ExitStack

import concourse.bass as bass
from concourse import mybir

ALU = mybir.AluOpType
ACT = mybir.ActivationFunctionType
F32 = mybir.dt.float32
F32R = mybir.dt.float32r
BF16 = mybir.dt.bfloat16
I32 = mybir.dt.int32
AX_X = mybir.AxisListType.X

P = 128
B, S, D = 8, 512, 256
KD = D // P
NT = S // P
H, HD = 16, 16
W = 64
NB = S // W
LH, LD, NL = 8, 128, 64
CH = S // NL
NP = LH // 2
E, HID = 16, 1024
T = B * S
CAP = int(1.25 * T / E)
SLOTS = E * CAP
ROW_X, ROW_P, ROW_T, ROW_G, ROW = D, 2 * D, 2 * D + 1, 2 * D + 2, 2 * D + 3
MH = HID // P
ST = [(0, 128), (128, 128), (256, CAP - 256)]
EPS = 1e-5
BIG = -1.0e30
QPART = [0, 0, 0, 1, 1, 2]
KPART = [0, 1, 2, 0, 1, 0]
KS_ROWS = 16 * len(QPART)
VW = HD + 1
HH = H // 2
SB = 3

SLOT_JOBS = {
    0: ["A.T0", "A.T1"],
    1: ["D.OT0", "D.OT1"],
    2: ["A.Q0", "A.Q1"],
    3: ["A.K0", "A.K1"],
    4: ["D.WO0", "D.WO1"],
    5: ["A.GQ", "A.V0"],
    6: ["L.LT0", "A.V1"],
    7: ["A.V2", "A.V3"],
    8: ["A.GK", "A.GV", "C.R0"],
    9: ["C.R1", "D.H0"],
    10: ["C.R2", "L.LT1", "D.H1"],
    11: ["C.R3", "D.LG"],
    12: ["C.PR0"],
    13: ["C.PR1", "D.LOC"],
    14: ["L.LT2", "C.PR2", "C.PR3"],
    15: ["C.RP"],
    16: ["C.RO0", "C.RO1", "L.LT3"],
}
S1_NEXT = {10: [0, 1], 11: [2, 3], 12: [4], 13: [5], 14: [6, 7], 15: [8, "M0"], 16: [9, 10]}
S1_NOW = {0: [11, 12], 1: [13, 14], 2: [15], 3: ["M1"]}
S1_ORDER = [j for s in range(17) for j in S1_NEXT.get(s, [])] + [j for s in range(17) for j in S1_NOW.get(s, [])]
S1_PARTS = {14: 0, 2: 1}
R_EXP = {9: 0, 10: 1, 11: 2, 12: 3}
R_SUM = {10: 0, 11: 1, 12: 2, 13: 3}
HBAR = 3
GATES = 9
NORM2 = 7
NORM1 = 5
ALL_JOBS = [j for s in range(17) for j in SLOT_JOBS[s]]
PRO = [j for j in ALL_JOBS if j[0] == "A"]
FIRST = [j for j in ALL_JOBS if j[0] != "D"]
LAST = [j for j in ALL_JOBS if j[0] != "A"]
EPI = [j for j in ALL_JOBS if j[0] == "D"]
ORDER = {"pro": PRO, "first": FIRST, "mid": ALL_JOBS, "last": LAST, "epi": EPI}
BEFORE = {"pro": [], "first": PRO, "mid": ALL_JOBS, "last": ALL_JOBS, "epi": LAST}
START = {"pro": 0, "first": len(PRO), "mid": len(PRO) + len(FIRST)}
START["last"] = START["mid"] + (B - 2) * len(ALL_JOBS)
START["epi"] = START["last"] + len(LAST)


def batch_of(name, step):
    return {"A": step + 1, "C": step, "L": step, "D": step - 1}[name[0]]


class Job:

    def __init__(self, kind, step, name):
        self.kind = kind
        at = ORDER[kind].index(name)
        turns = (step - 1) if kind == "mid" else 0
        self.bank = (START[kind] + at) % SB
        self.done = START[kind] + at + 1 + len(ALL_JOBS) * turns
        if at >= SB:
            prev = ORDER[kind][at - SB]
            self.before = (prev, batch_of(prev, step))
        elif BEFORE[kind]:
            prev = BEFORE[kind][at - SB]
            self.before = (prev, batch_of(prev, step - 1))
        else:
            self.before = None


class Signal:

    def __init__(self, sem, per, by=1):
        self.sem, self.per, self.by = sem, per, by

    def at(self, b, k):
        return b * (self.per * self.by) + k * self.by


def bc(ap, shape):
    return ap.to_broadcast(shape)


def adaln_moe_kernel(nc, x, wq, wk, wv, wgq, wgk, wgv, r_out, gl_w, gr_w, w_out, gate_w, w1, w2, c_in, wmod, out):
    top = ExitStack()
    sems = {}

    def sem(name):
        if name not in sems:
            sems[name] = top.enter_context(nc.semaphore(name))
        return sems[name]

    def alloc(ctx, name, shape, dt):
        return ctx.enter_context(nc.sbuf_tensor(name, shape, dt))

    with top:
        qk_d = nc.dram_tensor("qk_parts", [2, 2, 3, D, S], BF16).ap()
        mod_d = nc.dram_tensor("mod_rows", [B, 4, D], F32).ap()
        xs_d = nc.dram_tensor("expert_in", [SLOTS, ROW], F32).ap()

        ident = alloc(top, "ident", [P, P], F32)
        blank_row = alloc(top, "blank_row", [1, 1], F32)
        shared = [alloc(top, f"q_stack_or_weights{i}", [P, H * S], BF16) for i in range(2)]
        w1_f, w2_f = ([half.bitcast(F32) for half in (s_[:, i * H * S // 2:(i + 1) * H * S // 2] for s_ in shared)] for i in range(2))
        w1_f = [w.rearrange("p (k n) -> p k n", k=KD) for w in w1_f]
        w2_f = [w.rearrange("p (m d) -> p m d", m=MH) for w in w2_f]
        w1_in, w2_in = ([Signal(sem(f"{name}{i}"), 1, 16) for i in range(2)] for name in ("w1_in", "w2_in"))

        def load_w1(sp, e, p):
            sp.dma_start(w1_f[p][:, :, :], w1[e].rearrange("(k p) n -> p k n", p=P)).then_inc(w1_in[p].sem, 16)

        def load_w2(sp, e, p):
            sp.dma_start(w2_f[p][:, :, :], w2[e].rearrange("(m p) n -> p m n", p=P)).then_inc(w2_in[p].sem, 16)

        ps = [top.enter_context(nc.psum_tensor(f"bank{i}", [P, 512], F32)) for i in range(8)]

        att = ExitStack()
        with att:
            def sb(name, shape, dt=F32):
                return alloc(att, name, shape, dt)

            ident_b = sb("ident_b", [P, P], BF16)
            mask_q = sb("mask_q", [P, NT, P], BF16)
            mask_k = sb("mask_k", [P, NB, W], BF16)
            mask_r = sb("mask_r", [P, NT, LH, NL], BF16)
            tri = sb("tri", [P, P], BF16)
            ones_b = sb("ones_b", [P, P], BF16)
            head_rows = sb("head_rows", [P, LH])
            pair_rows = sb("pair_rows", [P, NP, 2, HD])
            iota_f = sb("iota_f", [P, E])
            token_i = sb("token_i", [P, NT], I32)
            zero = sb("zero", [P, ROW])
            slots_zeroed = sem("slots_zeroed")
            N_ZERO, ZERO_ROWS = 10, SLOTS // P // 10

            def zero_slots(sp, parts):
                for i in parts:
                    sp.dma_start(xs_d[i * ZERO_ROWS * P:(i + 1) * ZERO_ROWS * P, :].rearrange("(p r) d -> p r d", p=P),
                                 zero[:, :].unsqueeze(1).to_broadcast([P, ZERO_ROWS, ROW])).then_inc(slots_zeroed, 16)

            wq_h, wq_l = sb("wq_h", [P, KD, D], F32R), sb("wq_l", [P, KD, D], F32R)
            wk_h, wk_l = sb("wk_h", [P, KD, D], F32R), sb("wk_l", [P, KD, D], F32R)
            wg_h, wg_l = sb("wg_h", [P, KD, LD], F32R), sb("wg_l", [P, KD, LD], F32R)
            VG = D + 2 * H
            wv_h, wv_l = sb("wv_h", [P, KD, VG], F32R), sb("wv_l", [P, KD, VG], F32R)
            wgk_s, wgv_s = sb("wgk_s", [P, KD, LD]), sb("wgv_s", [P, KD, LD])
            rout_s, wout_s = sb("rout_s", [P, D]), sb("wout_s", [P, KD, D])
            gate_t = sb("gate_t", [P, KD, E])
            xin = sb("xin", [P, NT, D])
            mod_t = sb("mod_t", [P, B, 2, KD])

            ln_raw = sb("ln_raw", [P, NT, 6])
            ln_mv = sb("ln_mv", [P, NT, 2])
            ln_ve = sb("ln_ve", [P, NT])
            ln_rs = sb("ln_rs", [P, NT])
            neg_half = sb("neg_half", [P, NT])

            def sig(name, per, by=1):
                return Signal(sem(name), per, by)

            x_in, ln1_ready, ln1_chain = sig("x_in", 1, 16), sig("ln1_ready", NT), sig("ln1_chain", 2 * NT + 1)
            var1_ready, rstd1_ready = sig("var1_ready", 1), sig("rstd1_ready", 1)

            def norm_stats(dve, x_, b, chain, var):
                v = nc.vector
                for t in range(NT):
                    v.bn_stats(ln_raw[:, t, :], x_[:, t, :]).then_inc(chain.sem, 1)
                dve.wait_ge(chain.sem, chain.at(b, NT))
                v.memset(ln_ve[:, :], EPS).then_inc(chain.sem, 1)
                for t in range(NT):
                    v.bn_aggr(ln_mv[:, t, :], ln_raw[:, t, :]).then_inc(chain.sem, 1)
                dve.wait_ge(chain.sem, chain.at(b, 2 * NT + 1))
                v.tensor_tensor(ln_ve[:, :], ln_ve[:, :], ln_mv[:, :, 1], ALU.add).then_inc(var.sem, 1)

            def norm_apply(dve, x_, y_, b, rstd, ready, per_pair):
                dve.wait_ge(rstd.sem, rstd.at(b, 1))
                for t in range(NT):
                    last = nc.vector.tensor_scalar(y_[:, t, :], x_[:, t, :], ln_mv[:, t, 0:1], ln_rs[:, t:t + 1], ALU.subtract, ALU.mult)
                    if (t + 1) % per_pair == 0:
                        last.then_inc(ready.sem, 1)

            def inverse_deviation(pool, b, var, rstd):
                pool.wait_ge(var.sem, var.at(b, 1))
                nc.gpsimd.tensor_tensor(ln_rs[:, :], ln_ve[:, :], neg_half[:, :], ALU.pow).then_inc(rstd.sem, 1)

            wmod_f = shared[1].bitcast(F32)[:, 0:KD * 6 * D].rearrange("p (k n) -> p k n", k=KD)
            c_t = sb("c_t", [P, KD, B])
            mod_s = sb("mod_s", [P, B, 2, KD])
            mod_o = sb("mod_o", [P, B, 4, KD])
            mod_rows = sb("mod_lines", [B * 4 * KD, P])
            wm_in = [sem("wmod_in0"), sem("wmod_in1")]

            def modulation(bank, c):
                for k in range(KD):
                    last = nc.tensor.matmul(bank[:, c * B:(c + 1) * B], wmod_f[:, k, c * P:(c + 1) * P],
                                            c_t[:, k, :], start=(k == 0), stop=(k == KD - 1))
                return last

            def modulation_of(bank):
                return bank[:, 0:12 * B].rearrange("p (r h b) -> p r b h", h=KD, b=B)

            setup = ExitStack()
            with setup:
                def st(name, shape, dt=F32):
                    return alloc(setup, name, shape, dt)

                wq_f, wk_f, wg_f = st("wq_f", [P, KD, D]), st("wk_f", [P, KD, D]), st("wg_f", [P, KD, LD])
                wv_f = st("wv_f", [P, KD, VG])
                gates_f = st("gates_f", [P, 2, D])
                gate_tmp = st("gate_tmp", [P, 2, KD, D])
                c_e = st("c_e", [P, KD, B])
                see_q, see_k = st("see_q", [P, P]), st("see_k", [P, W])
                see_r = st("see_r", [P, NT, NL])
                tri_f = st("tri_f", [P, P])
                iota_i = st("iota_i", [P, E], I32)
                gate_r = st("gate_r", [E, D])
                c_inn = sem("cond_in")
                wv_in, wk_in, w_in = sem("gate_weights_in"), sem("key_weights_in"), sem("weights_in")
                with nc.Block() as block:
                    @block.sync
                    def _(sp):
                        def rows_of(w_):
                            return w_.rearrange("(k p) n -> p k n", p=P)

                        with nc.allow_non_contiguous_dma("condition, transposed"):
                            for k in range(KD):
                                sp.dma_start(c_t[:, k, :], c_in.rearrange("b (k p) -> k p b", p=P)[k]).then_inc(c_inn, 16)
                        sp.dma_start(wq_f[:, :, :], rows_of(wq)).then_inc(wv_in, 16)
                        for i, g in enumerate((gl_w, gr_w)):
                            sp.dma_start(gates_f[:, i, :], g.rearrange("h d -> (h d)")[None, :].to_broadcast([P, D])).then_inc(wv_in, 16)
                        sp.dma_start(wv_f[:, :, 0:D], rows_of(wv)).then_inc(wv_in, 16)
                        for dst, src in ((wk_f, wk), (wg_f, wgq)):
                            sp.dma_start(dst[:, :, :], rows_of(src)).then_inc(wk_in, 16)
                        sp.dma_start(wmod_f[:, :, 0:2 * D], rows_of(wmod)[:, :, 0:2 * D]).then_inc(wm_in[0], 16)
                        sp.dma_start(xin[:, :, :], x.rearrange("b (t p) d -> b p t d", p=P)[0]).then_inc(x_in.sem, 16)
                        sp.dma_start(wmod_f[:, :, 2 * D:6 * D], rows_of(wmod)[:, :, 2 * D:6 * D]).then_inc(wm_in[1], 16)
                        for dst, src in ((wgk_s, wgk), (wgv_s, wgv), (wout_s, w_out)):
                            sp.dma_start(dst[:, :, :], rows_of(src)).then_inc(w_in, 16)
                        sp.dma_start(rout_s[:, :], r_out).then_inc(w_in, 16)
                        sp.dma_start(gate_r[:, :], gate_w).then_inc(sem("gate_w_in"), 16)
                        sp.wait_ge(sem("zero_set"), 1)
                        zero_slots(sp, range(3))
                        sp.wait_ge(w_in, 16 * 4)

                    @block.gpsimd
                    def _(pool):
                        shapes = sem("shapes")
                        n = [0]

                        def select(ap, cond, fill, base, pattern, mult):
                            nc.gpsimd.affine_select(out=ap, in_=ap, compare_op=cond, fill=fill, base=base,
                                                    pattern=pattern, channel_multiplier=mult).then_inc(shapes, 1)
                            n[0] += 1
                            pool.wait_ge(shapes, n[0])

                        pool.wait_ge(sem("blank"), 7)
                        select(ident[:, :], ALU.not_equal, 1.0, 0, [[-1, P]], 1)
                        for half in range(2):
                            m = see_q[64 * half:64 * half + 64, :]
                            select(m, ALU.is_gt, BIG, 0, [[1, P]], -1)
                            select(m, ALU.is_ge, BIG, W, [[-1, P]], 1)
                        select(see_k[:, :], ALU.is_gt, BIG, 0, [[-1, W]], 1)
                        select(see_k[:, :], ALU.is_ge, BIG, W, [[1, W]], -1)
                        select(see_r[:, :, :], ALU.is_ge, BIG, 0, [[P, NT], [-CH, NL]], 1)
                        select(tri_f[:, :], ALU.is_ge, 0.0, 0, [[1, P]], -1)
                        select(head_rows[:, :], ALU.is_ge, 0.0, 0, [[-HD, LH]], 1)
                        select(head_rows[:, :], ALU.is_ge, 0.0, HD - 1, [[HD, LH]], -1)
                        select(pair_rows[:, :, 0, :], ALU.is_ge, 0.0, NL - 1, [[0, NP], [0, HD]], -1)
                        select(pair_rows[:, :, 1, :], ALU.is_ge, 0.0, -NL, [[0, NP], [0, HD]], 1)
                        nc.gpsimd.iota(iota_i[:, :], pattern=[[1, E]], base=0, channel_multiplier=0).then_inc(shapes, 1)
                        nc.gpsimd.iota(token_i[:, :], pattern=[[P, NT]], base=-T - S, channel_multiplier=1).then_inc(shapes, 1)
                        nc.gpsimd.memset(neg_half[:, :], -0.5).then_inc(shapes, 1)
                        pool.wait_ge(shapes, n[0] + 3)
                        inverse_deviation(pool, 0, var1_ready, rstd1_ready)

                    @block.scalar
                    def _(act):
                        act.wait_ge(c_inn, 16 * KD)
                        nc.scalar.activation(c_e[:, :, :], c_t[:, :, :], ACT.Exp, scale=-1.0).then_inc(sem("cond_exp"), 1)
                        hi = sem("weights_hi")
                        act.wait_ge(wv_in, 16 * 4)
                        nc.scalar.activation(wq_h[:, :, :], wq_f[:, :, :], ACT.Copy).then_inc(hi, 1)
                        act.wait_ge(sem("gate_columns"), 2)
                        nc.scalar.activation(wv_h[:, :, :], wv_f[:, :, :], ACT.Copy).then_inc(hi, 1)
                        act.wait_ge(wk_in, 16 * 2)
                        nc.scalar.activation(wk_h[:, :, :], wk_f[:, :, :], ACT.Copy).then_inc(hi, 1)
                        nc.scalar.activation(wg_h[:, :, :], wg_f[:, :, :], ACT.Copy).then_inc(hi, 1)
                        act.wait_ge(sem("shapes"), 14)
                        nc.scalar.activation(mask_q[:, :, :], bc(see_q[:, :].unsqueeze(1), [P, NT, P]), ACT.Copy).then_inc(sem("masks_spread"), 1)
                        nc.scalar.activation(mask_k[:, :, :], bc(see_k[:, :].unsqueeze(1), [P, NB, W]), ACT.Copy).then_inc(sem("masks_spread"), 1)
                        for t in range(NT):
                            nc.scalar.activation(mask_r[:, t, :, :], bc(see_r[:, t, :].unsqueeze(1), [P, LH, NL]), ACT.Copy)

                    @block.tensor
                    def _(pe):
                        pe.wait_ge(sem("silu_ready"), 1)
                        pe.wait_ge(wm_in[0], 16)
                        for c in range(4):
                            last = modulation(ps[0], c)
                        last.then_inc(sem("mod_matmul"), 1)
                        pe.wait_ge(sem("gate_w_in"), 16)
                        pe.wait_ge(sem("shapes"), 1)
                        for k in range(KD):
                            last = nc.tensor.matmul(ps[4][:, k * E:(k + 1) * E], gate_r[:, k * P:(k + 1) * P],
                                                    ident[0:E, 0:E], start=True, stop=True, is_transpose=True)
                        last.then_inc(sem("gate_transposed"), 1)

                    @block.vector
                    def _(dve):
                        v = nc.vector
                        step = sem("setup_vector")
                        n = [0]

                        def then(ins):
                            ins.then_inc(step, 1)
                            n[0] += 1
                            dve.wait_ge(step, n[0])

                        for t_, value in ((ident, 0.0), (see_q, 0.0), (see_k, 0.0), (see_r, 0.0), (tri_f, 1.0), (head_rows, 1.0),
                                          (pair_rows, 1.0)):
                            v.memset(t_.ap(), value).then_inc(sem("blank"), 1)
                        v.memset(zero[:, :], 0.0).then_inc(sem("zero_set"), 1)
                        v.memset(blank_row[:, :], 0.0)
                        v.memset(ones_b[:, :], 1.0)
                        dve.wait_ge(sem("cond_exp"), 1)
                        then(v.tensor_scalar(c_e[:, :, :], c_e[:, :, :], 1.0, None, ALU.add))
                        then(v.reciprocal(c_e[:, :, :], c_e[:, :, :]))
                        v.tensor_tensor(c_t[:, :, :], c_t[:, :, :], c_e[:, :, :], ALU.mult).then_inc(sem("silu_ready"), 1)
                        dve.wait_ge(wv_in, 16 * 4)
                        for i in range(2):
                            v.tensor_tensor(gate_tmp[:, i, :, :], wq_f[:, :, :], bc(gates_f[:, i, :].unsqueeze(1), [P, KD, D]),
                                            ALU.mult).then_inc(step, 1)
                        n[0] += 2
                        dve.wait_ge(step, n[0])
                        for i in range(2):
                            v.tensor_reduce(wv_f[:, :, D + i * H:D + (i + 1) * H],
                                            gate_tmp[:, i, :, :].rearrange("p k (h d) -> p k h d", d=HD), AX_X, ALU.add
                                            ).then_inc(sem("gate_columns"), 1)
                        dve.wait_ge(sem("gate_columns"), 2)
                        for i, (f, hi, lo) in enumerate(((wq_f, wq_h, wq_l), (wv_f, wv_h, wv_l), (wk_f, wk_h, wk_l), (wg_f, wg_h, wg_l))):
                            dve.wait_ge(sem("weights_hi"), i + 1)
                            v.tensor_tensor(lo[:, :, :], f[:, :, :], hi[:, :, :].bitcast(F32), ALU.subtract)
                        dve.wait_ge(x_in.sem, x_in.at(0, 1))
                        norm_stats(dve, xin, 0, ln1_chain, var1_ready)
                        norm_apply(dve, xin, xin, 0, rstd1_ready, ln1_ready, 1)
                        dve.wait_ge(sem("shapes"), 14)
                        v.tensor_copy(ident_b[:, :], ident[:, :])
                        v.tensor_copy(tri[:, :], tri_f[:, :])
                        v.tensor_copy(iota_f[:, :], iota_i[:, :])
                        dve.wait_ge(sem("masks_spread"), 2)
                        v.memset(mask_q[0:64, 0, 0:W], BIG)
                        v.memset(mask_k[0:64, 0, :], BIG)
                        mod = modulation_of(ps[0])
                        dve.wait_ge(sem("mod_matmul"), 1)
                        v.tensor_copy(mod_t[:, :, 0, :], mod[:, 0])
                        v.tensor_scalar(mod_t[:, :, 1, :], mod[:, 1], 1.0, None, ALU.add)
                        dve.wait_ge(sem("gate_transposed"), 1)
                        v.tensor_copy(gate_t[:, :, :], ps[4][:, 0:KD * E].rearrange("p (k e) -> p k e", k=KD)).then_inc(step, 1)

            q_st = [s_[0:KS_ROWS + 3, :].rearrange("p (h s) -> p h s", h=H) for s_ in shared]
            k_st = [sb(f"k_stack{i}", [KS_ROWS + 3, H, W + S], BF16) for i in range(2)]
            v_al = [sb(f"v_aligned{i}", [P, NT, H, VW]) for i in range(2)]
            v_sh = [sb(f"v_shifted{i}", [P, NT, H, VW]) for i in range(2)]
            hT = sb("hT", [P, KD, S])
            hT_h, hT_l = sb("hT_h", [P, KD, S], F32R), sb("hT_l", [P, KD, S], F32R)
            hbar = sb("hbar", [P, KD, 2, NL])
            mod_b = sb("mod_b", [P, 2, KD])
            parts = [sb(f"parts{i}", [P, 3, S], BF16) for i in range(3)]
            rest = [sb(f"rest{i}", [P, S]) for i in range(2)]
            gates = [sb(f"gates{i}", [P, NT, 2 * H]) for i in range(2)]
            gq_t = [sb(f"gq_t{i}", [P, S]) for i in range(2)]
            gk_bd = [sb(f"gk_bd{i}", [P, LH, NL]) for i in range(2)]
            gv_bd = [sb(f"gv_bd{i}", [P, NP, 2, HD]) for i in range(2)]
            nmx = sb("nmx", [P, NT, H])
            nmx_r = sb("nmx_r", [P, NT, HH])
            mx_p = [sb(f"mx_parts{i}", [P, NT, P], BF16) for i in range(2)]
            mx_t = [sb(f"mx_t{i}", [P, S], BF16) for i in range(2)]
            NPT = 3
            p_t = [sb(f"p_t{i}", [P, S]) for i in range(NPT)]
            pv_s = sb("pv_s", [P, S])
            o = sb("o", [P, NT, D])
            fac = sb("fac", [P, 2, NT, 4])
            sr = sb("sr", [P, NT, LH, NL])
            rstat = sb("rstat", [P, 3, NT, LH])
            pr_t = sb("pr_t", [P, NP, S])
            rm = pr_t[:, 0:2, :].rearrange("p q s -> p (q s)").rearrange("p (t d) -> p t d", d=D)
            rem_t = sb("rem_t", [P, S])
            d_t = sb("d_t", [P, KD, S])
            rows = sb("rows", [P, NT, ROW])
            h2, x1 = rows[:, :, 0:D], rows[:, :, ROW_X:ROW_X + D]
            mod_bc = sb("mod_bc", [P, 3, D])
            turn = sb("turn", [1, 1])
            lg = sb("lg", [P, NT, E])
            lge = sb("lge", [P, NT, E])
            cand = sb("cand", [P, NT, E])
            loc_e = sb("loc_e", [P, NT, E])
            rt = sb("rt", [P, 8, NT])
            oh = sb("oh", [P, NT, E], BF16)
            seen = sb("seen", [P, NT + 1, E], BF16)
            slot_i = [sb(f"slot_i{i}", [P, NT], I32) for i in range(2)]

            S1 = [ps[0], ps[1]]
            S2 = [ps[2], ps[3]]
            PV = ps[4]
            RING = [ps[5], ps[6], ps[7]]

            modb_ready = sig("modb_ready", 1)
            hT_ready = sig("hT_ready", KD)
            hTh_ready = sig("hTh_ready", KD)
            hTl_ready = sig("hTl_ready", KD)
            hbar_ready = sig("hbar_ready", KD)
            p1_ready, p2_ready, p3_ready = sig("part1_ready", 4), sig("part2_ready", 4), sig("part3_ready", 4)
            rest_ready = sig("rest_ready", 4)
            PB, PBEFORE = (0, 1, 2, 0), (3, 1, 2, 0)
            parts_stored = [sig(f"parts_stored{m}", 1, 16) for m in range(4)]
            stack_in, max_in = sig("stack_in", 12, 16), sig("max_in", 6, 16)
            gq_ready, gk_ready = sig("gq_ready", 1), sig("gk_ready", 2)
            v_ready, v_shifted = sig("v_ready", NT), sig("v_shifted", 2, 16)
            gexp_ready = sig("gate_exp_ready", NT)
            gate_ready = sig("gate_ready", 1)
            s1_full, s1_free = sig("s1_full", 18), sig("s1_free", 18)
            mxp_ready = sig("max_parts_ready", 2)
            s2_full, exp_ready, pv_done = sig("s2_full", H), sig("exp_ready", H), sig("pv_done", H)
            pv_out = sig("pv_out", 4)
            lt_done = sig("local_done", 4)
            ring_full = sem("ring_full")
            rshift_ready, rexp_ready, rinv_ready = sig("r_shift_ready", NT), sig("r_exp_ready", NT), sig("r_inv_ready", NT)
            rprob_ready, prt_ready = sig("r_prob_ready", NT), sig("prt_ready", NT)
            remt_ready, rm_ready = sig("rem_t_ready", 1), sig("rm_ready", 2)
            o_ready, ot_ready = sig("o_ready", 2), sig("o_t_ready", 2)
            ao_ready, x1_ready, x1_stored = sig("attn_out_ready", 2), sig("x1_ready", 2), sig("x1_stored", 1, 16)
            xres_in, modbc_in = sig("x_again_in", 1, 16), sig("mod_bc_in", 1, 16)
            h2n_ready, h2_ready, h2t_ready = sig("h2_norm_ready", 2), sig("h2_ready", 2), sig("h2_t_ready", 2)
            lg_ready, lge_ready, oh_ready, slot_ready = sig("lg_ready", 1), sig("lg_exp_ready", 1), sig("onehot_ready", 1), sig("slot_ready", 1)
            scattered = sig("scattered", NT, 16)
            loc_ready = sig("loc_ready", 1)
            var2_ready, rstd2_ready = sig("var2_ready", 1), sig("rstd2_ready", 1)
            ones_set = sem("ones_rows_set")
            blanks, N_BLANKS = sem("buffers_blanked"), 12
            hbar_chain = sig("hbar_chain", KD)
            gate_chain, mx_chain = sig("gate_chain", 1), sig("max_chain", 8)
            r_chain, lt_chain = sig("r_chain", 2 * NT), sig("lt_chain", 8)
            rmax_chain = sig("r_max_chain", NT)
            ln2_chain, route_chain = sig("ln2_chain", 2 * NT + 1), sig("route_chain", 13)
            add_chain = sig("modulate_chain", 2)
            read_by = {"A.GQ": (gq_ready, 1), "A.GK": (gk_ready, 1), "A.GV": (gk_ready, 2), "C.RP": (remt_ready, 1),
                       "D.LG": (lg_ready, 1), "D.LOC": (loc_ready, 1)}
            for i in range(2):
                read_by.update({f"A.T{i}": (hT_ready, i + 1), f"A.Q{i}": (rest_ready, i + 1), f"A.K{i}": (rest_ready, i + 3),
                                f"C.RO{i}": (rm_ready, i + 1), f"D.OT{i}": (ot_ready, i + 1), f"D.WO{i}": (ao_ready, i + 1),
                                f"D.H{i}": (h2t_ready, i + 1)})
            for i in range(4):
                read_by.update({f"A.V{i}": (gexp_ready, i + 1), f"C.R{i}": (rshift_ready, i + 1),
                                f"C.PR{i}": (prt_ready, i + 1), f"L.LT{i}": (lt_done, i + 1)})

            def steps(run):
                run("pro", -1, 1)
                run("first", 0, 0)
                run("mid", 1, 1)
                with run.engine.Fori(0, (B - 4) // 2) as i:
                    run("mid", i * 2 + 2, 0)
                    run("mid", i * 2 + 3, 1)
                run("mid", B - 2, 0)
                run("last", B - 1, 1)
                run("epi", B, 0)

            class Run:

                def __init__(self, engine, jobs, head=None):
                    self.engine, self.jobs, self.head = engine, jobs, head

                def __call__(self, kind, s, c):
                    for slot in range(17):
                        if self.head is not None:
                            self.head(kind, s, c, slot)
                        for name in SLOT_JOBS[slot]:
                            if name not in ORDER[kind]:
                                continue
                            stage, what = name.split(".")
                            b, p = batch_of(name, s), c if stage in "CL" else 1 - c
                            fn = self.jobs.get(what.rstrip("0123456789"))
                            if fn is not None:
                                fn(Job(kind, s, name), b, p, int(what[-1]) if what[-1].isdigit() else 0)

            def seen_latents(t):
                return P // CH * (t + 1)

            def is0(b):
                return isinstance(b, int) and b == 0

            def norm_batch(kind, s, slot, at):
                if kind == "pro" and slot == 0:
                    return 0
                if slot == at and kind in ("pro", "first", "mid") and not (isinstance(s, int) and s + 2 >= B):
                    return s + 2
                return None

            def add_latent(eng, ns, b, j):
                eng.wait_ge(lt_done.sem, lt_done.at(b, 4))
                eng.wait_ge(rm_ready.sem, rm_ready.at(b, 2))
                ns.tensor_tensor(o[:, 2 * j:2 * j + 2, :], o[:, 2 * j:2 * j + 2, :], rm[:, 2 * j:2 * j + 2, :],
                                 ALU.add).then_inc(o_ready.sem, 1)

            def add_residual(eng, ns, b, j):
                eng.wait_ge(ao_ready.sem, ao_ready.at(b, j + 1))
                eng.wait_ge(xres_in.sem, xres_in.at(b, 1))
                ns.tensor_tensor(x1[:, 2 * j:2 * j + 2, :], x1[:, 2 * j:2 * j + 2, :], h2[:, 2 * j:2 * j + 2, :],
                                 ALU.add).then_inc(x1_ready.sem, 1)

            def modulate(eng, ns, b):
                for j in range(2):
                    eng.wait_ge(h2n_ready.sem, h2n_ready.at(b, j + 1))
                    h = h2[:, 2 * j:2 * j + 2, :]
                    ns.tensor_tensor(h, h, bc(mod_bc[:, 1:2, :], [P, 2, D]), ALU.mult).then_inc(add_chain.sem, 1)
                    eng.wait_ge(add_chain.sem, add_chain.at(b, j + 1))
                    ns.tensor_tensor(h, h, bc(mod_bc[:, 2:3, :], [P, 2, D]), ALU.add).then_inc(h2_ready.sem, 1)

            with nc.Block() as block:

                @block.tensor
                def _(pe):
                    mm = nc.tensor.matmul

                    def bank(job):
                        if job.before is not None:
                            name, b = job.before
                            last_read, k = read_by[name]
                            pe.wait_ge(last_read.sem, last_read.at(b, k))
                        return RING[job.bank]

                    def tr(dst, src, idn):
                        return mm(dst, src, idn, start=True, stop=True, is_transpose=True)

                    def mm3(dst, a, b_):
                        terms = [(a[i][k], b_[j][k]) for k in range(KD) for i, j in ((0, 0), (1, 0), (0, 1))]
                        for n, (l, r) in enumerate(terms):
                            last = mm(dst, l, r, start=(n == 0), stop=(n == len(terms) - 1))
                        return last

                    def job_T(job, b, p, k):
                        r = bank(job)
                        pe.wait_ge(ln1_ready.sem, ln1_ready.at(b, NT))
                        for t in range(NT):
                            last = tr(r[:, t * P:(t + 1) * P], xin[:, t, k * P:(k + 1) * P], ident[:, :])
                        last.then_inc(ring_full, 1)

                    def halves(hi, lo, c0, n):
                        return [[w[:, k, c0:c0 + n] for k in range(KD)] for w in (hi, lo)]

                    def proj(job, b, hi, lo, c0):
                        r = bank(job)
                        pe.wait_ge(hTl_ready.sem, hTl_ready.at(b, KD))
                        mm3(r[:, :], halves(hi, lo, c0, P), halves(hT_h, hT_l, 0, S)).then_inc(ring_full, 1)

                    def job_Q(job, b, p, m):
                        proj(job, b, wq_h, wq_l, m * P)

                    def job_K(job, b, p, m):
                        proj(job, b, wk_h, wk_l, m * P)

                    def job_GQ(job, b, p, m):
                        proj(job, b, wg_h, wg_l, 0)

                    def job_V(job, b, p, t):
                        r = bank(job)
                        mm3(r[:, 0:VG], halves(hT_h, hT_l, t * P, P), halves(wv_h, wv_l, 0, VG)).then_inc(ring_full, 1)

                    def job_GK(job, b, p, m):
                        r = bank(job)
                        pe.wait_ge(hbar_ready.sem, hbar_ready.at(b, KD))
                        for k in range(KD):
                            last = mm(r[:, 0:NL], wgk_s[:, k, :], hbar[:, k, 0, :], start=(k == 0), stop=(k == KD - 1))
                        last.then_inc(ring_full, 1)

                    def job_GV(job, b, p, m):
                        r = bank(job)
                        for k in range(KD):
                            last = mm(r[:, 0:LD], hbar[:, k, :, :], wgv_s[:, k, :], start=(k == 0), stop=(k == KD - 1))
                        last.then_inc(ring_full, 1)

                    def job_R(job, b, p, t):
                        r = bank(job)
                        pe.wait_ge(gq_ready.sem, gq_ready.at(b, 1))
                        pe.wait_ge(gk_ready.sem, gk_ready.at(b, 2))
                        n = seen_latents(t)
                        mm(r[:, 0:LH * n], ident_b[:, :], mask_r[:, t, :, 0:n], start=True, stop=False)
                        mm(r[:, 0:LH * n], gq_t[p][:, t * P:(t + 1) * P], gk_bd[p][:, :, 0:n], start=False, stop=True).then_inc(ring_full, 1)

                    def job_PR(job, b, p, t):
                        r = bank(job)
                        pe.wait_ge(rprob_ready.sem, rprob_ready.at(b, t + 1))
                        for q in range(NP):
                            last = tr(r[:, q * P:(q + 1) * P], sr[:, t, 2 * q:2 * q + 2, :], ident[:, :])
                        last.then_inc(ring_full, 1)

                    def job_RP(job, b, p, m):
                        r = bank(job)
                        pe.wait_ge(prt_ready.sem, prt_ready.at(b, NT))
                        for q in range(NP):
                            last = mm(r[32 * q:32 * q + 32, :], gv_bd[p][:, q, :, :], pr_t[:, q, :], start=True, stop=True)
                        last.then_inc(ring_full, 1)

                    def job_RO(job, b, p, j):
                        r = bank(job)
                        pe.wait_ge(remt_ready.sem, remt_ready.at(b, 1))
                        for i in range(2):
                            t = 2 * j + i
                            last = mm(r[:, i * D:(i + 1) * D], rem_t[:, t * P:(t + 1) * P], rout_s[:, :], start=True, stop=True)
                        last.then_inc(ring_full, 1)

                    def job_LT(job, b, p, g):
                        r = bank(job)
                        pe.wait_ge(pv_out.sem, pv_out.at(b, g + 1))
                        for t in range(NT):
                            last = tr(r[:, t * P:(t + 1) * P], pv_s[:, t * P:(t + 1) * P], ident[:, :])
                        last.then_inc(ring_full, 1)

                    def pair_tr(job, src, j):
                        r = bank(job)
                        for i in range(2):
                            for k in range(KD):
                                at = (i * KD + k) * P
                                last = tr(r[:, at:at + P], src[:, 2 * j + i, k * P:(k + 1) * P], ident[:, :])
                        last.then_inc(ring_full, 1)

                    def job_OT(job, b, p, j):
                        pe.wait_ge(o_ready.sem, o_ready.at(b, 2))
                        pair_tr(job, o, j)

                    def job_WO(job, b, p, j):
                        r = bank(job)
                        pe.wait_ge(ot_ready.sem, ot_ready.at(b, j + 1))
                        for i in range(2):
                            t = 2 * j + i
                            for k in range(KD):
                                last = mm(r[:, i * D:(i + 1) * D], d_t[:, k, t * P:(t + 1) * P], wout_s[:, k, :],
                                          start=(k == 0), stop=(k == KD - 1))
                        last.then_inc(ring_full, 1)

                    def job_H(job, b, p, j):
                        pe.wait_ge(h2_ready.sem, h2_ready.at(b, j + 1))
                        pair_tr(job, h2, j)

                    def job_LG(job, b, p, j):
                        r = bank(job)
                        pe.wait_ge(h2t_ready.sem, h2t_ready.at(b, 2))
                        for t in range(NT):
                            for k in range(KD):
                                last = mm(r[:, t * E:(t + 1) * E], d_t[:, k, t * P:(t + 1) * P], gate_t[:, k, :],
                                          start=(k == 0), stop=(k == KD - 1))
                        last.then_inc(ring_full, 1)

                    def job_LOC(job, b, p, j):
                        r = bank(job)
                        pe.wait_ge(oh_ready.sem, oh_ready.at(b, 1))
                        mm(r[:, 0:NT * E], tri[:, :], oh[:, :, :], start=True, stop=False)
                        mm(r[:, 0:NT * E], ones_b[:, :], seen[:, 0:NT, :], start=False, stop=True).then_inc(ring_full, 1)

                    def s1_bank(b, job):
                        n = S1_ORDER.index(job)
                        if not (is0(b) and n < 2):
                            pe.wait_ge(s1_free.sem, s1_free.at(b, n - 1))
                        return S1[n % 2]

                    def scores_q(b, p, h):
                        if h == 0:
                            pe.wait_ge(stack_in.sem, stack_in.at(b, 12))
                        r = s1_bank(b, h)
                        mm(r[:, :], ident_b[:, :], mask_q[:, :, :], start=True, stop=False, skip_group_check=True)
                        for w in range(NB):
                            t, a = divmod(w, 2)
                            last = mm(r[64 * a:64 * a + 64, t * P:(t + 1) * P], q_st[p][0:KS_ROWS, h, w * W:(w + 1) * W],
                                      k_st[p][0:KS_ROWS, h, w * W:w * W + 2 * W], start=False, stop=(w == NB - 1), skip_group_check=True)
                        last.then_inc(s1_full.sem, 1)

                    def max_rows(b, p, half):
                        pe.wait_ge(mxp_ready.sem, mxp_ready.at(b, half + 1))
                        r = s1_bank(b, f"M{half}")[:, 0:S // 2].bitcast(BF16)
                        for t in range(NT):
                            last = tr(r[:, t * P:(t + 1) * P], mx_p[half][:, t, :], ident_b[:, :])
                        last.then_inc(s1_full.sem, 1)

                    def s1_jobs(b, p, jobs):
                        for job in jobs:
                            if isinstance(job, int):
                                scores_q(b, p, job)
                            else:
                                max_rows(b, p, int(job[1]))

                    def scores_k(b, p, h):
                        half, n = divmod(h, HH)
                        if n == 0:
                            if is0(b):
                                pe.wait_ge(ones_set, 2)
                            pe.wait_ge(max_in.sem, max_in.at(b, 3 * half + 3))
                        if not (is0(b) and h < 2):
                            pe.wait_ge(exp_ready.sem, exp_ready.at(b, h - 1))
                        r = S2[h % 2]
                        mm(r[:, :], ident_b[:, :], mask_k[:, :, :], start=True, stop=False, skip_group_check=True)
                        for w in range(NB):
                            last = mm(r[:, w * W:(w + 1) * W], k_st[p][:, h, w * W:w * W + 2 * W],
                                      q_st[p][:, h, w * W:(w + 1) * W], start=False, stop=(w == NB - 1), skip_group_check=True)
                        last.then_inc(s2_full.sem, 1)

                    def weigh_values(b, p, h):
                        if h == 0:
                            pe.wait_ge(v_shifted.sem, v_shifted.at(b, 2))
                        if h % 4 == 0 and not (is0(b) and h == 0):
                            pe.wait_ge(pv_out.sem, pv_out.at(b, h // 4))
                        pe.wait_ge(exp_ready.sem, exp_ready.at(b, h + 1))
                        g = h % 4
                        for w in range(NB):
                            v = v_al[p][:, w // 2, h, :] if w % 2 else v_sh[p][:, w // 2, h, :]
                            last = mm(PV[32 * g:32 * g + VW, w * W:(w + 1) * W], v, p_t[h % NPT][:, w * W:(w + 1) * W],
                                      start=True, stop=True, skip_group_check=True)
                        last.then_inc(pv_done.sem, 1)

                    def head(kind, s, c, slot):
                        if kind == "first" and slot == 0:
                            pe.wait_ge(sem("mod_rows_ready"), 1)
                        if kind in ("first", "mid", "last"):
                            now, later = S1_NOW.get(slot, []), S1_NEXT.get(slot, []) if kind != "last" else []
                            s1_jobs(s, c, [j for j in now if isinstance(j, int)])
                            s1_jobs(s + 1, 1 - c, [j for j in later if isinstance(j, int)])
                            if slot < H:
                                scores_k(s, c, slot)
                            if slot >= 1:
                                weigh_values(s, c, slot - 1)
                            s1_jobs(s, c, [j for j in now if j == "M1"])
                            s1_jobs(s + 1, 1 - c, [j for j in later if j == "M0"])
                        elif kind == "pro" and slot == 4:
                            pe.wait_ge(wm_in[1], 16)
                            for chunk in range(4, 12):
                                last = modulation(S2[0], chunk)
                            last.then_inc(sem("mod_rest"), 1)
                        elif kind == "pro" and slot == 8:
                            pe.wait_ge(sem("mod_o_ready"), 3)
                            tr(S2[1][0:B * 4 * KD, 0:P], mod_o[:, :, :, :], ident[:, :]).then_inc(sem("mod_transposed"), 1)
                        elif kind == "pro" and slot == 16:
                            pe.wait_ge(blanks, N_BLANKS)
                            for at in range(17):
                                s1_jobs(0, 0, S1_NEXT.get(at, []))

                    steps(Run(pe, {"T": job_T, "Q": job_Q, "K": job_K, "GQ": job_GQ, "V": job_V, "GK": job_GK, "GV": job_GV,
                                   "R": job_R, "PR": job_PR, "RP": job_RP, "RO": job_RO, "LT": job_LT, "OT": job_OT,
                                   "WO": job_WO, "H": job_H, "LG": job_LG, "LOC": job_LOC}, head))

                @block.scalar
                def _(act):
                    def full(job):
                        act.wait_ge(ring_full, job.done)
                        return RING[job.bank]

                    def job_T(job, b, p, k):
                        r = full(job)
                        act.wait_ge(modb_ready.sem, modb_ready.at(b, 1))
                        if not is0(b):
                            act.wait_ge(hbar_ready.sem, hbar_ready.at(b - 1, KD))
                            act.wait_ge(hTl_ready.sem, hTl_ready.at(b - 1, KD))
                        nc.scalar.activation(hT[:, k, :], r[:, :], ACT.Identity, bias=mod_b[:, 0, k:k + 1],
                                             scale=mod_b[:, 1, k:k + 1]).then_inc(hT_ready.sem, 1)

                    def first_part(job, b, m, scale):
                        r = full(job)
                        if m == 3:
                            act.wait_ge(parts_stored[PBEFORE[m]].sem, parts_stored[PBEFORE[m]].at(b, 1))
                        elif not is0(b):
                            act.wait_ge(parts_stored[PBEFORE[m]].sem, parts_stored[PBEFORE[m]].at(b - 1, 1))
                        nc.scalar.activation(parts[PB[m]][:, 0, :], r[:, :], ACT.Copy, scale=scale).then_inc(p1_ready.sem, 1)

                    def job_Q(job, b, p, m):
                        first_part(job, b, m, HD ** -0.5)

                    def job_K(job, b, p, m):
                        first_part(job, b, 2 + m, 1.0)

                    def job_GQ(job, b, p, m):
                        r = full(job)
                        nc.scalar.activation(gq_t[p][:, :], r[:, :], ACT.Copy, scale=HD ** -0.5).then_inc(gq_ready.sem, 1)

                    def job_V(job, b, p, t):
                        r = full(job)
                        nc.scalar.activation(v_al[p][:, t, :, 0:HD], r[:, 0:D].rearrange("p (h d) -> p h d", d=HD),
                                             ACT.Copy).then_inc(v_ready.sem, 1)
                        nc.scalar.activation(gates[p][:, t, :], r[:, D:VG], ACT.Exp, scale=-1.0).then_inc(gexp_ready.sem, 1)

                    def latent_exp(b, t):
                        act.wait_ge(rshift_ready.sem, rshift_ready.at(b, t + 1))
                        e = sr[:, t, :, 0:seen_latents(t)]
                        nc.scalar.activation(e, e, ACT.Exp).then_inc(rexp_ready.sem, 1)

                    def job_PR(job, b, p, t):
                        r = full(job)
                        nc.scalar.activation(pr_t[:, :, t * P:(t + 1) * P], r[:, :].rearrange("p (q n) -> p q n", q=NP),
                                             ACT.Copy).then_inc(prt_ready.sem, 1)

                    def job_RP(job, b, p, m):
                        r = full(job)
                        nc.scalar.activation(rem_t[:, :], r[:, :], ACT.Copy).then_inc(remt_ready.sem, 1)

                    def pair_out(job, j, ready):
                        r = full(job)
                        nc.scalar.activation(d_t[:, :, 2 * j * P:(2 * j + 2) * P].rearrange("p k (t n) -> p t k n", t=2),
                                             r[:, :].rearrange("p (t k n) -> p t k n", t=2, k=KD), ACT.Copy).then_inc(ready.sem, 1)

                    def job_OT(job, b, p, j):
                        pair_out(job, j, ot_ready)

                    def job_H(job, b, p, j):
                        pair_out(job, j, h2t_ready)

                    def job_LG(job, b, p, j):
                        act.wait_ge(lg_ready.sem, lg_ready.at(b, 1))
                        nc.scalar.activation(lge[:, :, :], lg[:, :, :], ACT.Exp).then_inc(lge_ready.sem, 1)

                    def head(kind, s, c, slot):
                        if kind == "pro" and slot == 9:
                            act.wait_ge(sem("mod_transposed"), 1)
                            nc.scalar.activation(mod_rows[:, :], S2[1][0:B * 4 * KD, 0:P], ACT.Copy).then_inc(sem("mod_rows_ready"), 1)
                        if kind not in ("first", "mid", "last"):
                            return
                        if slot in (5, 9, 13, 16):
                            g = {5: 0, 9: 1, 13: 2, 16: 3}[slot]
                            act.wait_ge(pv_done.sem, pv_done.at(s, 4 * g + 4))
                            nc.scalar.activation(pv_s[:, :], PV[:, :], ACT.Copy).then_inc(pv_out.sem, 1)
                        if slot < H:
                            act.wait_ge(s2_full.sem, s2_full.at(s, slot + 1))
                            if not (is0(s) and slot < NPT):
                                act.wait_ge(pv_done.sem, pv_done.at(s, slot - NPT + 1))
                            nc.scalar.activation(p_t[slot % NPT][:, :], S2[slot % 2][:, :], ACT.Exp).then_inc(exp_ready.sem, 1)
                        if slot in R_EXP:
                            latent_exp(s, R_EXP[slot])

                    steps(Run(act, {"T": job_T, "Q": job_Q, "K": job_K, "GQ": job_GQ, "V": job_V, "PR": job_PR,
                                    "RP": job_RP, "OT": job_OT, "H": job_H, "LG": job_LG}, head))

                @block.vector
                def _(dve):
                    v = nc.vector

                    def chained(ins, chain, b, k):
                        ins.then_inc(chain.sem, 1)
                        dve.wait_ge(chain.sem, chain.at(b, k))

                    def full(job):
                        dve.wait_ge(ring_full, job.done)
                        return RING[job.bank]

                    def first_stats(b):
                        dve.wait_ge(x_in.sem, x_in.at(b, 1))
                        norm_stats(dve, xin, b, ln1_chain, var1_ready)

                    def first_norm(b):
                        if not is0(b):
                            norm_apply(dve, xin, xin, b, rstd1_ready, ln1_ready, 1)
                        if not is0(b):
                            dve.wait_ge(hT_ready.sem, hT_ready.at(b - 1, KD))
                        v.tensor_copy(mod_b[:, :, :], mod_t[:, b, :, :]).then_inc(modb_ready.sem, 1)

                    def job_T(job, b, p, k):
                        dve.wait_ge(hT_ready.sem, hT_ready.at(b, k + 1))
                        v.tensor_copy(hT_h[:, k, :], hT[:, k, :]).then_inc(hTh_ready.sem, 1)
                        dve.wait_ge(hTh_ready.sem, hTh_ready.at(b, k + 1))
                        v.tensor_tensor(hT_l[:, k, :], hT[:, k, :], hT_h[:, k, :].bitcast(F32), ALU.subtract).then_inc(hTl_ready.sem, 1)

                    def pool_tokens(b):
                        for k in range(KD):
                            chained(v.tensor_reduce(hbar[:, k, 0, :], hT[:, k, :].rearrange("p (n c) -> p n c", c=CH), AX_X, ALU.add),
                                    hbar_chain, b, k + 1)
                            v.tensor_copy(hbar[:, k, 1, :], hbar[:, k, 0, :]).then_inc(hbar_ready.sem, 1)

                    def part_rest(job, b, m, scale):
                        r = RING[job.bank]
                        dve.wait_ge(p1_ready.sem, p1_ready.at(b, m + 1))
                        if not (is0(b) and m < 2):
                            dve.wait_ge(p3_ready.sem, p3_ready.at(b, m - 1))
                        v.scalar_tensor_tensor(rest[m % 2][:, :], r[:, :], scale, parts[PB[m]][:, 0, :], ALU.mult,
                                               ALU.subtract).then_inc(rest_ready.sem, 1)
                        dve.wait_ge(rest_ready.sem, rest_ready.at(b, m + 1))
                        v.tensor_copy(parts[PB[m]][:, 1, :], rest[m % 2][:, :]).then_inc(p2_ready.sem, 1)

                    def job_Q(job, b, p, m):
                        part_rest(job, b, m, HD ** -0.5)

                    def job_K(job, b, p, m):
                        part_rest(job, b, 2 + m, 1.0)

                    def gate_quotients(b, p):
                        dve.wait_ge(gexp_ready.sem, gexp_ready.at(b, NT))
                        chained(v.tensor_scalar(gates[p][:, :, :], gates[p][:, :, :], 1.0, None, ALU.add), gate_chain, b, 1)
                        v.reciprocal(gates[p][:, :, :], gates[p][:, :, :]).then_inc(gate_ready.sem, 1)

                    def job_GK(job, b, p, m):
                        r = full(job)
                        v.scalar_tensor_tensor(gk_bd[p][:, :, :], bc(r[:, 0:NL].unsqueeze(1), [P, LH, NL]), 1.0 / CH,
                                               bc(head_rows[:, :].unsqueeze(2), [P, LH, NL]), ALU.mult, ALU.mult).then_inc(gk_ready.sem, 1)

                    def job_GV(job, b, p, m):
                        r = full(job)
                        v.scalar_tensor_tensor(gv_bd[p][:, :, :, :], r[:, 0:LD].rearrange("p (q e d) -> p q e d", q=NP, e=2), 1.0 / CH,
                                               pair_rows[:, :, :, :], ALU.mult, ALU.mult).then_inc(gk_ready.sem, 1)

                    def job_R(job, b, p, t):
                        r = full(job)
                        n = seen_latents(t)
                        r3 = r[:, 0:LH * n].rearrange("p (h n) -> p h n", h=LH)
                        chained(v.tensor_reduce(rstat[:, 0, t, :], r3, AX_X, ALU.max, negate=True), rmax_chain, b, t + 1)
                        v.tensor_tensor(sr[:, t, :, 0:n], r3, bc(rstat[:, 0, t, :].unsqueeze(2), [P, LH, n]),
                                        ALU.add).then_inc(rshift_ready.sem, 1)

                    def latent_sum(b, t):
                        dve.wait_ge(rexp_ready.sem, rexp_ready.at(b, t + 1))
                        chained(v.tensor_reduce(rstat[:, 1, t, :], sr[:, t, :, 0:seen_latents(t)], AX_X, ALU.add), r_chain, b, 2 * t + 1)
                        chained(v.reciprocal(rstat[:, 2, t, :], rstat[:, 1, t, :]), r_chain, b, 2 * t + 2)
                        v.tensor_copy(rstat[:, 1, t, :], rstat[:, 2, t, :]).then_inc(rinv_ready.sem, 1)

                    def job_RO(job, b, p, j):
                        r = full(job)
                        dve.wait_ge(gate_ready.sem, gate_ready.at(b, 1))
                        if not is0(b):
                            dve.wait_ge(o_ready.sem, o_ready.at(b - 1, 2))
                        v.tensor_tensor(rm[:, 2 * j:2 * j + 2, :].rearrange("p t (h d) -> p t h d", d=HD),
                                        r[:, :].rearrange("p (t h d) -> p t h d", t=2, d=HD),
                                        bc(gates[p][:, 2 * j:2 * j + 2, H:2 * H].unsqueeze(3), [P, 2, H, HD]),
                                        ALU.mult).then_inc(rm_ready.sem, 1)

                    def job_LT(job, b, p, g):
                        r = full(job)
                        r4 = r[:, :].rearrange("p (t h d) -> p t h d", t=NT, d=32)
                        dve.wait_ge(gate_ready.sem, gate_ready.at(b, 1))
                        chained(v.reciprocal(fac[:, 0, :, :], r4[:, :, :, HD]), lt_chain, b, 2 * g + 1)
                        chained(v.tensor_tensor(fac[:, 1, :, :], fac[:, 0, :, :], gates[p][:, :, 4 * g:4 * g + 4], ALU.mult),
                                lt_chain, b, 2 * g + 2)
                        v.tensor_tensor(o[:, :, g * 64:g * 64 + 64].rearrange("p t (h d) -> p t h d", d=HD), r4[:, :, :, 0:HD],
                                        bc(fac[:, 1, :, :].unsqueeze(3), [P, NT, 4, HD]), ALU.mult).then_inc(lt_done.sem, 1)

                    def job_WO(job, b, p, j):
                        r = full(job)
                        dve.wait_ge(modbc_in.sem, modbc_in.at(b, 1))
                        if not is0(b):
                            dve.wait_ge(scattered.sem, scattered.at(b - 1, NT))
                        v.tensor_tensor(h2[:, 2 * j:2 * j + 2, :], r[:, :].rearrange("p (t d) -> p t d", t=2),
                                        bc(mod_bc[:, 0:1, :], [P, 2, D]), ALU.mult).then_inc(ao_ready.sem, 1)
                        if job.kind == "epi":
                            add_residual(dve, v, b, j)

                    def second_stats(b):
                        dve.wait_ge(x1_ready.sem, x1_ready.at(b, 2))
                        norm_stats(dve, x1, b, ln2_chain, var2_ready)

                    def second_norm(b):
                        norm_apply(dve, x1, h2, b, rstd2_ready, h2n_ready, 2)

                    def job_LG(job, b, p, j):
                        r = full(job)
                        r3 = r[:, 0:NT * E].rearrange("p (t e) -> p t e", e=E)
                        chained(v.tensor_reduce(rt[:, 0, :], r3, AX_X, ALU.max), route_chain, b, 1)
                        v.tensor_tensor(lg[:, :, :], r3, bc(rt[:, 0, :].unsqueeze(2), [P, NT, E]), ALU.subtract).then_inc(lg_ready.sem, 1)
                        dve.wait_ge(lg_ready.sem, lg_ready.at(b, 1))
                        chained(v.tensor_scalar(cand[:, :, :], lg[:, :, :], 0.0, -float(E), ALU.is_ge, ALU.mult), route_chain, b, 2)
                        chained(v.tensor_tensor(cand[:, :, :], cand[:, :, :], bc(iota_f[:, :].unsqueeze(1), [P, NT, E]), ALU.add),
                                route_chain, b, 3)
                        chained(v.tensor_reduce(rt[:, 1, :], cand[:, :, :], AX_X, ALU.min), route_chain, b, 4)
                        chained(v.tensor_tensor(oh[:, :, :], cand[:, :, :], bc(rt[:, 1, :].unsqueeze(2), [P, NT, E]), ALU.is_equal),
                                route_chain, b, 5)
                        if not is0(b):
                            chained(v.tensor_copy(seen[:, 0, :], seen[:, NT, :]), route_chain, b, 6)
                        else:
                            chained(v.memset(seen[:, 0, :], 0.0), route_chain, b, 6)
                        for t in range(NT):
                            last = v.tensor_tensor(seen[:, t + 1, :], seen[:, t, :], oh[:, t, :], ALU.add)
                            if t < NT - 1:
                                chained(last, route_chain, b, 7 + t)
                            else:
                                last.then_inc(oh_ready.sem, 1)
                        dve.wait_ge(lge_ready.sem, lge_ready.at(b, 1))
                        chained(v.tensor_reduce(rt[:, 2, :], lge[:, :, :], AX_X, ALU.add), route_chain, b, 10)
                        v.reciprocal(rows[:, :, ROW_P], rt[:, 2, :])
                        v.tensor_scalar(rows[:, :, ROW_T], rows[:, :, ROW_T], float(S), None, ALU.add)
                        v.tensor_scalar(rows[:, :, ROW_G], rows[:, :, ROW_G], 4.0, None, ALU.add)

                    def job_LOC(job, b, p, j):
                        r = full(job)
                        v.tensor_tensor(loc_e[:, :, :], r[:, 0:NT * E].rearrange("p (t e) -> p t e", e=E), oh[:, :, :],
                                        ALU.mult).then_inc(loc_ready.sem, 1)
                        dve.wait_ge(loc_ready.sem, loc_ready.at(b, 1))
                        chained(v.tensor_reduce(rt[:, 3, :], loc_e[:, :, :], AX_X, ALU.add), route_chain, b, 11)
                        v.tensor_scalar(rt[:, 4, :], rt[:, 3, :], float(CAP), None, ALU.is_le)
                        chained(v.scalar_tensor_tensor(rt[:, 5, :], rt[:, 1, :], float(CAP), rt[:, 3, :], ALU.mult, ALU.add),
                                route_chain, b, 12)
                        chained(v.scalar_tensor_tensor(rt[:, 6, :], rt[:, 5, :], -1.0, rt[:, 4, :], ALU.add, ALU.mult), route_chain, b, 13)
                        v.tensor_scalar(slot_i[p][:, :], rt[:, 6, :], float(SLOTS), None, ALU.add).then_inc(slot_ready.sem, 1)

                    def take_max(b, h):
                        n = S1_ORDER.index(h)
                        dve.wait_ge(s1_full.sem, s1_full.at(b, n + 1))
                        v.tensor_reduce(nmx[:, :, h], S1[n % 2][:, :].rearrange("p (t j) -> p t j", t=NT),
                                        AX_X, ALU.max, negate=True).then_inc(s1_free.sem, 1)

                    def max_parts(b, half):
                        dve.wait_ge(s1_free.sem, s1_free.at(b, S1_ORDER.index(half * HH + HH - 1) + 1))
                        m = nmx[:, :, half * HH:(half + 1) * HH]
                        pt = [mx_p[half][:, :, j * HH:(j + 1) * HH] for j in range(3)]
                        k = 4 * half
                        chained(v.tensor_copy(pt[0], m), mx_chain, b, k + 1)
                        chained(v.tensor_tensor(nmx_r[:, :, :], m, pt[0], ALU.subtract), mx_chain, b, k + 2)
                        chained(v.tensor_copy(pt[1], nmx_r[:, :, :]), mx_chain, b, k + 3)
                        chained(v.tensor_tensor(nmx_r[:, :, :], nmx_r[:, :, :], pt[1], ALU.subtract), mx_chain, b, k + 4)
                        v.tensor_copy(pt[2], nmx_r[:, :, :]).then_inc(mxp_ready.sem, 1)

                    def max_rows_out(b, half):
                        n = S1_ORDER.index(f"M{half}")
                        dve.wait_ge(s1_full.sem, s1_full.at(b, n + 1))
                        v.tensor_copy(mx_t[half][:, :], S1[n % 2][:, 0:S // 2].bitcast(BF16)).then_inc(s1_free.sem, 1)

                    def mod_gates():
                        dve.wait_ge(sem("mod_rest"), 1)
                        mod = modulation_of(S2[0])
                        done = sem("mod_steps")
                        for i, (src, dst) in enumerate(((2, 0), (5, 3))):
                            g = mod_o[:, :, dst, :]
                            sign = mod_s[:, :, i, :]
                            v.tensor_scalar(sign, mod[:, src], 0.0, 2.0, ALU.is_ge, ALU.mult).then_inc(done, 1)
                            dve.wait_ge(done, 4 * i + 1)
                            v.tensor_scalar(sign, sign, 1.0, None, ALU.subtract).then_inc(done, 1)
                            dve.wait_ge(done, 4 * i + 2)
                            v.tensor_tensor(g, mod[:, src], sign, ALU.mult).then_inc(done, 1)
                            dve.wait_ge(done, 4 * i + 3)
                            v.tensor_scalar(g, g, 0.25, None, ALU.max).then_inc(done, 1)
                            dve.wait_ge(done, 4 * i + 4)
                            v.tensor_tensor(g, g, sign, ALU.mult).then_inc(sem("mod_o_ready"), 1)
                        v.tensor_scalar(mod_o[:, :, 1, :], mod[:, 4], 1.0, None, ALU.add)
                        v.tensor_copy(mod_o[:, :, 2, :], mod[:, 3]).then_inc(sem("mod_o_ready"), 1)

                    def set_blanks():
                        for i in range(2):
                            v.memset(k_st[i][0:KS_ROWS, :, 0:W], 0.0).then_inc(blanks, 1)
                            v.memset(v_al[i][:, :, :, HD:VW], 1.0).then_inc(blanks, 1)
                            v.memset(v_sh[i][0:64, 0, :, :], 0.0).then_inc(blanks, 1)
                            v.memset(mx_p[i][:, :, :], 0.0).then_inc(blanks, 1)
                        v.memset(PV[:, :], 0.0).then_inc(blanks, 3)
                        v.memset(sr[:, :, :, :], 0.0).then_inc(blanks, 1)
                        v.tensor_copy(rows[:, :, ROW_T], token_i[:, :])
                        v.memset(rows[:, :, ROW_G], -1.0)

                    def s1_jobs(b, jobs):
                        for job in jobs:
                            if isinstance(job, int):
                                take_max(b, job)
                            else:
                                max_rows_out(b, int(job[1]))

                    def head(kind, s, c, slot):
                        if slot == 0 and kind in ("mid", "last", "epi"):
                            add_latent(dve, v, s - 1, 0)
                        if slot == GATES and kind in ("pro", "first", "mid"):
                            gate_quotients(s + 1, 1 - c)
                        if kind in ("first", "mid", "last"):
                            s1_jobs(s, S1_NOW.get(slot, []))
                            if S1_PARTS.get(slot) == 1:
                                max_parts(s, 1)
                            if kind != "last":
                                s1_jobs(s + 1, S1_NEXT.get(slot, []))
                                if S1_PARTS.get(slot) == 0:
                                    max_parts(s + 1, 0)
                            if slot in R_SUM:
                                latent_sum(s, R_SUM[slot])
                        elif kind == "pro" and slot == 16:
                            for at in range(17):
                                s1_jobs(0, S1_NEXT.get(at, []))
                                if S1_PARTS.get(at) == 0:
                                    max_parts(0, 0)
                        if kind == "pro" and slot == 8:
                            set_blanks()
                        if kind == "pro" and slot == 5:
                            mod_gates()
                        if kind in ("pro", "first", "mid") and slot == HBAR:
                            pool_tokens(s + 1)
                        b = norm_batch(kind, s, slot, NORM1)
                        if b is not None and not is0(b):
                            first_stats(b)
                        b = norm_batch(kind, s, slot, NORM1 + 1)
                        if b is not None:
                            first_norm(b)
                        if kind in ("mid", "last", "epi"):
                            if slot == NORM2:
                                second_stats(s - 1)
                            if slot == NORM2 + 1:
                                second_norm(s - 1)
                                if kind == "epi":
                                    modulate(dve, v, s - 1)

                    steps(Run(dve, {"T": job_T, "Q": job_Q, "K": job_K, "GK": job_GK, "GV": job_GV, "R": job_R,
                                    "RO": job_RO, "LT": job_LT, "WO": job_WO, "LG": job_LG, "LOC": job_LOC}, head))

                @block.gpsimd
                def _(pool):
                    g = nc.gpsimd

                    def third_part(b, m):
                        pool.wait_ge(p2_ready.sem, p2_ready.at(b, m + 1))
                        g.tensor_tensor(parts[PB[m]][:, 2, :], rest[m % 2][:, :], parts[PB[m]][:, 1, :],
                                        ALU.subtract).then_inc(p3_ready.sem, 1)

                    def job_Q(job, b, p, m):
                        third_part(b, m)

                    def job_K(job, b, p, m):
                        third_part(b, 2 + m)

                    def latent_prob(b, t):
                        pool.wait_ge(rinv_ready.sem, rinv_ready.at(b, t + 1))
                        n = seen_latents(t)
                        g.tensor_tensor(sr[:, t, :, 0:n], sr[:, t, :, 0:n], bc(rstat[:, 1, t, :].unsqueeze(2), [P, LH, n]),
                                        ALU.mult).then_inc(rprob_ready.sem, 1)

                    def job_WO(job, b, p, j):
                        if job.kind != "epi":
                            add_residual(pool, g, b, j)

                    def job_LOC(job, b, p, j):
                        pool.wait_ge(slot_ready.sem, slot_ready.at(b, 1))
                        pool.wait_ge(h2_ready.sem, h2_ready.at(b, 2))
                        pool.wait_ge(slots_zeroed, 16 * N_ZERO)
                        g.tensor_tensor(turn[:, :], blank_row[:, :], blank_row[:, :], ALU.add)
                        for t in range(NT):
                            g.indirect_dma_start(xs_d, bass.IndirectOffsetOnAxis(slot_i[p][:, t:t + 1], 0), rows[:, t, :], None,
                                                 bounds_check=SLOTS - 1, oob_is_err=False).then_inc(scattered.sem, 16)

                    def head(kind, s, c, slot):
                        if kind == "pro" and slot == 1:
                            ones_rows(0)
                        if kind == "pro" and slot == 16:
                            pool.wait_ge(p3_ready.sem, p3_ready.at(0, 4))
                            pool.wait_ge(rstd1_ready.sem, rstd1_ready.at(1, 1))
                            ones_rows(1)
                        if slot == 0 and kind in ("mid", "last", "epi"):
                            add_latent(pool, g, s - 1, 1)
                        b = norm_batch(kind, s, slot, NORM1)
                        if b is not None and not is0(b):
                            inverse_deviation(pool, b, var1_ready, rstd1_ready)
                        if slot in R_SUM and kind in ("first", "mid", "last"):
                            latent_prob(s, R_SUM[slot])
                        if slot == NORM2 and kind in ("mid", "last", "epi"):
                            inverse_deviation(pool, s - 1, var2_ready, rstd2_ready)
                            if kind != "epi":
                                modulate(pool, g, s - 1)

                    def ones_rows(i):
                        g.memset(k_st[i][KS_ROWS:KS_ROWS + 3, :, :], 1.0).then_inc(ones_set, 1)
                        pool.wait_ge(ones_set, i + 1)


                    steps(Run(pool, {"Q": job_Q, "K": job_K, "WO": job_WO, "LOC": job_LOC}, head))
                    pool.wait_ge(scattered.sem, scattered.at(B - 1, NT))

                @block.sync
                def _(sp):
                    xv = x.rearrange("b (t p) d -> b p t d", p=P)

                    def max_beside_q(b, p, half):
                        sp.wait_ge(s1_free.sem, s1_free.at(b, S1_ORDER.index(f"M{half}") + 1))
                        for j in range(3):
                            sp.dma_start(q_st[p][KS_ROWS + j:KS_ROWS + j + 1, half * HH:(half + 1) * HH, :],
                                         mx_t[half][j * HH:(j + 1) * HH, :]).then_inc(max_in.sem, 16)

                    def head(kind, s, c, slot):
                        if kind == "last" and slot == 4:
                            max_beside_q(s, c, 1)
                        if (kind, slot) in (("last", 8), ("epi", 1)):
                            sp.wait_ge(s2_full.sem, s2_full.at(s - 1, H))
                            load_w1(sp, s - (B - 1), s - (B - 1))
                            load_w2(sp, s - (B - 1), s - (B - 1))
                        if kind in ("pro", "first", "mid") and slot == 16:
                            max_beside_q(s + 1, 1 - c, 0)
                        b = norm_batch(kind, s, slot, 1)
                        if b is not None:
                            if not is0(b):
                                sp.wait_ge(hT_ready.sem, hT_ready.at(b - 1, KD))
                                sp.dma_start(xin[:, :, :], xv[b]).then_inc(x_in.sem, 16)
                        if kind in ("pro", "first", "mid"):
                            b, p = s + 1, 1 - c
                            if slot == 4:
                                for m in range(4):
                                    if m == 3 and kind != "pro":
                                        max_beside_q(s, c, 1)
                                    sp.wait_ge(p3_ready.sem, p3_ready.at(b, m + 1))
                                    sp.dma_start(qk_d[p, m // 2, :, (m % 2) * P:(m % 2 + 1) * P, :].rearrange("j r n -> r j n"),
                                                 parts[PB[m]][:, :, :]).then_inc(parts_stored[m].sem, 16)
                                for kq, (dst, off, slots) in enumerate(((q_st[p], 0, QPART), (k_st[p], W, KPART))):
                                    for m in (2 * kq, 2 * kq + 1):
                                        sp.wait_ge(parts_stored[m].sem, parts_stored[m].at(b, 1))
                                    for n, part in enumerate(slots):
                                        sp.dma_start(dst[16 * n:16 * n + 16, :, off:off + S],
                                                     qk_d[p, kq, part, :, :].rearrange("(h r) n -> r h n", r=HD)).then_inc(stack_in.sem, 16)
                            if slot == 8:
                                sp.wait_ge(blanks, N_BLANKS)
                                sp.wait_ge(v_ready.sem, v_ready.at(b, NT))
                                sp.dma_start(v_sh[p][64:128, :, :, :], v_al[p][0:64, :, :, :]).then_inc(v_shifted.sem, 16)
                                sp.dma_start(v_sh[p][0:64, 1:NT, :, :], v_al[p][64:128, 0:NT - 1, :, :]).then_inc(v_shifted.sem, 16)
                                if kind == "pro":
                                    sp.wait_ge(sem("mod_rows_ready"), 1)
                                    sp.dma_start(mod_d.rearrange("b r (h d) -> (b r h) d", h=KD), mod_rows[:, :]).then_inc(sem("mod_stored"), 16)
                                if kind in ("pro", "first"):
                                    zero_slots(sp, range(3, 6) if kind == "pro" else range(6, N_ZERO))
                        if kind in ("mid", "last", "epi"):
                            b, p = s - 1, 1 - c
                            if slot == 0:
                                if not is0(b):
                                    sp.wait_ge(x1_stored.sem, x1_stored.at(b - 1, 1))
                                    sp.wait_ge(scattered.sem, scattered.at(b - 1, NT))
                                sp.dma_start(x1[:, :, :], xv[b]).then_inc(xres_in.sem, 16)
                                if is0(b):
                                    sp.wait_ge(sem("mod_stored"), 16)
                                sp.dma_start(mod_bc[:, :, :], mod_d[b, 0:3, :].unsqueeze(0).to_broadcast([P, 3, D])).then_inc(modbc_in.sem, 16)
                            if slot == 6:
                                sp.wait_ge(x1_ready.sem, x1_ready.at(b, 2))
                                sp.dma_start(out.rearrange("b (t p) d -> b p t d", p=P)[b], x1[:, :, :]).then_inc(x1_stored.sem, 16)

                    steps(Run(sp, {}, head))
                    sp.wait_ge(x1_stored.sem, x1_stored.at(B - 1, 1))

        ffn = ExitStack()
        with ffn:
            def fb(name, shape, dt=F32):
                return alloc(ffn, name, shape, dt)

            w1_h, w1_l = ([fb(f"w1_{part}{i}", [P, KD, HID], F32R) for i in range(2)] for part in "hl")
            w2_h, w2_l = ([fb(f"w2_{part}{i}", [P, MH, D], F32R) for i in range(2)] for part in "hl")
            xg = [fb(f"xg{i}", [P, 3, D]) for i in range(2)]
            xt_h, xt_l = fb("xt_h", [P, KD, CAP], F32R), fb("xt_l", [P, KD, CAP], F32R)
            h_h, h_l = fb("h_h", [P, MH, CAP], F32R), fb("h_l", [P, MH, CAP], F32R)
            y_t = fb("y_t", [P, KD, CAP])
            res = [fb(f"residual{i}", [P, 3, ROW - D]) for i in range(2)]
            token = [fb(f"token{i}", [P, 3], I32) for i in range(2)]
            gate_row = [fb(f"gate_row{i}", [P, 3], I32) for i in range(2)]
            gb = [fb(f"gb{i}", [P, 3, D]) for i in range(2)]
            y_s = fb("y_s", [P, 3, D])
            turn2 = fb("turn2", [1, 6])
            SR = [P, P, CAP - 2 * P]
            XT = [ps[0], ps[1]]
            YA = [ps[2], ps[3]]
            YT = ps[4]
            UP = [ps[5], ps[6], ps[7]]
            NU = len(UP)
            LASTROWS = UP[5 % NU]

            def esig(name, per, by=1):
                return Signal(sem(name), per, by)

            xg_in = [esig(f"xg_in{i}", 3, 16) for i in range(2)]
            w1h_ready, w1_split = esig("w1_hi", KD), esig("w1_split", KD)
            w2h_ready, w2_split = esig("w2_hi", 4), esig("w2_split", 4)
            xt_full, xth_ready, xt_split = esig("xt_full", 1), esig("xt_hi", KD), esig("xt_split", KD)
            up_full, hh_ready, h_split = esig("up_full", MH), esig("h_hi", MH), esig("h_split", MH)
            down_full, yt_ready = esig("down_full", KD), esig("y_t_ready", KD)
            ytr_full, y_weighed, y_added = esig("y_rows_full", 1), esig("y_weighed", 3), esig("y_added", 2)
            res_in, gb_in = ([esig(f"{name}{i}", per, 16) for i in range(2)] for name, per in (("residual_in", 3), ("gb_in", 3)))
            index_ready, y_out = esig("index_ready", 2), esig("y_out", 3, 16)
            xs_e = xs_d.rearrange("(e s) d -> e s d", e=E)

            def expert_steps(eng, run):
                run("first", 0, 0, 0)
                run("mid", 0, 1, 1)
                with eng.Fori(0, (E - 4) // 2) as i:
                    run("mid", i + 1, 0, i * 2 + 2)
                    run("mid", i + 1, 1, i * 2 + 3)
                run("noload", E // 2 - 1, 0, E - 2)
                run("last", E // 2 - 1, 1, E - 1)

            with nc.Block() as block:
                @block.sync
                def _(sp):
                    def rows_in(e, dst, cols, sig_):
                        sp.dma_start(dst[:, 0:2, :], xs_e[e, 0:2 * P, cols].rearrange("(s p) d -> p s d", p=P)).then_inc(sig_.sem, 16)
                        sp.dma_start(dst[0:SR[2], 2, :], xs_e[e, 2 * P:CAP, cols]).then_inc(sig_.sem, 32)

                    def load_res(e, p):
                        rows_in(e, res[p], slice(D, ROW), res_in[p])

                    def load(e, p):
                        rows_in(e, xg[p], slice(0, D), xg_in[p])
                        load_w1(sp, e, p)

                    for e in range(2):
                        rows_in(e, xg[e], slice(0, D), xg_in[e])
                    for e in range(2):
                        load_res(e, e)

                    def run(kind, j, p, e):
                        if kind in ("first", "mid"):
                            sp.wait_ge(xt_split.sem, xt_split.at(e, KD))
                            sp.wait_ge(w1_split.sem, w1_split.at(e, KD))
                            load(e + 2, p)
                            sp.wait_ge(w2_split.sem, w2_split.at(e, 4))
                            load_w2(sp, e + 2, p)

                        if kind in ("mid", "noload"):
                            sp.wait_ge(y_out.sem, y_out.at(e - 1, 3))
                            load_res(e + 1, 1 - p)

                    expert_steps(sp, run)

                @block.tensor
                def _(pe):
                    mm = nc.tensor.matmul

                    def transpose_rows(j, p, e):
                        pe.wait_ge(xg_in[p].sem, xg_in[p].at(j, 3))
                        if not (isinstance(e, int) and e == 0):
                            pe.wait_ge(xt_split.sem, xt_split.at(e - 1, KD))
                        for k in range(KD):
                            for i, (s0, n) in enumerate(ST):
                                last = mm(XT[k][:, s0:s0 + n], xg[p][0:n, i, k * P:(k + 1) * P], ident[0:n, 0:n],
                                          start=True, stop=True, is_transpose=True)
                        last.then_inc(xt_full.sem, 1)

                    def mm3(dst, terms):
                        for n, (l, r) in enumerate(terms):
                            last = mm(dst, l, r, start=(n == 0), stop=(n == len(terms) - 1))
                        return last

                    def rows_out(e, free_from, up_jobs):
                        pe.wait_ge(h_split.sem, h_split.at(free_from, up_jobs))
                        pe.wait_ge(yt_ready.sem, yt_ready.at(e, KD))
                        if not (isinstance(e, int) and e == 0):
                            pe.wait_ge(y_weighed.sem, y_weighed.at(e - 1, 3))
                        for k in range(KD):
                            for i in range(2):
                                mm(YT[:, i * D + k * P:i * D + (k + 1) * P], y_t[:, k, i * P:(i + 1) * P], ident[:, :],
                                   start=True, stop=True, is_transpose=True)
                            last = mm(LASTROWS[0:64, k * P:(k + 1) * P], y_t[:, k, 2 * P:CAP], ident[:, :], start=True, stop=True, is_transpose=True)
                        last.then_inc(ytr_full.sem, 1)

                    def run(kind, j, p, e):
                        pe.wait_ge(xt_split.sem, xt_split.at(e, KD))
                        for m in range(MH):
                            if m == 0:
                                pe.wait_ge(w1_split.sem, w1_split.at(e, KD))
                            if not (kind == "first" and m < NU):
                                pe.wait_ge(h_split.sem, h_split.at(e, m - NU + 1 if m >= NU else min(m - 1, 0)))
                            if m == 5 % NU and kind != "first" and not (isinstance(e, int) and e < 2):
                                pe.wait_ge(y_weighed.sem, y_weighed.at(e - 2, 3))
                            c = slice(m * P, (m + 1) * P)
                            terms = [(w[p][:, k, c], x_[:, k, :]) for k in range(KD) for w, x_ in ((w1_h, xt_h), (w1_l, xt_h), (w1_h, xt_l))]
                            mm3(UP[m % NU][:, 0:CAP], terms).then_inc(up_full.sem, 1)
                        if kind != "first":
                            rows_out(e - 1, e, 6)
                        if kind != "last":
                            transpose_rows(j + p, 1 - p, e + 1)
                        for k in range(KD):
                            if k == 0:
                                pe.wait_ge(w2_split.sem, w2_split.at(e, 4))
                                pe.wait_ge(h_split.sem, h_split.at(e, MH))
                            if kind != "first":
                                pe.wait_ge(yt_ready.sem, yt_ready.at(e - 1, k + 1))
                            c = slice(k * P, (k + 1) * P)
                            terms = [(w[p][:, m, c], h_[:, m, :]) for m in range(MH) for w, h_ in ((w2_h, h_h), (w2_l, h_h), (w2_h, h_l))]
                            mm3(YA[k][:, 0:CAP], terms).then_inc(down_full.sem, 1)

                    transpose_rows(0, 0, 0)
                    expert_steps(pe, run)
                    rows_out(E - 1, E - 1, MH)

                @block.scalar
                def _(act):
                    def split_rows(e):
                        act.wait_ge(xt_full.sem, xt_full.at(e, 1))
                        if not (isinstance(e, int) and e == 0):
                            act.wait_ge(up_full.sem, up_full.at(e - 1, MH))
                        for k in range(KD):
                            nc.scalar.activation(xt_h[:, k, :], XT[k][:, 0:CAP], ACT.Copy).then_inc(xth_ready.sem, 1)

                    def split_w1(j, p, e, k):
                        if k == 0:
                            act.wait_ge(w1_in[p].sem, w1_in[p].at(j, 1))
                            if not (isinstance(e, int) and e < 2):
                                act.wait_ge(up_full.sem, up_full.at(e - 2, MH))
                        nc.scalar.activation(w1_h[p][:, k, :], w1_f[p][:, k, :], ACT.Copy).then_inc(w1h_ready.sem, 1)

                    def split_w2(j, p, e):
                        act.wait_ge(w2_in[p].sem, w2_in[p].at(j, 1))
                        if not (isinstance(e, int) and e < 2):
                            act.wait_ge(down_full.sem, down_full.at(e - 2, KD))
                        for i in range(4):
                            c = slice(2 * i, 2 * i + 2)
                            nc.scalar.activation(w2_h[p][:, c, :], w2_f[p][:, c, :], ACT.Copy).then_inc(w2h_ready.sem, 1)

                    def run(kind, j, p, e):
                        if kind != "first":
                            act.wait_ge(down_full.sem, down_full.at(e - 1, KD))
                        for m in range(MH):
                            act.wait_ge(up_full.sem, up_full.at(e, m + 1))
                            nc.scalar.activation(h_h[:, m, :], UP[m % NU][:, 0:CAP], ACT.Relu).then_inc(hh_ready.sem, 1)
                            if m in (0, 5) and kind != "last":
                                split_w1(j + p, 1 - p, e + 1, m // 5)
                        if kind != "last":
                            split_rows(e + 1)
                            split_w2(j + p, 1 - p, e + 1)
                        for k in range(KD):
                            act.wait_ge(down_full.sem, down_full.at(e, k + 1))
                            nc.scalar.activation(y_t[:, k, :], YA[k][:, 0:CAP], ACT.Copy).then_inc(yt_ready.sem, 1)

                    split_w1(0, 0, 0, 0)
                    split_w1(0, 0, 0, 1)
                    split_rows(0)
                    split_w2(0, 0, 0)
                    expert_steps(act, run)

                @block.vector
                def _(dve):
                    v = nc.vector

                    def split_w1(p, e, k):
                        dve.wait_ge(w1h_ready.sem, w1h_ready.at(e, k + 1))
                        v.tensor_tensor(w1_l[p][:, k, :], w1_f[p][:, k, :], w1_h[p][:, k, :].bitcast(F32), ALU.subtract).then_inc(w1_split.sem, 1)

                    def split_w2(p, e):
                        for i in range(4):
                            c = slice(2 * i, 2 * i + 2)
                            dve.wait_ge(w2h_ready.sem, w2h_ready.at(e, i + 1))
                            v.tensor_tensor(w2_l[p][:, c, :], w2_f[p][:, c, :], w2_h[p][:, c, :].bitcast(F32), ALU.subtract).then_inc(w2_split.sem, 1)

                    def split_rows(e):
                        for k in range(KD):
                            dve.wait_ge(xth_ready.sem, xth_ready.at(e, k + 1))
                            v.tensor_tensor(xt_l[:, k, :], XT[k][:, 0:CAP], xt_h[:, k, :].bitcast(F32), ALU.subtract).then_inc(xt_split.sem, 1)

                    def run(kind, j, p, e):
                        for m in range(MH):
                            dve.wait_ge(hh_ready.sem, hh_ready.at(e, m + 1))
                            v.scalar_tensor_tensor(h_l[:, m, :], UP[m % NU][:, 0:CAP], 0.0, h_h[:, m, :].bitcast(F32), ALU.max,
                                                   ALU.subtract).then_inc(h_split.sem, 1)
                            if m == 3 and kind != "last":
                                split_w1(1 - p, e + 1, 0)
                        if kind != "first":
                            weigh(j - 1 + p, 1 - p, e - 1)
                        indices(j, p, e)
                        if kind != "last":
                            split_rows(e + 1)
                            split_w1(1 - p, e + 1, 1)
                            split_w2(1 - p, e + 1)

                    def indices(j, p, e):
                        dve.wait_ge(res_in[p].sem, res_in[p].at(j, 3))
                        v.tensor_scalar(token[p][:, 0:2], res[p][:, 0:2, ROW_T - D], float(T), None, ALU.add)
                        v.tensor_scalar(token[p][0:SR[2], 2:3], res[p][0:SR[2], 2:3, ROW_T - D], float(T), None, ALU.add
                                        ).then_inc(index_ready.sem, 1)
                        v.tensor_scalar(gate_row[p][:, 0:2], res[p][:, 0:2, ROW_G - D], 0.0, None, ALU.add)
                        v.tensor_scalar(gate_row[p][0:SR[2], 2:3], res[p][0:SR[2], 2:3, ROW_G - D], 0.0, None, ALU.add
                                        ).then_inc(index_ready.sem, 1)

                    def weigh(j, p, e, last=False):
                        dve.wait_ge(ytr_full.sem, ytr_full.at(e, 1))
                        dve.wait_ge(gb_in[p].sem, gb_in[p].at(j, 3))
                        if not (isinstance(e, int) and e == 0):
                            dve.wait_ge(y_out.sem, y_out.at(e - 1, 3))
                        for i, n in enumerate(SR):
                            y = YT[:, i * D:(i + 1) * D] if i < 2 else LASTROWS[0:n, 0:D]
                            v.scalar_tensor_tensor(y_s[0:n, i, :], y, res[p][0:n, i, ROW_P - D:ROW_P - D + 1], gb[p][0:n, i, :],
                                                   ALU.mult, ALU.mult).then_inc(y_weighed.sem, 1)
                            if last:
                                dve.wait_ge(y_weighed.sem, y_weighed.at(e, i + 1))
                                v.tensor_tensor(y_s[0:n, i, :], y_s[0:n, i, :], res[p][0:n, i, 0:D], ALU.add).then_inc(y_added.sem, 1)

                    split_w1(0, 0, 0)
                    split_w1(0, 0, 1)
                    split_rows(0)
                    split_w2(0, 0)
                    expert_steps(dve, run)
                    weigh(E // 2 - 1, 1, E - 1, last=True)

                @block.gpsimd
                def _(pool):
                    g = nc.gpsimd

                    def gather_gates(e, p):
                        pool.wait_ge(index_ready.sem, index_ready.at(e, 2))
                        g.tensor_tensor(turn2[:, p:p + 1], blank_row[:, :], blank_row[:, :], ALU.add)
                        for i, n in enumerate(SR):
                            g.indirect_dma_start(gb[p][0:n, i, :], None, mod_d.rearrange("b r d -> (b r) d"),
                                                 bass.IndirectOffsetOnAxis(gate_row[p][0:n, i:i + 1], 0),
                                                 bounds_check=4 * B - 1, oob_is_err=False).then_inc(gb_in[p].sem, 16)

                    def store_rows(e, p, i):
                        g.indirect_dma_start(out.rearrange("b s d -> (b s) d"), bass.IndirectOffsetOnAxis(token[p][0:SR[i], i:i + 1], 0),
                                             y_s[0:SR[i], i, :], None, bounds_check=T - 1, oob_is_err=False).then_inc(y_out.sem, 16)

                    def rows_out(e, p):
                        pool.wait_ge(y_weighed.sem, y_weighed.at(e, 3))
                        g.tensor_tensor(y_s[:, 0:2, :], y_s[:, 0:2, :], res[p][:, 0:2, 0:D], ALU.add).then_inc(y_added.sem, 1)
                        g.tensor_tensor(y_s[0:SR[2], 2, :], y_s[0:SR[2], 2, :], res[p][0:SR[2], 2, 0:D], ALU.add).then_inc(y_added.sem, 1)
                        pool.wait_ge(y_added.sem, y_added.at(e, 2))
                        g.tensor_tensor(turn2[:, 2:3], blank_row[:, :], blank_row[:, :], ALU.add)
                        for i in range(3):
                            store_rows(e, p, i)

                    def run(kind, j, p, e):
                        gather_gates(e, p)
                        if kind != "first":
                            rows_out(e - 1, 1 - p)

                    expert_steps(pool, run)
                    for i in range(3):
                        pool.wait_ge(y_added.sem, y_added.at(E - 1, i + 1))
                        g.tensor_tensor(turn2[:, 3 + i:4 + i], blank_row[:, :], blank_row[:, :], ALU.add)
                        store_rows(E - 1, 1, i)
                    pool.wait_ge(y_out.sem, y_out.at(E - 1, 3))


_INS = ["L0_attn_x", "L0_attn_wq", "L0_attn_wk", "L0_attn_wv", "L0_attn_wgq", "L0_attn_wgk", "L0_attn_wgv", "L0_attn_r_out_w",
        "L0_attn_gate_local_w", "L0_attn_gate_remote_w", "L0_attn_w_out", "L0_ffn_gate_w", "L0_ffn_w1", "L0_ffn_w2", "L0_c", "L0_wmod"]


def kernel(**inputs):
    import numpy as np
    import concourse.bacc as bacc
    from concourse.bass_utils import run_bass_kernel_spmd

    nc = bacc.Bacc("TRN2", target_bir_lowering=False, num_devices=1)
    arrays, args = {}, []
    for name in _INS:
        a = np.ascontiguousarray(inputs[name])
        arrays[f"in_{name}"] = a
        args.append(nc.dram_tensor(f"in_{name}", a.shape, mybir.dt.from_np(a.dtype), kind="ExternalInput").ap())
    args.append(nc.dram_tensor("out_rows", (B, S, D), F32, kind="ExternalOutput").ap())
    adaln_moe_kernel(nc, *args)
    r = run_bass_kernel_spmd(nc, [arrays], core_ids=[0])
    return r.results[0]["out_rows"]
```
